# Optimizing a Trainium2 kernel written in Bass

```python
import numpy as np
import jax
import jax.numpy as jnp

def _softmax(x, axis=-1):
    return jax.nn.softmax(x, axis=axis)

def _gelu(x):
    return jax.nn.gelu(x, approximate=True)

def _silu(x):
    return jax.nn.silu(x)

def _sigmoid(x):
    return jax.nn.sigmoid(x)

def _layernorm(x, axis=-1, eps=1e-05):
    m = jnp.mean(x, axis=axis, keepdims=True)
    v = jnp.var(x, axis=axis, keepdims=True)
    return (x - m) / jnp.sqrt(v + eps)

def _scatter_add(tgt, idx, src, axis=0):
    return tgt.at[idx].add(src)

def _segment_sum(src, seg, n):
    return jax.ops.segment_sum(src, seg, n)
kernel_name = 'mk_prb_d1_jaxref_r4_f01439'

def setup_inputs(seed: int=0):
    np.random.seed(seed)
    _w = jnp.asarray

    def _L0_attn_setup():
        import jax, jax.numpy as jnp
        import numpy as np
        D_MODEL = 256
        NUM_HEADS = 16
        D_K = D_MODEL // NUM_HEADS
        ROPE_THETA = 10000.0

        def _apply_rope(t):
            S, dk = (t.shape[-2], t.shape[-1])
            inv_freq = 1.0 / ROPE_THETA ** (jnp.arange(0, dk, 2) / dk)
            angles = jnp.outer(jnp.arange(S), inv_freq)
            cos = jnp.repeat(jnp.cos(angles), 2, axis=-1).astype(t.dtype)
            sin = jnp.repeat(jnp.sin(angles), 2, axis=-1).astype(t.dtype)
            t_even = t[..., 0::2]
            t_odd = t[..., 1::2]
            t_rot = jnp.stack([-t_odd, t_even], axis=-1).reshape(t.shape)
            return t * cos + t_rot * sin
        key = jax.random.key(seed)
        kx, kq, kk, kv, ko = jax.random.split(key, 5)
        B, S = (4, 512)
        std = (2.0 / (D_MODEL + D_MODEL)) ** 0.5

        def w(k):
            return jax.random.truncated_normal(k, -3.0, 3.0, (D_MODEL, D_MODEL), jnp.float32) * std
        return {'x': jax.random.normal(kx, (B, S, D_MODEL), jnp.float32), 'Wq': w(kq), 'Wk': w(kk), 'Wv': w(kv), 'Wo': w(ko)}
    _L0_attn_in = _L0_attn_setup()

    def _L0_ffn_setup():
        import jax, jax.numpy as jnp
        import numpy as np
        B, S, H, E = (2, 512, 256, 16)
        key = jax.random.key(seed)
        k0, k1, k2, k3 = jax.random.split(key, 4)
        tokens = jax.random.normal(k0, (B, S, H), dtype=jnp.float32)
        gate_w = jax.random.normal(k1, (E, H), dtype=jnp.float32) * H ** (-0.5)
        expert_w = jax.random.normal(k2, (E, H, H), dtype=jnp.float32) * H ** (-0.5)
        expert_b = jax.random.normal(k3, (E, H), dtype=jnp.float32) * 0.01
        return {'tokens': tokens, 'gate_w': gate_w, 'expert_w': expert_w, 'expert_b': expert_b}
    _L0_ffn_in = _L0_ffn_setup()
    _d = {'L0_attn_x': _L0_attn_in['x'], 'L0_attn_Wq': _L0_attn_in['Wq'], 'L0_attn_Wk': _L0_attn_in['Wk'], 'L0_attn_Wv': _L0_attn_in['Wv'], 'L0_attn_Wo': _L0_attn_in['Wo'], 'L0_ffn_gate_w': _L0_ffn_in['gate_w'], 'L0_ffn_expert_w': _L0_ffn_in['expert_w'], 'L0_ffn_expert_b': _L0_ffn_in['expert_b']}
    _x0 = _d['L0_attn_x']
    _d['L0_attn_x'] = jax.random.normal(jax.random.fold_in(jax.random.key(seed), 1), (8, 1024, 256), dtype=_x0.dtype)
    del _x0
    return _d

def reference(L0_attn_x, L0_attn_Wq, L0_attn_Wk, L0_attn_Wv, L0_attn_Wo, L0_ffn_gate_w, L0_ffn_expert_w, L0_ffn_expert_b):

    def _L0_attn_ref(x, Wq, Wk, Wv, Wo):
        import jax, jax.numpy as jnp
        import numpy as np
        D_MODEL = 256
        NUM_HEADS = 16
        D_K = D_MODEL // NUM_HEADS
        ROPE_THETA = 10000.0

        def _apply_rope(t):
            S, dk = (t.shape[-2], t.shape[-1])
            inv_freq = 1.0 / ROPE_THETA ** (jnp.arange(0, dk, 2) / dk)
            angles = jnp.outer(jnp.arange(S), inv_freq)
            cos = jnp.repeat(jnp.cos(angles), 2, axis=-1).astype(t.dtype)
            sin = jnp.repeat(jnp.sin(angles), 2, axis=-1).astype(t.dtype)
            t_even = t[..., 0::2]
            t_odd = t[..., 1::2]
            t_rot = jnp.stack([-t_odd, t_even], axis=-1).reshape(t.shape)
            return t * cos + t_rot * sin
        B, S, D = x.shape
        H, dk = (NUM_HEADS, D_K)
        q = jnp.einsum('bsi,io->bso', x, Wq).reshape(B, S, H, dk).swapaxes(1, 2)
        k = jnp.einsum('bsi,io->bso', x, Wk).reshape(B, S, H, dk).swapaxes(1, 2)
        v = jnp.einsum('bsi,io->bso', x, Wv).reshape(B, S, H, dk).swapaxes(1, 2)
        q = _apply_rope(q)
        k = _apply_rope(k)
        scores = jnp.einsum('bhqd,bhkd->bhqk', q, k) / dk ** 0.5
        causal = jnp.tril(jnp.ones((S, S), dtype=bool))
        scores = jnp.where(causal, scores, -jnp.inf)
        attn = jax.nn.softmax(scores, axis=-1)
        out = jnp.einsum('bhqk,bhkd->bhqd', attn, v)
        out = out.swapaxes(1, 2).reshape(B, S, D)
        return jnp.einsum('bsi,io->bso', out, Wo)

    def _L0_ffn_ref(tokens, gate_w, expert_w, expert_b):
        import jax, jax.numpy as jnp
        import numpy as np
        B, S, H, E = (2, 512, 256, 16)
        b, s, h = tokens.shape
        logits = jnp.einsum('bsh,eh->bse', tokens, gate_w)
        weights = jax.nn.softmax(logits, axis=-1)
        top2_w, top2_idx = jax.lax.top_k(weights, 2)
        flat = tokens.reshape(b * s, h)
        flat_w = top2_w.reshape(b * s, 2)
        flat_idx = top2_idx.reshape(b * s, 2)
        y = jax.nn.relu(jnp.einsum('nh,edh->ned', flat, expert_w) + expert_b[None, :, :])
        sel = jnp.take_along_axis(y, flat_idx[:, :, None], axis=1)
        out = jnp.sum(sel * flat_w[:, :, None], axis=1)
        return out.reshape(b, s, h)
    x = L0_attn_x
    xn = _layernorm(x, axis=-1)
    x = x + _L0_attn_ref(xn, L0_attn_Wq, L0_attn_Wk, L0_attn_Wv, L0_attn_Wo) + _L0_ffn_ref(xn, L0_ffn_gate_w, L0_ffn_expert_w, L0_ffn_expert_b)
    return x

_drawn_inputs = setup_inputs


def setup_inputs(seed=0):
    import zlib

    import numpy as np

    out = dict(_drawn_inputs(seed))
    spreads = {}
    factors = {'L0_ffn_expert_b': 26.919}
    for name, (base, spread) in spreads.items():
        noise = np.random.default_rng([zlib.crc32(name.encode()), seed]).standard_normal(out[name].shape)
        drawn = base * np.exp(spread * noise) if base else spread * noise
        out[name] = jnp.asarray(drawn.astype(out[name].dtype))
    for name, factor in factors.items():
        out[name] = (out[name] * factor).astype(out[name].dtype)
    return out
```

```python
from contextlib import ExitStack

import numpy as np

import concourse.bass as bass
from concourse import mybir

F32 = mybir.dt.float32
BF16 = mybir.dt.bfloat16
I32 = mybir.dt.int32
ALU = mybir.AluOpType
ACT = mybir.ActivationFunctionType
X = mybir.AxisListType.X
ds = bass.ds

P = 128
B, S, D = 8, 1024, 256
H, DK = 16, 16
G = 4
HG = H // G
GD = HG * DK
C = D // P
TB = S // P
T = B * TB
N = B * S
E = 16
MT = 2 * N // P + E
PAIRS = MT // 2
PU = 6
B_MOE, B_COMB = 2, 5
B_LAST = B - 1
CU = 4
assert (B_COMB - B_MOE) * G * PU == PAIRS
HALF = S // 2
SCALE = DK ** -0.5
SAFE = 60.0
NORM2 = SAFE / SCALE
BIG = -1.0e38
EPS = 1e-5

STEPS = [(1, j) for j in range(8)] + [(0, j) for j in range(4)]
NS = len(STEPS)
EX = 2 * NS
MK = NS - 4
SLOTS_Q = [0, 0, 0, 1, 1, 2]
SLOTS_K = [0, 1, 2, 0, 1, 0]
CREDIT = 2
MASK0 = S - P
MASKW = MASK0 + S
SLOW = TB * HG * 2
SLOW_PE = SLOW + 1
SLOW_DVE = 2 * SLOW + 6
NLOAD = 7


def first_q(k):
    hf, j = STEPS[k]
    return max(HALF * hf, P * j)


def width(k):
    return HALF * (STEPS[k][0] + 1) - first_q(k)


def is_diag(k):
    hf, j = STEPS[k]
    return j * P >= HALF * hf


def wait(eng, sem, value):
    if isinstance(value, int) and value <= 0:
        return
    eng.wait_ge(sem, value)


def wait_apart(eng, sem, value, tick):
    eng.wait_ge(sem, value)
    eng.sem_inc(tick, 1)


def build(nc, a):
    xnt_d = nc.dram_tensor("xnt_scratch", [B, P, C, S], F32, kind="Internal").ap()
    xn_d = nc.dram_tensor("xn_scratch", [N, D], F32, kind="Internal").ap()
    h_d = nc.dram_tensor("h_scratch", [N, D], F32, kind="Internal").ap()
    y_d = nc.dram_tensor("y_scratch", [MT * P, D], F32, kind="Internal").ap()
    list_d = nc.dram_tensor("list_scratch", [P * MT, 1], I32, kind="Internal").ap()
    part_d = [nc.dram_tensor(f"part_scratch{i}", [3, 2, DK, HG * S], BF16, kind="Internal").ap() for i in range(2)]
    max_d = [nc.dram_tensor(f"max_scratch{i}", [3, HG, TB, P], BF16, kind="Internal").ap() for i in range(2)]

    x_rows = a["x"].rearrange("b s d -> (b s) d")
    out_rows = a["out"].rearrange("b s d -> (b s) d")

    with ExitStack() as ctx:
        def sb(name, shape, dt=F32, to=ctx):
            return to.enter_context(nc.sbuf_tensor(name, shape, dt))

        def sem(name):
            return ctx.enter_context(nc.semaphore(name))

        ident = sb("ident", [P, P])
        identb = sb("identb", [P, P], BF16)
        headsum = sb("headsum", [P, 2 * HG], BF16)
        wv = sb("wv", [P, C, D])
        wo = sb("wo", [P, C, D])
        wqk = sb("wqk", [P, G, C, P])
        cosT = sb("cosT", [P, S])
        sinT = sb("sinT", [P, S])
        w_top = sb("w_top", [P, 2, T])
        y_row = sb("y_row", [P, 2, T], I32)
        list_at = sb("list_at", [P, 2, T], I32)
        token = sb("token", [P, T], I32)
        tile_expert = sb("tile_expert", [1, MT], I32)
        zero_i = sb("zero_i", [P, MT], I32)
        future = sb("future", [P, P], BF16)
        masks = sb("masks", [P, MASKW], BF16)

        s_const = sem("s_const")
        s_made = sem("s_made")
        s_tick = sem("s_tick")

        with ExitStack() as p1:
            def sb1(name, shape, dt=F32):
                return sb(name, shape, dt, p1)

            def ps1(name, shape, dt=F32):
                return p1.enter_context(nc.psum_tensor(name, shape, dt))

            gate = sb1("gate", [P, C, E])
            xin = [sb1(f"xin{i}", [P, TB, D]) for i in range(2)]
            xt = [sb1(f"xt_out{i}", [P, C, S]) for i in range(2)]
            stat = sb1("stat", [P, TB, 6])
            mv = sb1("mv", [P, TB, 2])
            vareps = sb1("vareps", [P, TB])
            std = sb1("std", [P, TB])
            rstd = sb1("rstd", [P, TB])
            logit = sb1("logit", [P, T, E])
            iota_e = sb1("iota_e", [P, E])
            iota_m = sb1("iota_m", [1, MT])
            ones_b = sb1("ones_b", [P, P], BF16)
            upper_b = sb1("upper_b", [P, P], BF16)
            lower = sb1("lower", [P, P])
            constf = sb1("constf", [P, P])
            work = [sb1(f"work{i}", [P, T, E]) for i in range(3)]
            hot = [sb1(f"hot{i}", [P, T, E]) for i in range(2)]
            hotb = sb1("hotb", [P, T, E], BF16)
            top = [sb1(f"top{i}", [P, T]) for i in range(2)]
            pick = sb1("pick", [P, T])
            den = sb1("den", [P, T])
            rden = sb1("rden", [P, T])
            onesT = sb1("onesT", [P, T])
            cnt = sb1("cnt", [P, E])
            cnt_i = sb1("cnt_i", [P, E], I32)
            nt_f = sb1("nt_f", [P, E])
            inc = sb1("inc", [P, E])
            base = sb1("base", [P, E])
            ones_e = sb1("ones_e", [P, E])
            posf = sb1("posf", [P, 2, T])
            lo_i = sb1("lo_i", [P, 2, T], I32)
            hi_i = sb1("hi_i", [P, 2, T], I32)
            at_f = sb1("at_f", [P, 2, T])
            ge = sb1("ge", [1, MT, E])
            te_f = sb1("te_f", [1, MT])

            turn = [ps1(f"turn{i}", [P, 4, P]) for i in range(4)]
            lg = ps1("lg", [P, TB, E])
            rank = ps1("rank", [P, 2, T // 2, E])

            s_x = [sem(f"s_x{i}") for i in range(2)]
            s_var = sem("s_var")
            s_std = sem("s_std")
            s_ln = sem("s_ln")
            s_turn = sem("s_turn")
            s_xt = sem("s_xt")
            s_lg = sem("s_lg")
            s_lgc = sem("s_lgc")
            s_xn_st = [sem(f"s_xn_st{i}") for i in range(2)]
            s_xt_st = [sem(f"s_xt_st{i}") for i in range(2)]
            s_r = sem("s_r")
            s_ract = sem("s_ract")
            s_rpe = sem("s_rpe")
            s_zero = sem("s_zero")
            s_list0 = sem("s_list0")

            with nc.Block() as block:

                @block.sync
                def _(sp):
                    sp.dma_start(xin[0][:], a["x"][0].rearrange("(t p) d -> p t d", p=P)).then_inc(s_x[0], 16)
                    sp.dma_start(xin[1][:], a["x"][1].rearrange("(t p) d -> p t d", p=P)).then_inc(s_x[1], 16)
                    sp.dma_start(ident[:], a["ident"]).then_inc(s_const, 16)
                    sp.dma_start(lower[:], a["lower"]).then_inc(s_const, 16)
                    sp.dma_start(constf[:], a["upper"]).then_inc(s_const, 16)
                    sp.dma_start(gate[:], a["gate_wT"].rearrange("(c p) e -> p c e", p=P)).then_inc(s_const, 16)
                    sp.dma_start(iota_e[:], a["iota_e"]).then_inc(s_const, 16)
                    sp.dma_start(iota_m[:], a["iota_m"]).then_inc(s_const, 16)
                    sp.dma_start(work[0][:, 0, 0:2 * HG], a["headsum"]).then_inc(s_const, 16)
                    sp.dma_start(wv[:], a["Wv"].rearrange("(c p) n -> p c n", p=P)).then_inc(s_const, 16)
                    sp.dma_start(wo[:], a["Wo"].rearrange("(c p) n -> p c n", p=P)).then_inc(s_const, 16)
                    sp.dma_start(wqk[:], a["Wqk"]).then_inc(s_const, 16)
                    sp.dma_start(cosT[:], a["cosT"]).then_inc(s_const, 16)
                    sp.dma_start(sinT[:], a["sinT"]).then_inc(s_const, 16)
                    sp.dma_start(xt[1][:].rearrange("p c s -> p (c s)")[:, 0:MASKW], a["masks"]).then_inc(s_const, 16)
                    sp.wait_ge(s_zero, 1)
                    sp.dma_start(list_d.rearrange("(p m) o -> p (m o)", p=P), zero_i[:]).then_inc(s_list0, 16)
                    def turn_over(i, more):
                        for par in range(2):
                            n = 2 * i + par
                            wait_apart(sp, s_ln, n + 1, s_tick)
                            sp.dma_start(xn_d[ds(n * S, S)].rearrange("(t p) d -> p t d", p=P), xin[par][:]).then_inc(s_xn_st[par], 16)
                            wait_apart(sp, s_xt, CREDIT + n * 4 + 4, s_tick)
                            sp.dma_start(xnt_d[ds(n, 1)].rearrange("o p c s -> p (o c) s"), xt[par][:]).then_inc(s_xt_st[par], 16)
                            if more:
                                wait_apart(sp, s_xn_st[par], 16 * (i + 1), s_tick)
                                sp.dma_start(xin[par][:], a["x"][ds(n + 2, 1)].rearrange("o (t p) d -> p (o t) d", p=P)).then_inc(s_x[par], 16)

                    with sp.Fori(0, B // 2 - 1) as i:
                        turn_over(i, True)
                    turn_over(B // 2 - 1, False)
                    for par in range(2):
                        sp.wait_ge(s_xn_st[par], 16 * (B // 2))
                        sp.wait_ge(s_xt_st[par], 16 * (B // 2))
                    sp.wait_ge(s_const, 16 * 13)
                    sp.wait_ge(s_list0, 16)

                @block.gpsimd
                def _(pool):
                    pool.memset(zero_i[:], 0).then_inc(s_zero, 1)
                    pool.iota(token[:], pattern=[[P, T]], base=0, channel_multiplier=1)
                    pool.memset(ones_b[:], 1.0)
                    pool.memset(onesT[:], 1.0)
                    pool.memset(ones_e[:], 1.0).then_inc(s_made, 1)

                @block.vector
                def _(dve):
                    dve.wait_ge(s_const, 16 * 13)
                    dve.sem_inc(s_lgc, CREDIT)
                    dve.wait_ge(s_made, 1)
                    dve.tensor_copy(identb[:], ident[:])
                    dve.tensor_copy(upper_b[:], constf[:])
                    dve.tensor_scalar(future[:], lower[:], BIG, None, ALU.mult)
                    dve.tensor_copy(masks[:], xt[1][:].rearrange("p c s -> p (c s)")[:, 0:MASKW])
                    dve.tensor_copy(headsum[:], work[0][:, 0, 0:2 * HG]).then_inc(s_made, 1)
                    with dve.Fori(0, B // 2) as i:
                        for par in range(2):
                            n = 2 * i + par
                            dve.wait_ge(s_x[par], 16 * (i + 1))
                            for t in range(TB):
                                last = dve.bn_stats(stat[:, t, :], xin[par][:, t, :])
                            last.then_inc(s_var, 1)
                            wait_apart(dve, s_var, 3 * n + 1, s_tick)
                            for t in range(TB):
                                last = dve.bn_aggr(mv[:, t, :], stat[:, t, :])
                            last.then_inc(s_var, 1)
                            dve.wait_ge(s_var, 3 * n + 2)
                            dve.tensor_scalar(vareps[:], mv[:, :, 1], EPS, None, ALU.add).then_inc(s_var, 1)
                            dve.wait_ge(s_std, n + 1)
                            dve.reciprocal(rstd[:], std[:]).then_inc(s_lgc, 1)
                            dve.wait_ge(s_lgc, CREDIT + 2 * n + 1)
                            for t in range(TB):
                                last = dve.tensor_scalar(xin[par][:, t, :], xin[par][:, t, :], mv[:, t, 0:1],
                                                         rstd[:, t:t + 1], ALU.subtract, ALU.mult)
                            last.then_inc(s_ln, 1)
                            dve.wait_ge(s_lg, n + 1)
                            dve.tensor_copy(logit[:, ds(n * TB, TB), :], lg[:]).then_inc(s_lgc, 1)

                    step = [0]

                    def then(ins):
                        step[0] += 1
                        ins.then_inc(s_r, 1)
                        dve.wait_ge(s_r, step[0])

                    def over_e(v):
                        return v.unsqueeze(2).broadcast_to([P, T, E])

                    iota_b = iota_e[:].unsqueeze(1).broadcast_to([P, T, E])
                    dve.wait_ge(s_lgc, CREDIT + 2 * B)
                    src = logit
                    for s in range(2):
                        then(dve.tensor_reduce(top[s][:], src[:], X, ALU.max))
                        then(dve.tensor_tensor(work[0][:], src[:], over_e(top[s][:]), ALU.is_equal))
                        then(dve.tensor_tensor(work[0][:], work[0][:], iota_b, ALU.mult))
                        then(dve.tensor_reduce(pick[:], work[0][:], X, ALU.min))
                        then(dve.tensor_tensor(hot[s][:], work[0][:], over_e(pick[:]), ALU.is_equal))
                        if s == 0:
                            then(dve.scalar_tensor_tensor(work[1][:], hot[0][:], BIG, logit[:], ALU.mult, ALU.add))
                            src = work[1]
                    then(dve.tensor_tensor(hotb[:], hot[0][:], hot[1][:], ALU.add))
                    n_hot = step[0]
                    then(dve.tensor_tensor(work[2][:], logit[:], over_e(top[0][:]), ALU.subtract))
                    then(dve.tensor_tensor(pick[:], top[1][:], top[0][:], ALU.subtract))
                    n_sub = step[0]
                    dve.wait_ge(s_ract, 2)
                    then(dve.tensor_reduce(den[:], work[2][:], X, ALU.add))
                    then(dve.reciprocal(w_top[:, 0, :], den[:]))
                    then(dve.tensor_tensor(w_top[:, 1, :], pick[:], w_top[:, 0, :], ALU.mult))
                    dve.wait_ge(s_rpe, 1)
                    tot = work[0]
                    for hh in range(2):
                        then(dve.tensor_copy(tot[:, hh * T // 2:(hh + 1) * T // 2, :].rearrange("p t e -> p (t e)"),
                                             turn[2 + hh][:].rearrange("p a b -> p (a b)")))
                    pre = work[1]
                    for e in range(E):
                        last = dve.tensor_tensor_scan(pre[:, :, e], onesT[:], tot[:, :, e], 0.0, ALU.mult, ALU.add)
                    then(last)
                    then(dve.tensor_scalar(cnt[:], pre[:, T - 1, :], float(P - 1), None, ALU.add))
                    then(dve.tensor_copy(cnt_i[:], cnt[:]))
                    then(dve.tensor_scalar(cnt_i[:], cnt_i[:], 7, None, ALU.arith_shift_right))
                    then(dve.tensor_copy(nt_f[:], cnt_i[:]))
                    then(dve.tensor_tensor_scan(inc[:], ones_e[:], nt_f[:], 0.0, ALU.mult, ALU.add))
                    then(dve.tensor_tensor(base[:], inc[:], nt_f[:], ALU.subtract))
                    then(dve.tensor_scalar(base[:], base[:], float(P), None, ALU.mult))
                    then(dve.tensor_tensor(pre[:], pre[:], tot[:], ALU.subtract))
                    then(dve.tensor_tensor(pre[:], pre[:], base[:].unsqueeze(1).broadcast_to([P, T, E]), ALU.add))
                    then(dve.tensor_tensor(pre[:], rank[:].rearrange("p a t e -> p (a t) e"), pre[:], ALU.add))
                    for s in range(2):
                        then(dve.tensor_tensor(work[2][:], pre[:], hot[s][:], ALU.mult))
                        then(dve.tensor_reduce(posf[:, s, :], work[2][:], X, ALU.add))
                    then(dve.tensor_copy(y_row[:], posf[:]))
                    then(dve.tensor_scalar(lo_i[:], y_row[:], P - 1, None, ALU.bitwise_and))
                    then(dve.tensor_scalar(hi_i[:], y_row[:], 7, None, ALU.arith_shift_right))
                    then(dve.tensor_scalar(at_f[:], lo_i[:], float(MT), None, ALU.mult))
                    then(dve.tensor_tensor(list_at[:], at_f[:], hi_i[:], ALU.add))
                    then(dve.tensor_tensor(ge[:], iota_m[:].unsqueeze(2).broadcast_to([1, MT, E]),
                                           inc[0:1, :].unsqueeze(1).broadcast_to([1, MT, E]), ALU.is_ge))
                    then(dve.tensor_reduce(te_f[:], ge[:, :, 0:E - 1], X, ALU.add))
                    then(dve.tensor_copy(tile_expert[:], te_f[:]))

                N_HOT, N_SUB = 12, 14

                @block.tensor
                def _(pe):
                    pe.wait_ge(s_const, 16 * 13)
                    with pe.Fori(0, B // 2) as i:
                        for par in range(2):
                            n = 2 * i + par
                            pe.wait_ge(s_ln, n + 1)
                            for q in range(4):
                                pe.wait_ge(s_xt, CREDIT + 4 * n)
                                for t in range(2):
                                    for c in range(C):
                                        last = pe.transpose(turn[q][:, 2 * t + c, :], xin[par][:, 2 * q + t, c * P:(c + 1) * P], ident[:])
                                last.then_inc(s_turn, 1)
                            pe.wait_ge(s_xt, CREDIT + 4 * n + 4)
                            pe.wait_ge(s_lgc, CREDIT + 2 * n)
                            for t in range(TB):
                                for c in range(C):
                                    last = pe.matmul(lg[:, t, :], xt[par][:, c, t * P:(t + 1) * P], gate[:, c, :], start=(c == 0), stop=(c == C - 1))
                            last.then_inc(s_lg, 1)
                    pe.wait_ge(s_r, N_HOT)
                    for hh in range(2):
                        rhs = hotb[:, hh * T // 2:(hh + 1) * T // 2, :]
                        pe.matmul(rank[:, hh], upper_b[:], rhs, start=True, stop=True)
                        last = pe.matmul(turn[2 + hh][:].rearrange("p a b -> p (a b)"), ones_b[:], rhs, start=True, stop=True)
                    last.then_inc(s_rpe, 1)

                @block.scalar
                def _(act):
                    def copy_out(i, first):
                        for par in range(2):
                            n = 2 * i + par
                            act.wait_ge(s_var, 3 * n + 3)
                            act.activation(std[:], vareps[:], ACT.Sqrt).then_inc(s_std, 1)
                            if not first:
                                act.wait_ge(s_xt_st[par], 16 * i)
                                act.wait_ge(s_lg, n - 1)
                            for q in range(4):
                                act.wait_ge(s_turn, 4 * n + q + 1)
                                act.activation(xt[par][:].rearrange("p c (t s) -> p t c s", s=P)[:, 2 * q:2 * q + 2],
                                               turn[q][:].rearrange("p (t c) s -> p t c s", c=C), ACT.Copy).then_inc(s_xt, 1)

                    act.sem_inc(s_xt, CREDIT)
                    copy_out(0, True)
                    with act.Fori(1, B // 2) as i:
                        copy_out(i, False)
                    act.wait_ge(s_r, N_SUB)
                    act.activation(work[2][:], work[2][:], ACT.Exp).then_inc(s_ract, 1)
                    act.activation(pick[:], pick[:], ACT.Exp).then_inc(s_ract, 1)

        xT = sb("xT", [P, C, S])
        rot_a = sb("rot_a", [P, S])
        rot_b = sb("rot_b", [P, S])
        qk = sb("qk", [P, S])
        parts = sb("parts", [P, 3, S], BF16)
        squares = sb("squares", [P, S], BF16)
        q_op = [sb(f"q_op{i}", [P, HG, S], BF16) for i in range(2)]
        k_op = [sb(f"k_op{i}", [P, HG, S], BF16) for i in range(2)]
        v_op = [sb(f"v_op{i}", [P, TB, HG, 2 * DK]) for i in range(2)]
        prob = [sb(f"prob{i}", [P, HG, HALF]) for i in range(3)]
        o_t = [sb(f"o_t{i}", [P, HALF]) for i in range(2)]
        inv = sb("inv", [P, 4, HG])
        attn = sb("attn", [P, TB, D])
        attn_t = sb("attn_t", [P, C, S])
        resid = [sb(f"resid{i}", [P, 2, D]) for i in range(2)]
        maxrow = sb("maxrow", [2 * DK, 3, P], BF16)
        nmax = sb("nmax", [P, 1])
        nbound = sb("nbound", [1, 1])
        flag = sb("flag", [1, 1], I32)
        rowmax = sb("rowmax", [P, TB, HG, 2])
        rm = sb("rm", [P, HG * TB])
        rmb = sb("rmb", [P, 3, HG * TB], BF16)
        ew = sb("ew", [P, E, C, D])
        ebias = sb("ebias", [P, E, D])
        lists = sb("lists", [P, MT + 4], I32)
        pick_m = [sb(f"pick_m{i}", [P, 2], I32) for i in range(3)]
        x_m = [sb(f"x_m{i}", [P, 2, D]) for i in range(3)]
        xt_m = [sb(f"xt_m{i}", [P, 2, C, P]) for i in range(2)]
        y_m = [sb(f"y_m{i}", [P, 2, D]) for i in range(2)]
        pick_c = pick_m
        y_c = [x_m[0], x_m[1]]
        h_c = [y_m[0][:, 0, :], y_m[1][:, 0, :]]

        def ps(name, shape, dt=F32):
            return ctx.enter_context(nc.psum_tensor(name, shape, dt))

        st_ps = [ps(f"st_ps{i}", [P, 2, HALF]) for i in range(2)]
        acc = ps("acc", [P, HALF])
        m0 = ps("m0", [P, HALF])
        m1 = ps("m1", [P, HALF])
        m2 = ps("m2", [P, HALF])

        names = ("xT_in xT_used qk_full qk_used rot_mul rot split sq v_full v_used n_full n_used nt_full "
                 "nt_used st exp pmask pv o_copied o_full o_inv o_used e_full e_used w_full w_used "
                 "flagged maxready slow_pe slow_dve ones scattered listed ew_in "
                 "mt_full mt_used mm_full mm_used y_bias y_relu picked pick_c_made h_c1 combined zeroed part_out max_out").split()
        s_ = {n: sem("s_" + n) for n in names}
        s_load = [sem(f"s_load{i}") for i in range(2)]
        s_res_in = [sem(f"s_res_in{i}") for i in range(2)]
        s_res_out = [sem(f"s_res_out{i}") for i in range(2)]
        s_xm = [sem(f"s_xm{i}") for i in range(3)]
        s_yst = [sem(f"s_yst{i}") for i in range(2)]
        s_yc = [sem(f"s_yc{i}") for i in range(2)]
        s_hc = [sem(f"s_hc{i}") for i in range(2)]
        s_oc = [sem(f"s_oc{i}") for i in range(2)]

        def kind(b):
            return "plain" if b < B_MOE else "moe" if b < B_COMB else "comb"

        def walk(eng, unit):
            for b in range(B_MOE):
                for g in range(G):
                    unit(b, g, "plain")
            with eng.Fori(B_MOE, B_COMB) as b:
                for g in range(G):
                    unit(b, g, "moe")
            with eng.Fori(B_COMB, B_LAST) as b:
                for g in range(G):
                    unit(b, g, "comb")
            for g in range(G):
                unit(B_LAST, g, "comb")

        def has_prev(b, g):
            return not (isinstance(b, int) and b == 0 and g == 0)

        def has_prev_batch(b):
            return not (isinstance(b, int) and b == 0)

        def has_next(b, g):
            return not (isinstance(b, int) and b == B_LAST and g == G - 1)

        def pair0(b, g):
            return G * PU * (b - B_MOE) + PU * g

        def round0(b, g, ring):
            return G * PU // ring * (b - B_MOE) + PU // ring * g

        def tile_c0(b, g):
            return G * CU * (b - B_COMB) + CU * g

        def crounds(b, g):
            return G * CU // 2 * (b - B_COMB) + CU // 2 * g

        with nc.Block() as block:

            @block.tensor
            def _(pe):
                def take(sems):
                    for name, value in sems:
                        wait(pe, s_[name], value)

                def project_qk(n, gn, hf, bn):
                    if gn == 0 and hf == 0:
                        wait(pe, s_["xT_in"], 16 * (bn + 1))
                    bank = (m0, m1)[hf]
                    for c in range(C):
                        last = pe.matmul(bank[:], wqk[:, gn, c, :], xT[:, c, hf * HALF:(hf + 1) * HALF], start=(c == 0), stop=(c == C - 1))
                    last.then_inc(s_["qk_full"], 1)

                def project_v(n, gn):
                    for t in range(TB):
                        for c in range(C):
                            last = pe.matmul(m2[:, t * GD:(t + 1) * GD], xT[:, c, t * P:(t + 1) * P], wv[:, c, gn * GD:(gn + 1) * GD],
                                             start=(c == 0), stop=(c == C - 1))
                    last.then_inc(s_["v_full"], 1)

                def norms(n):
                    wait(pe, s_["sq"], n + 1)
                    for t in range(TB):
                        last = pe.matmul(m2[:, t * 2 * HG:(t + 1) * 2 * HG], squares[:, t * P:(t + 1) * P], headsum[:], start=True, stop=True)
                    last.then_inc(s_["n_full"], 1)

                def norm_turn(n):
                    wait(pe, s_["n_used"], n + 1)
                    pe.transpose(m0[0:1, 0:P], nmax[:], ident[:]).then_inc(s_["nt_full"], 1)

                def find_max(n, sl, rnd):
                    wait_apart(pe, s_["flagged"], n + 1, s_tick)
                    v = pe.value_load(flag[0:1, 0:1], min_val=0, max_val=1)
                    with pe.If(v > 0):
                        wait_apart(pe, s_load[sl], 16 * (NLOAD * rnd + 6), s_tick)
                        with pe.Fori(0, TB) as i:
                            for w in range(2 * HG):
                                h, half = w // 2, w % 2
                                pe.wait_ge(s_["slow_dve"], CREDIT + SLOW_DVE * n + 2 * (2 * HG * i + w))
                                pe.matmul(m0[:], q_op[sl][0:96, h, ds(i * P, P)], k_op[sl][0:96, h, half * HALF:(half + 1) * HALF],
                                          start=True, stop=True).then_inc(s_["slow_pe"], 1)
                        pe.wait_ge(s_["slow_dve"], CREDIT + SLOW_DVE * (n + 1))
                        for r in range(3):
                            last = pe.matmul(m0[0:HG * TB, r * P:(r + 1) * P], rmb[:, r, :], identb[:], start=True, stop=True)
                        last.then_inc(s_["slow_pe"], 1)
                        pe.wait_ge(s_["maxready"], n + 1)
                    with pe.Else():
                        pe.sem_inc(s_["slow_pe"], SLOW_PE)

                def scores(u, g, k, pr):
                    hf, j = STEPS[k]
                    sl = g % 2
                    wait(pe, s_["exp"], EX * u + 2 * k + pr - 1)
                    for hh in range(2):
                        h = 2 * pr + hh
                        last = pe.matmul(st_ps[pr][:, hh, 0:width(k)], k_op[sl][0:99, h, j * P:(j + 1) * P],
                                         q_op[sl][0:99, h, first_q(k):first_q(k) + width(k)], start=True, stop=not is_diag(k))
                        if is_diag(k):
                            last = pe.matmul(st_ps[pr][:, hh, 0:P], identb[:], future[:], start=False, stop=True)
                    last.then_inc(s_["st"], 1)

                def values(u, g, k):
                    hf, j = STEPS[k]
                    sl = g % 2
                    first, final = j == 0, k in (7, 11)
                    if first:
                        wait(pe, s_["o_copied"], 2 * u + (1 - hf))
                        if k == 0:
                            wait(pe, s_["v_used"], u + 1)
                    wait(pe, s_["exp"], EX * u + 2 * k + 2)
                    at = first_q(k) - HALF * hf
                    for h in range(HG):
                        last = pe.matmul(acc[32 * h:32 * h + 32, at:at + width(k)], v_op[sl][:, j, h, :], prob[k % 3][:, h, 0:width(k)],
                                         start=first, stop=final, tile_position=(0, 32 * h))
                    last.then_inc(s_["pv"], 1)

                def out_turn(u, half):
                    bank = m1 if half == 0 else m0
                    wait(pe, s_["o_copied"], 2 * u + half + 1)
                    for t in range(4):
                        last = pe.transpose(bank[:, t * P:(t + 1) * P], o_t[half][:, t * P:(t + 1) * P], ident[:])
                    last.then_inc(s_["o_full"], 1)

                def attn_turn(bp, i, bank):
                    t0 = (4, 6, 0, 2)[i]
                    for t in range(2):
                        for c in range(C):
                            last = pe.transpose(bank[:, (2 * t + c) * P:(2 * t + c + 1) * P], attn[:, t0 + t, c * P:(c + 1) * P], ident[:])
                    last.then_inc(s_["e_full"], 1)

                def out_project(bp, i, bank):
                    t0 = (4, 6, 0, 2)[i]
                    for t in range(2):
                        for c in range(C):
                            last = pe.matmul(bank[:, t * D:(t + 1) * D], attn_t[:, c, (t0 + t) * P:(t0 + t + 1) * P], wo[:, c, :],
                                             start=(c == 0), stop=(c == C - 1))
                    last.then_inc(s_["w_full"], 1)

                def expert_turn(b, g, p):
                    wait(pe, s_xm[p % 3], 32 * (round0(b, g, 3) + p // 3 + 1))
                    for t in range(2):
                        for c in range(C):
                            last = pe.transpose(m1[:, (2 * t + c) * P:(2 * t + c + 1) * P], x_m[p % 3][:, t, c * P:(c + 1) * P], ident[:])
                    last.then_inc(s_["mt_full"], 1)

                def expert_product(m, p):
                    wait(pe, s_["mt_used"], CREDIT + m + 1)
                    for t in range(2):
                        e = pe.value_load(tile_expert[0:1, ds(2 * m + t, 1)], min_val=0, max_val=E - 1)
                        for c in range(C):
                            last = pe.matmul(m2[:, t * D:(t + 1) * D], xt_m[p % 2][:, t, c, :],
                                             ew[:, ds(e, 1), c, :].rearrange("p o d -> p (o d)"), start=(c == 0), stop=(c == C - 1))
                    last.then_inc(s_["mm_full"], 1)

                def unit(b, g, kd):
                    u = G * b + g
                    n, gn = u + 1, (g + 1) % G
                    bn = b + (1 if g == G - 1 else 0)
                    prev, nxt = has_prev(b, g), has_next(b, g)
                    tail = g == 0 and has_prev_batch(b)
                    moe = kd == "moe"
                    m = pair0(b, g) if moe else None
                    done = {"qk": 2 * n, "v": n, "n": n, "nt": n, "o": 2 * u - 1, "e": G * (b - 1) if g == 0 else 0,
                            "w": G * (b - 1) if g == 0 else 0, "mt": m if moe else PAIRS if kd == "comb" and g == 0 else 0,
                            "mm": m if moe else PAIRS if kd == "comb" and g == 0 else 0}
                    if g == 1:
                        done["w"] = G * b if has_prev_batch(b) else 0

                    def free(*kinds):
                        take([(kk + "_used", done[kk] + (CREDIT if kk in ("mt", "mm") else 0)) for kk in kinds if not (isinstance(done[kk], int) and done[kk] <= 0)])

                    if moe and g == 0:
                        wait(pe, s_["ew_in"], 32)
                    for k in range(NS):
                        if k == 0:
                            wait(pe, s_load[g % 2], 16 * NLOAD * ((u // 2 + 1) if isinstance(u, int) else (2 * b + g // 2 + 1)))
                        scores(u, g, k, 0)
                        scores(u, g, k, 1)
                        if k == 9 and nxt:
                            find_max(n, (g + 1) % 2, (n // 2) if isinstance(n, int) else 2 * b + (g + 1) // 2)
                        if k == 0 and nxt:
                            free("nt", "o", "w")
                            project_qk(n, gn, 0, bn)
                            done["qk"] += 1
                        if moe and k % 2 == 0:
                            free("mt", "qk", "o", "e", "w")
                            expert_turn(b, g, k // 2)
                            done["mt"] += 1
                        if k == 1 and nxt:
                            free("o", "mt", "w")
                            project_qk(n, gn, 1, bn)
                            done["qk"] += 1
                        if k == 2 and nxt:
                            free("mm", "n", "e")
                            project_v(n, gn)
                            done["v"] += 1
                        if k == 3 and prev:
                            free("qk", "w")
                            out_turn(u - 1, 1)
                            done["o"] += 1
                        if moe and k % 2 == 1:
                            free("mm", "v", "n", "e")
                            expert_product(m + k // 2, k // 2)
                            done["mm"] += 1
                        if tail and k in (4, 5):
                            wait(pe, s_["o_used"], 2 * u)
                            free("qk", "mt", "o", "e")
                            attn_turn(b - 1, 2 * (k - 4), m1)
                            done["e"] += 1
                            free("v", "mm")
                            attn_turn(b - 1, 2 * (k - 4) + 1, m2)
                            done["e"] += 1
                        if k == 6 and nxt:
                            free("v", "mm", "e")
                            norms(n)
                            done["n"] += 1
                        if tail and k in (7, 9):
                            free("qk", "o", "nt", "w")
                            wait(pe, s_["e_used"], 4 * (b - 1) + k - 6)
                            out_project(b - 1, k - 7, m0)
                            done["w"] += 1
                            free("mt", "e", "w")
                            out_project(b - 1, k - 6, m1)
                            done["w"] += 1
                        if k == 8 and nxt:
                            free("o", "qk", "w")
                            norm_turn(n)
                            done["nt"] += 1
                        if k >= 2:
                            values(u, g, k - 2)
                        elif prev:
                            values(u - 1, (g - 1) % G, NS - 2 + k)
                        if k == 10:
                            free("qk", "mt", "w")
                            out_turn(u, 0)
                            done["o"] += 1

                pe.sem_inc(s_["mm_full"], CREDIT)
                pe.sem_inc(s_["mt_full"], CREDIT)
                project_qk(0, 0, 0, 0)
                project_qk(0, 0, 1, 0)
                project_v(0, 0)
                wait(pe, s_["v_used"], 1)
                norms(0)
                wait(pe, s_["qk_used"], 2)
                norm_turn(0)
                find_max(0, 0, 0)
                walk(pe, unit)
                U = G * B
                values(U - 1, G - 1, NS - 2)
                values(U - 1, G - 1, NS - 1)
                out_turn(U - 1, 1)
                wait(pe, s_["o_used"], 2 * U)
                for i in range(4):
                    wait(pe, s_["e_used"], 4 * (B - 1) + i - 1)
                    attn_turn(B - 1, i, (m1, m2)[i % 2])
                for i in range(4):
                    wait(pe, s_["w_used"], 4 * (B - 1) + i - 1)
                    wait(pe, s_["e_used"], 4 * (B - 1) + i + 1)
                    out_project(B - 1, i, (m0, acc)[i % 2])

            @block.scalar
            def _(act):
                def exps(u, k, pr):
                    wait(act, s_["pv"], NS * u + k - 2)
                    wait(act, s_["st"], EX * u + 2 * k + pr + 1)
                    act.activation(prob[k % 3][:, 2 * pr:2 * pr + 2, 0:width(k)], st_ps[pr][:, :, 0:width(k)], ACT.Exp,
                                   scale=SCALE).then_inc(s_["exp"], 1)

                def copy_v(n, sl):
                    wait(act, s_["v_full"], n + 1)
                    wait(act, s_["pv"], NS * (n - 1))
                    act.activation(v_op[sl][:, :, :, 0:DK], m2[:].rearrange("p (t h d) -> p t h d", t=TB, h=HG), ACT.Copy).then_inc(s_["v_used"], 1)

                def square(n):
                    wait(act, s_["rot"], 2 * n + 2)
                    wait(act, s_["n_full"], n)
                    act.activation(squares[:], qk[:], ACT.Square).then_inc(s_["sq"], 1)

                def copy_o(u, half):
                    wait(act, s_["pv"], NS * u + (8, 12)[half])
                    wait(act, s_["o_used"], 2 * (u - 1) + half + 1)
                    act.activation(o_t[half][:], acc[:], ACT.Copy).then_inc(s_["o_copied"], 1)

                def copy_attn(bp, i, bank):
                    t0 = (4, 6, 0, 2)[i]
                    wait(act, s_["e_full"], 4 * bp + i + 1)
                    wait(act, s_["w_full"], 4 * bp)
                    act.activation(attn_t[:].rearrange("p c (t s) -> p t c s", s=P)[:, t0:t0 + 2],
                                   bank[:].rearrange("p (t c s) -> p t c s", t=2, c=C), ACT.Copy).then_inc(s_["e_used"], 1)

                def copy_tokens(m, p):
                    wait(act, s_["mt_full"], CREDIT + m + 1)
                    wait(act, s_["mm_full"], CREDIT + m - 1)
                    act.activation(xt_m[p % 2][:].rearrange("p t c s -> p (t c s)"), m1[:], ACT.Copy).then_inc(s_["mt_used"], 1)

                def relu(m, p):
                    wait(act, s_["mm_used"], CREDIT + m + 1)
                    act.activation(y_m[p % 2][:], y_m[p % 2][:], ACT.Relu).then_inc(s_["y_relu"], 1)

                def unit(b, g, kd):
                    u = G * b + g
                    n = u + 1
                    prev, nxt = has_prev(b, g), has_next(b, g)
                    tail = g == 0 and has_prev_batch(b)
                    moe = kd == "moe"
                    m = pair0(b, g) if moe else None
                    for k in range(NS):
                        exps(u, k, 0)
                        exps(u, k, 1)
                        if moe and k % 2 == 0:
                            copy_tokens(m + k // 2, k // 2)
                        if k == 2 and nxt:
                            copy_v(n, (g + 1) % 2)
                        if k == 2 and prev:
                            copy_o(u - 1, 1)
                        if tail and k in (4, 5):
                            copy_attn(b - 1, 2 * (k - 4), m1)
                            copy_attn(b - 1, 2 * (k - 4) + 1, m2)
                        if k == 5 and nxt:
                            square(n)
                        if moe and k % 2 == 1:
                            relu(m + k // 2, k // 2)
                        if k == 9:
                            copy_o(u, 0)

                act.sem_inc(s_["mt_used"], CREDIT)
                act.wait_ge(s_["ones"], 1)
                copy_v(0, 0)
                square(0)
                walk(act, unit)
                U = G * B
                copy_o(U - 1, 1)
                for i in range(4):
                    copy_attn(B - 1, i, (m1, m2)[i % 2])

            @block.vector
            def _(dve):
                def rotate(n, hf):
                    bank = (m0, m1)[hf]
                    cols = slice(hf * HALF, (hf + 1) * HALF)
                    wait(dve, s_["qk_full"], 2 * n + hf + 1)
                    wait(dve, s_["split"], 4 * n)
                    dve.tensor_tensor(rot_a[:, cols], bank[:], cosT[:, cols], ALU.mult)
                    dve.stream_shuffle(rot_b[:, cols], bank[:], [i ^ HG for i in range(32)]).then_inc(s_["qk_used"], 1)

                def split(n):
                    wait(dve, s_["rot"], 2 * n + 2)
                    wait(dve, s_["part_out"], 16 * n)
                    dve.tensor_copy(parts[:, 0, :], qk[:]).then_inc(s_["split"], 1)
                    wait(dve, s_["split"], 4 * n + 1)
                    dve.tensor_tensor(rot_a[:], qk[:], parts[:, 0, :], ALU.subtract).then_inc(s_["split"], 1)
                    wait(dve, s_["split"], 4 * n + 2)
                    dve.tensor_copy(parts[:, 1, :], rot_a[:]).then_inc(s_["split"], 1)
                    wait(dve, s_["split"], 4 * n + 3)
                    dve.tensor_tensor(parts[:, 2, :], rot_a[:], parts[:, 1, :], ALU.subtract).then_inc(s_["split"], 1)

                def norm_max(n):
                    wait(dve, s_["n_full"], n + 1)
                    dve.tensor_reduce(nmax[:], m2[:, 0:TB * 2 * HG], X, ALU.max).then_inc(s_["n_used"], 1)

                def bound(n, sl):
                    wait(dve, s_["nt_full"], n + 1)
                    dve.tensor_reduce(nbound[:], m0[0:1, 0:P], X, ALU.max).then_inc(s_["nt_used"], 1)
                    wait(dve, s_["nt_used"], n + 1)
                    wait(dve, s_["slow_pe"], SLOW_PE * n)
                    dve.tensor_scalar(flag[:], nbound[:], NORM2, None, ALU.is_gt).then_inc(s_["flagged"], 1)
                    wait_apart(dve, s_["flagged"], n + 1, s_tick)
                    if not (isinstance(n, int) and n == 0):
                        wait_apart(dve, s_["max_out"], 16 * n, s_tick)
                    v = dve.value_load(flag[0:1, 0:1], min_val=0, max_val=1)
                    with dve.If(v > 0):
                        find_max(n)
                    with dve.Else():
                        dve.sem_inc(s_["slow_dve"], SLOW_DVE)
                        dve.memset(maxrow[:], 0.0).then_inc(s_["maxready"], 1)

                def find_max(n):
                    c0 = CREDIT + SLOW_DVE * n
                    tmp = rot_a[:, 0:HALF]
                    with dve.Fori(0, TB) as i:
                        for w in range(2 * HG):
                            h, half = w // 2, w % 2
                            at = 2 * HG * i + w
                            wait_apart(dve, s_["slow_pe"], SLOW_PE * n + at + 1, s_tick)
                            dve.tensor_tensor(tmp, m0[:], masks[:, ds(MASK0 + half * HALF - i * P, HALF)], ALU.add).then_inc(s_["slow_dve"], 1)
                            dve.wait_ge(s_["slow_dve"], c0 + 2 * at + 1)
                            dve.tensor_reduce(rowmax[:, ds(i, 1), h, half:half + 1], tmp, X, ALU.max).then_inc(s_["slow_dve"], 1)
                    c0 = c0 + 2 * SLOW
                    dve.wait_ge(s_["slow_dve"], c0)
                    dve.tensor_reduce(rm[:].rearrange("p (h t) -> p h t", h=HG), rowmax[:].rearrange("p t h w -> p h t w"), X, ALU.max).then_inc(s_["slow_dve"], 1)
                    dve.wait_ge(s_["slow_dve"], c0 + 1)
                    dve.tensor_scalar(rm[:], rm[:], -1.0, None, ALU.mult).then_inc(s_["slow_dve"], 1)
                    for r in range(2):
                        dve.wait_ge(s_["slow_dve"], c0 + 2 + 2 * r)
                        dve.tensor_copy(rmb[:, r, :], rm[:]).then_inc(s_["slow_dve"], 1)
                        dve.wait_ge(s_["slow_dve"], c0 + 3 + 2 * r)
                        dve.tensor_tensor(rm[:] if r == 0 else rmb[:, 2, :], rm[:], rmb[:, r, :], ALU.subtract).then_inc(s_["slow_dve"], 1)
                    dve.wait_ge(s_["slow_pe"], SLOW_PE * (n + 1))
                    dve.tensor_copy(maxrow[:].rearrange("p r s -> p (r s)"), m0[0:HG * TB, 0:3 * P]).then_inc(s_["maxready"], 1)

                def normalise(u, g, half):
                    bank = (m1 if half == 0 else m0)[:].rearrange("p (t h d) -> p t h d", t=4, h=HG)
                    t0 = 4 * (1 - half)
                    wait(dve, s_["o_full"], 2 * u + half + 1)
                    dve.reciprocal(inv[:], bank[:, :, :, DK]).then_inc(s_["o_inv"], 1)
                    wait(dve, s_["o_inv"], 2 * u + half + 1)
                    dve.tensor_tensor(attn[:, t0:t0 + 4, g * GD:(g + 1) * GD].rearrange("p t (h d) -> p t h d", h=HG),
                                      bank[:, :, :, 0:DK], inv[:].unsqueeze(3).broadcast_to([P, 4, HG, DK]), ALU.mult).then_inc(s_["o_used"], 1)

                def add_resid(bp, i, bank):
                    wait(dve, s_["w_full"], 4 * bp + i + 1)
                    wait(dve, s_res_in[i % 2], 16 * (2 * bp + i // 2 + 1))
                    dve.tensor_tensor(resid[i % 2][:].rearrange("p t d -> p (t d)"), bank[:], resid[i % 2][:].rearrange("p t d -> p (t d)"),
                                      ALU.add).then_inc(s_["w_used"], 1)

                def add_bias(b, g, p):
                    m = pair0(b, g) + p
                    wait(dve, s_["ew_in"], 32)
                    wait(dve, s_["mm_full"], CREDIT + m + 1)
                    wait(dve, s_yst[p % 2], 16 * (round0(b, g, 2) + p // 2 + 1))
                    for t in range(2):
                        e = dve.value_load(tile_expert[0:1, ds(2 * m + t, 1)], min_val=0, max_val=E - 1)
                        last = dve.tensor_tensor(y_m[p % 2][:, t, :], m2[:, t * D:(t + 1) * D],
                                                 ebias[:, ds(e, 1), :].rearrange("p o d -> p (o d)"), ALU.add)
                    last.then_inc(s_["mm_used"], 1)

                def combine(b, g, i):
                    c = tile_c0(b, g) + i
                    wait(dve, s_yc[i % 2], 32 * (crounds(b, g) + i // 2 + 1))
                    wait(dve, s_hc[i % 2], 16 * (crounds(b, g) + i // 2 + 1))
                    dve.scalar_tensor_tensor(h_c[i % 2], y_c[i % 2][:, 0, :], w_top[:, 0, ds(c, 1)], h_c[i % 2], ALU.mult, ALU.add).then_inc(s_["h_c1"], 1)
                    wait(dve, s_["h_c1"], c + 1)
                    dve.scalar_tensor_tensor(h_c[i % 2], y_c[i % 2][:, 1, :], w_top[:, 1, ds(c, 1)], h_c[i % 2], ALU.mult, ALU.add).then_inc(s_["combined"], 1)

                def unit(b, g, kd):
                    u = G * b + g
                    n = u + 1
                    prev, nxt = has_prev(b, g), has_next(b, g)
                    tail = g == 0 and has_prev_batch(b)
                    moe = kd == "moe"
                    m = pair0(b, g) if moe else None
                    for k in range(NS):
                        if k in (0, 1) and nxt:
                            rotate(n, k)
                        if k == 3 and prev:
                            normalise(u - 1, (g - 1) % G, 1)
                        if k == 4 and nxt:
                            split(n)
                        if moe and k % 2 == 1:
                            add_bias(b, g, k // 2)
                        if k == 6 and nxt:
                            norm_max(n)
                        if tail and k in (7, 9):
                            add_resid(b - 1, k - 7, m0)
                            add_resid(b - 1, k - 6, m1)
                        if k == 8 and nxt:
                            bound(n, (g + 1) % 2)
                        if kd == "comb" and k % 3 == 2:
                            combine(b, g, k // 3)
                        if k == 10:
                            if tail:
                                wait(dve, s_["e_full"], 4 * b)
                            normalise(u, g, 0)

                dve.sem_inc(s_["combined"], CREDIT)
                dve.sem_inc(s_["slow_dve"], CREDIT)
                dve.sem_inc(s_["mm_used"], CREDIT)
                dve.memset(k_op[0][96:99, :, :], 1.0)
                dve.memset(k_op[1][96:99, :, :], 1.0)
                dve.memset(v_op[0][:, :, :, DK:2 * DK], 1.0)
                dve.memset(v_op[1][:, :, :, DK:2 * DK], 1.0).then_inc(s_["ones"], 1)
                rotate(0, 0)
                rotate(0, 1)
                split(0)
                norm_max(0)
                bound(0, 0)
                walk(dve, unit)
                U = G * B
                normalise(U - 1, G - 1, 1)
                for i in range(4):
                    add_resid(B - 1, i, (m0, acc)[i % 2])
                for i in range(T - tile_c0(B, 0)):
                    combine(B, 0, i)

            @block.gpsimd
            def _(pool):
                def rotate(n, hf):
                    cols = slice(hf * HALF, (hf + 1) * HALF)
                    wait(pool, s_["qk_used"], 2 * n + hf + 1)
                    pool.tensor_tensor(rot_b[:, cols], rot_b[:, cols], sinT[:, cols], ALU.mult).then_inc(s_["rot_mul"], 1)
                    wait(pool, s_["split"], 4 * n)
                    wait(pool, s_["sq"], n)
                    wait(pool, s_["rot_mul"], 2 * n + hf + 1)
                    pool.tensor_tensor(qk[:, cols], rot_a[:, cols], rot_b[:, cols], ALU.add).then_inc(s_["rot"], 1)

                def scatter(t):
                    for s in range(2):
                        pool.indirect_dma_start(list_d, bass.IndirectOffsetOnAxis(ap=list_at[:, s, t:t + 1], axis=0),
                                                token[:, t:t + 1], None).then_inc(s_["scattered"], 16)

                def gather_tokens(m, sl):
                    wait(pool, s_["mt_full"], CREDIT + m - 2)
                    pool.wait_ge(s_["listed"], 16)
                    pool.tensor_copy(pick_m[sl][:], lists[:, ds(2 * m, 2)]).then_inc(s_["picked"], 1)
                    wait_apart(pool, s_["picked"], m + 1, s_tick)
                    for t in range(2):
                        pool.indirect_dma_start(x_m[sl][:, t, :], None, xn_d,
                                                bass.IndirectOffsetOnAxis(ap=pick_m[sl][:, t:t + 1], axis=0)).then_inc(s_xm[sl], 16)

                def gather_outputs(c, sl):
                    wait(pool, s_["combined"], CREDIT + c - 1)
                    pool.wait_ge(s_["listed"], 16)
                    for s in range(2):
                        last = pool.tensor_copy(pick_c[sl][:, s:s + 1], y_row[:, s, ds(c, 1)])
                    last.then_inc(s_["pick_c_made"], 1)
                    wait_apart(pool, s_["pick_c_made"], c + 1, s_tick)
                    for s in range(2):
                        pool.indirect_dma_start(y_c[sl][:, s, :], None, y_d,
                                                bass.IndirectOffsetOnAxis(ap=pick_c[sl][:, s:s + 1], axis=0)).then_inc(s_yc[sl], 16)

                def unit(b, g, kd):
                    u = G * b + g
                    n = u + 1
                    nxt = has_next(b, g)
                    for k in range(NS):
                        if k in (0, 1) and nxt:
                            rotate(n, k)
                        if kd == "plain" and k < 8:
                            scatter(8 * u + k)
                        if kd == "moe" and k % 2 == 1:
                            gather_tokens(pair0(b, g) + k // 2 + 2, (k // 2 + 2) % 3)
                        if kd == "comb" and k % 3 == 1:
                            gather_outputs(tile_c0(b, g) + k // 3, (k // 3) % 2)
                    if kd == "plain" and isinstance(b, int) and b == B_MOE - 1 and g == G - 1:
                        pool.wait_ge(s_["scattered"], 16 * 2 * T)
                        pool.wait_ge(s_["zeroed"], 1)
                        pool.dma_start(lists[:, 0:MT], list_d.rearrange("(p m) o -> p (m o)", p=P)).then_inc(s_["listed"], 16)
                        gather_tokens(0, 0)
                        gather_tokens(1, 1)

                pool.memset(lists[:], 0).then_inc(s_["zeroed"], 1)
                rotate(0, 0)
                rotate(0, 1)
                for b in range(B_MOE):
                    for g in range(G):
                        unit(b, g, "plain")
                with pool.Fori(B_MOE, B_COMB) as b:
                    for g in range(G):
                        unit(b, g, "moe")
                for sl in range(3):
                    pool.wait_ge(s_xm[sl], 32 * ((PAIRS + 2 - sl + 2) // 3))
                pool.wait_ge(s_["mt_full"], CREDIT + PAIRS)
                for sl in range(2):
                    pool.wait_ge(s_yst[sl], 16 * (PAIRS // 2 + 1))
                with pool.Fori(B_COMB, B_LAST) as b:
                    for g in range(G):
                        unit(b, g, "comb")
                for g in range(G):
                    unit(B_LAST, g, "comb")
                for c in range(tile_c0(B, 0), T):
                    gather_outputs(c, c % 2)

            @block.sync
            def _(sp):
                def wait_sp(sem, value):
                    if isinstance(value, int):
                        wait(sp, sem, value)
                    else:
                        wait_apart(sp, sem, value, s_tick)

                def load_xT(bn):
                    wait_sp(s_["v_full"], 4 * bn)
                    sp.dma_start(xT[:], xnt_d[ds(bn, 1)].rearrange("o p c s -> p (o c) s")).then_inc(s_["xT_in"], 16)

                def stack(n, sl):
                    wait_sp(s_["split"], 4 * n + 4)
                    wait_sp(s_["st"], EX * (n - 1))
                    sp.dma_start(part_d[sl].rearrange("r w d (h s) -> (w d h) r s", h=HG), parts[:]).then_inc(s_["part_out"], 16)
                    wait_sp(s_["part_out"], 16 * (n + 1))
                    d = part_d[sl]
                    sp.dma_start(flat(q_op[sl][0:48]), again(d[0, 0], 3)).then_inc(s_load[sl], 16)
                    sp.dma_start(flat(q_op[sl][48:80]), again(d[1, 0], 2)).then_inc(s_load[sl], 16)
                    sp.dma_start(flat(q_op[sl][80:96]), d[2, 0]).then_inc(s_load[sl], 16)
                    sp.dma_start(flat(k_op[sl][0:48]), d[0:3, 1]).then_inc(s_load[sl], 16)
                    sp.dma_start(flat(k_op[sl][48:80]), d[0:2, 1]).then_inc(s_load[sl], 16)
                    sp.dma_start(flat(k_op[sl][80:96]), d[0, 1]).then_inc(s_load[sl], 16)

                def flat(v):
                    return v.rearrange("p h s -> p (h s)")

                def again(v, times):
                    return bass.AP(tensor=v.tensor, offset=v.offset, ap=[[0, times]] + [list(q) for q in v.ap])

                def load_max(n, sl):
                    wait_sp(s_["maxready"], n + 1)
                    sp.dma_start(max_d[sl].rearrange("r h t s -> (h t) r s"), maxrow[:]).then_inc(s_["max_out"], 16)
                    wait_sp(s_["max_out"], 16 * (n + 1))
                    sp.dma_start(q_op[sl][96:99], max_d[sl].rearrange("r h t s -> r h (t s)")).then_inc(s_load[sl], 16)

                def load_resid(bp, i):
                    t0 = (4, 6, 0, 2)[i]
                    wait_sp(s_res_out[i % 2], 16 * (2 * bp + i // 2))
                    sp.dma_start(resid[i % 2][:], x_rows[ds(bp * S + t0 * P, 2 * P)].rearrange("(t p) d -> p t d", p=P)).then_inc(s_res_in[i % 2], 16)

                def store_h(bp, i):
                    t0 = (4, 6, 0, 2)[i]
                    wait_sp(s_["w_used"], 4 * bp + i + 1)
                    sp.dma_start(h_d[ds(bp * S + t0 * P, 2 * P)].rearrange("(t p) d -> p t d", p=P), resid[i % 2][:]).then_inc(s_res_out[i % 2], 16)

                def store_y(m, p):
                    wait_sp(s_["y_relu"], m + 1)
                    sp.dma_start(y_d[ds(2 * m * P, 2 * P)].rearrange("(t p) d -> p t d", p=P), y_m[p % 2][:]).then_inc(s_yst[p % 2], 16)

                def load_h(b, g, i):
                    c = tile_c0(b, g) + i
                    wait_sp(s_oc[i % 2], 16 * (crounds(b, g) + i // 2 + 1))
                    sp.dma_start(h_c[i % 2], h_d[ds(c * P, P)]).then_inc(s_hc[i % 2], 16)

                def store_out(b, g, i):
                    c = tile_c0(b, g) + i
                    wait_sp(s_["combined"], CREDIT + c + 1)
                    sp.dma_start(out_rows[ds(c * P, P)], h_c[i % 2]).then_inc(s_oc[i % 2], 16)

                def unit(b, g, kd):
                    u = G * b + g
                    n = u + 1
                    prev, nxt = has_prev(b, g), has_next(b, g)
                    tail = g == 0 and has_prev_batch(b)
                    moe = kd == "moe"
                    m = pair0(b, g) if moe else None
                    c0 = tile_c0(b, g) if kd == "comb" else None
                    for k in range(NS):
                        if k == 2 and g == G - 2 and nxt and not (isinstance(b, int) and b == B_LAST):
                            load_xT(b + 1)
                        if tail and k == 0:
                            load_resid(b - 1, 0)
                            load_resid(b - 1, 1)
                        if k == 5 and nxt:
                            stack(n, (g + 1) % 2)
                        if moe and k % 2 == 1 and k >= 3:
                            store_y(m + k // 2 - 1, k // 2 - 1)
                        if tail and k == 8:
                            store_h(b - 1, 0)
                            store_h(b - 1, 1)
                            load_resid(b - 1, 2)
                            load_resid(b - 1, 3)
                        if k == 9 and nxt:
                            load_max(n, (g + 1) % 2)
                        if tail and k == 11:
                            store_h(b - 1, 2)
                            store_h(b - 1, 3)
                            if kd == "comb":
                                pass
                        if kd == "comb" and k % 3 == 0:
                            load_h(b, g, k // 3)
                        if kd == "comb" and k % 3 == 2:
                            store_out(b, g, k // 3)
                    if moe:
                        store_y(m + PU - 1, PU - 1)

                for i in range(2):
                    sp.sem_inc(s_yst[i], 16)
                    sp.sem_inc(s_oc[i], 16)
                load_xT(0)
                sp.dma_start(ew[:], a["expert_wT"].rearrange("e (c p) d -> p e c d", p=P)).then_inc(s_["ew_in"], 16)
                sp.dma_start(ebias[:], a["expert_b"].unsqueeze(0).broadcast_to([P, E, D])).then_inc(s_["ew_in"], 16)
                stack(0, 0)
                load_max(0, 0)
                walk(sp, unit)
                for i in range(4):
                    if i < 2:
                        load_resid(B - 1, i)
                for i in range(2):
                    store_h(B - 1, i)
                    load_resid(B - 1, i + 2)
                for i in range(2, 4):
                    store_h(B - 1, i)
                for i in range(2):
                    sp.wait_ge(s_res_out[i], 16 * 2 * B)
                rest = T - tile_c0(B, 0)
                for i in range(2):
                    load_h(B, 0, i)
                for i in range(rest):
                    store_out(B, 0, i)
                    if i + 2 < rest:
                        load_h(B, 0, i + 2)
                for i in range(2):
                    sp.wait_ge(s_oc[i], 16 * (T // 2 + 1))


_NAMES = {"x": "L0_attn_x", "Wv": "L0_attn_Wv", "Wo": "L0_attn_Wo", "expert_b": "L0_ffn_expert_b"}


def _shape_constants():
    inv_freq = (np.float32(1.0) / np.power(np.float32(10000.0), np.arange(0, DK, 2, dtype=np.float32) / np.float32(DK))).astype(np.float32)
    ang = np.outer(np.arange(S, dtype=np.float32), inv_freq).astype(np.float32)
    cos, sin = np.cos(ang).astype(np.float32), np.sin(ang).astype(np.float32)
    dim = np.arange(P) // HG % DK
    pair = dim // 2
    sign = np.where(dim % 2 == 0, -1.0, 1.0).astype(np.float32)
    head = np.arange(P) % HG + HG * (np.arange(P) // GD)
    return {
        "cosT": np.ascontiguousarray(cos[:, pair].T),
        "sinT": np.ascontiguousarray(sin[:, pair].T * sign[:, None]),
        "ident": np.eye(P, dtype=np.float32),
        "upper": np.triu(np.ones((P, P), np.float32), 1),
        "lower": np.tril(np.ones((P, P), np.float32), -1),
        "headsum": (head[:, None] == np.arange(2 * HG)[None, :]).astype(np.float32),
        "iota_e": np.tile(np.arange(E, dtype=np.float32) - 99.0, (P, 1)),
        "masks": np.where(np.arange(MASKW)[None, :] - MASK0 <= np.arange(P)[:, None], np.float32(0), np.float32(BIG)),
        "iota_m": np.arange(MT, dtype=np.float32)[None, :],
    }


def kernel(**inputs):
    import concourse.bacc as _bacc
    from concourse.bass_utils import run_bass_kernel_spmd as _run

    nc = _bacc.Bacc("TRN2", target_bir_lowering=False, num_devices=1)
    arrays = {k: np.ascontiguousarray(inputs[v]) for k, v in _NAMES.items()}
    arrays["gate_wT"] = np.ascontiguousarray(np.asarray(inputs["L0_ffn_gate_w"]).T)
    arrays["expert_wT"] = np.ascontiguousarray(np.asarray(inputs["L0_ffn_expert_w"]).transpose(0, 2, 1))
    wq, wk = (np.asarray(inputs[k]).reshape(C, P, G, HG, DK).transpose(1, 2, 0, 4, 3).reshape(P, G, C, GD) for k in ("L0_attn_Wq", "L0_attn_Wk"))
    arrays["Wqk"] = np.ascontiguousarray(np.concatenate([wq, wk], axis=3))
    arrays.update(_shape_constants())
    feeds, a = {}, {}
    for name, v in arrays.items():
        feeds[f"in_{name}"] = v
        a[name] = nc.dram_tensor(f"in_{name}", v.shape, mybir.dt.from_np(v.dtype), kind="ExternalInput").ap()
    a["out"] = nc.dram_tensor("out_0", (B, S, D), F32, kind="ExternalOutput").ap()
    build(nc, a)
    r = _run(nc, [feeds], core_ids=[0])
    return r.results[0]["out_0"]
```

```python
from contextlib import ExitStack

import numpy as np

import concourse.bass as bass
from concourse import mybir

F32 = mybir.dt.float32
BF16 = mybir.dt.bfloat16
I32 = mybir.dt.int32
ALU = mybir.AluOpType
ACT = mybir.ActivationFunctionType
X = mybir.AxisListType.X
ds = bass.ds

P = 128
B, S, D = 8, 1024, 256
H, DK = 16, 16
G = 4
HG = H // G
GD = HG * DK
C = D // P
TB = S // P
T = B * TB
N = B * S
E = 16
MT = 2 * N // P + E
PAIRS = MT // 2
PU = 6
B_MOE, B_COMB = 2, 5
B_LAST = B - 1
CU = 4
CU_LAST = 6
assert (B_COMB - B_MOE) * G * PU == PAIRS
assert G * (CU * (B_LAST - B_COMB) + CU_LAST) == T - TB
HALF = S // 2
SCALE = DK ** -0.5
SAFE = 60.0
NORM2 = SAFE / SCALE
BIG = -1.0e38
EPS = 1e-5

STEPS = [(1, j) for j in range(8)] + [(0, j) for j in range(4)]
NS = len(STEPS)
EX = 2 * NS
MK = NS - 4
SLOTS_Q = [0, 0, 0, 1, 1, 2]
SLOTS_K = [0, 1, 2, 0, 1, 0]
CREDIT = 2
MASK0 = S - P
MASKW = MASK0 + S
SLOW = TB * HG * 2
SLOW_PE = SLOW + 1
SLOW_DVE = 2 * SLOW + 6
LAST = [(0, 1, 2), (3, 4, 5), (6, 7)]
XS = 4
NLOAD = 7


def first_q(k):
    hf, j = STEPS[k]
    return max(HALF * hf, P * j)


def width(k):
    return HALF * (STEPS[k][0] + 1) - first_q(k)


def is_diag(k):
    hf, j = STEPS[k]
    return j * P >= HALF * hf


def wait(eng, sem, value):
    if isinstance(value, int) and value <= 0:
        return
    eng.wait_ge(sem, value)


def wait_apart(eng, sem, value, tick):
    eng.wait_ge(sem, value)
    eng.sem_inc(tick, 1)


def build(nc, a):
    xnt_d = nc.dram_tensor("xnt_scratch", [B, P, C, S], F32, kind="Internal").ap()
    xn_d = nc.dram_tensor("xn_scratch", [N, D], F32, kind="Internal").ap()
    h_d = nc.dram_tensor("h_scratch", [N, D], F32, kind="Internal").ap()
    y_d = nc.dram_tensor("y_scratch", [MT * P, D], F32, kind="Internal").ap()
    list_d = nc.dram_tensor("list_scratch", [P * MT, 1], I32, kind="Internal").ap()
    part_d = [nc.dram_tensor(f"part_scratch{i}", [3, 2, DK, HG * S], BF16, kind="Internal").ap() for i in range(2)]
    bias_d = nc.dram_tensor("bias_scratch", [3, E, D], BF16, kind="Internal").ap()
    max_d = [nc.dram_tensor(f"max_scratch{i}", [3, HG, TB, P], BF16, kind="Internal").ap() for i in range(2)]

    x_rows = a["x"].rearrange("b s d -> (b s) d")
    out_rows = a["out"].rearrange("b s d -> (b s) d")

    with ExitStack() as ctx:
        def sb(name, shape, dt=F32, to=ctx):
            return to.enter_context(nc.sbuf_tensor(name, shape, dt))

        def sem(name):
            return ctx.enter_context(nc.semaphore(name))

        ident = sb("ident", [P, P])
        identb = sb("identb", [P, P], BF16)
        headsum = sb("headsum", [P, 2 * HG], BF16)
        wv = sb("wv", [P, C, D])
        wo = sb("wo", [P, C, D])
        wqk = sb("wqk", [P, G, C, P])
        cosT = sb("cosT", [P, S])
        sinT = sb("sinT", [P, S])
        w_top = sb("w_top", [P, 2, T])
        y_row = sb("y_row", [P, 2, T], I32)
        list_at = sb("list_at", [P, 2, T], I32)
        token = sb("token", [P, T], I32)
        tile_expert = sb("tile_expert", [1, MT], I32)
        zero_i = sb("zero_i", [P, MT], I32)
        ebias = sb("ebias", [3, E, D], BF16)
        ones3 = sb("ones3", [3, P], BF16)
        future = sb("future", [P, P], BF16)
        masks = sb("masks", [P, MASKW], BF16)

        s_const = sem("s_const")
        s_made = sem("s_made")
        s_tick = sem("s_tick")

        with ExitStack() as p1:
            def sb1(name, shape, dt=F32):
                return sb(name, shape, dt, p1)

            def ps1(name, shape, dt=F32):
                return p1.enter_context(nc.psum_tensor(name, shape, dt))

            gate = sb1("gate", [P, C, E])
            xin = [sb1(f"xin{i}", [P, TB, D]) for i in range(XS)]
            xt = [sb1(f"xt_out{i}", [P, C, S]) for i in range(2)]
            stat = sb1("stat", [P, TB, 6])
            mv = sb1("mv", [P, TB, 2])
            vareps = sb1("vareps", [P, TB])
            std = sb1("std", [P, TB])
            rstd = sb1("rstd", [P, TB])
            logits = sb1("logits", [P, TB + T, E])
            logit = logits[:, TB:TB + T, :]
            iota_e = sb1("iota_e", [P, E])
            iota_m = sb1("iota_m", [1, MT])
            ones_b = sb1("ones_b", [P, P], BF16)
            upper_b = sb1("upper_b", [P, P], BF16)
            lower = sb1("lower", [P, P])
            bias_f = sb1("bias_f", [E, D])
            bias_p = sb1("bias_p", [E, 3, D], BF16)
            constf = sb1("constf", [P, P])
            work = [sb1(f"work{i}", [P, T, E]) for i in range(3)]
            hot = [sb1(f"hot{i}", [P, T, E]) for i in range(2)]
            hotb = sb1("hotb", [P, T, E], BF16)
            top = [sb1(f"top{i}", [P, T]) for i in range(2)]
            pick = sb1("pick", [P, T])
            den = sb1("den", [P, T])
            rden = sb1("rden", [P, T])
            onesT = sb1("onesT", [P, T])
            cnt = sb1("cnt", [P, E])
            cnt_i = sb1("cnt_i", [P, E], I32)
            nt_f = sb1("nt_f", [P, E])
            inc = sb1("inc", [P, E])
            base = sb1("base", [P, E])
            ones_e = sb1("ones_e", [P, E])
            posf = sb1("posf", [P, 2, T])
            lo_i = sb1("lo_i", [P, 2, T], I32)
            hi_i = sb1("hi_i", [P, 2, T], I32)
            at_f = sb1("at_f", [P, 2, T])
            ge = sb1("ge", [1, MT, E])
            te_f = sb1("te_f", [1, MT])

            turn = [ps1(f"turn{i}", [P, 4, P]) for i in range(4)]
            lg = ps1("lg", [P, 2 * P])
            lgt = sb1("lgt", [P, 2 * P])
            rank = ps1("rank", [P, 2, T // 2, E])

            s_x = [sem(f"s_x{i}") for i in range(XS)]
            s_var = sem("s_var")
            s_std = sem("s_std")
            s_ln = sem("s_ln")
            s_turn = sem("s_turn")
            s_xt = sem("s_xt")
            s_lg = sem("s_lg")
            s_lgm = sem("s_lgm")
            s_lgt = sem("s_lgt")
            s_lgc = sem("s_lgc")
            s_xn_st = [sem(f"s_xn_st{i}") for i in range(XS)]
            s_xt_st = [sem(f"s_xt_st{i}") for i in range(2)]
            s_r = sem("s_r")
            s_ract = sem("s_ract")
            s_rpe = sem("s_rpe")
            s_zero = sem("s_zero")
            s_list0 = sem("s_list0")
            s_bias = sem("s_bias")
            s_bias_d = sem("s_bias_d")

            with nc.Block() as block:

                @block.sync
                def _(sp):
                    def load_x(n):
                        sp.dma_start(xin[n % XS][:], a["x"][n].rearrange("(t p) d -> p t d", p=P)).then_inc(s_x[n % XS], 16)

                    load_x(0)
                    sp.dma_start(ident[:], a["ident"]).then_inc(s_const, 16)
                    sp.dma_start(bias_f[:], a["expert_b"]).then_inc(s_const, 16)
                    sp.dma_start(lower[:], a["lower"]).then_inc(s_const, 16)
                    sp.dma_start(constf[:], a["upper"]).then_inc(s_const, 16)
                    sp.dma_start(gate[:], a["gate_wT"].rearrange("(c p) e -> p c e", p=P)).then_inc(s_const, 16)
                    sp.dma_start(iota_e[:], a["iota_e"]).then_inc(s_const, 16)
                    sp.dma_start(iota_m[:], a["iota_m"]).then_inc(s_const, 16)
                    sp.dma_start(work[0][:, 0, 0:2 * HG], a["headsum"]).then_inc(s_const, 16)
                    sp.dma_start(wv[:], a["Wv"].rearrange("(c p) n -> p c n", p=P)).then_inc(s_const, 16)
                    sp.dma_start(wo[:], a["Wo"].rearrange("(c p) n -> p c n", p=P)).then_inc(s_const, 16)
                    sp.dma_start(wqk[:], a["Wqk"]).then_inc(s_const, 16)
                    sp.dma_start(cosT[:], a["cosT"]).then_inc(s_const, 16)
                    sp.dma_start(sinT[:], a["sinT"]).then_inc(s_const, 16)
                    sp.dma_start(xt[1][:].rearrange("p c s -> p (c s)")[:, 0:MASKW], a["masks"]).then_inc(s_const, 16)
                    for n in range(1, XS):
                        load_x(n)
                    sp.wait_ge(s_zero, 1)
                    sp.dma_start(list_d.rearrange("(p m) o -> p (m o)", p=P), zero_i[:]).then_inc(s_list0, 16)
                    for n in range(B):
                        sp.wait_ge(s_ln, n + 1)
                        sp.dma_start(xn_d[n * S:(n + 1) * S].rearrange("(t p) d -> p t d", p=P), xin[n % XS][:]).then_inc(s_xn_st[n % XS], 16)
                        sp.wait_ge(s_xt, CREDIT + 4 * n + 4)
                        sp.dma_start(xnt_d[n], xt[n % 2][:]).then_inc(s_xt_st[n % 2], 16)
                        if 1 <= n and n - 1 + XS < B:
                            sp.wait_ge(s_xn_st[(n - 1) % XS], 16 * ((n - 1) // XS + 1))
                            load_x(n - 1 + XS)
                    sp.wait_ge(s_bias, 5)
                    sp.dma_start(bias_d.rearrange("r e d -> e r d"), bias_p[:]).then_inc(s_bias_d, 16)
                    sp.wait_ge(s_bias_d, 16)
                    sp.dma_start(ebias[:], bias_d).then_inc(s_bias_d, 16)
                    sp.wait_ge(s_bias_d, 32)
                    for i in range(XS):
                        sp.wait_ge(s_xn_st[i], 16 * (B // XS))
                    for i in range(2):
                        sp.wait_ge(s_xt_st[i], 16 * (B // 2 + 1))
                    sp.wait_ge(s_const, 16 * 14)
                    sp.wait_ge(s_list0, 16)

                @block.gpsimd
                def _(pool):
                    pool.memset(zero_i[:], 0).then_inc(s_zero, 1)
                    pool.iota(token[:], pattern=[[P, T]], base=0, channel_multiplier=1)
                    pool.memset(ones_b[:], 1.0)
                    pool.memset(onesT[:], 1.0)
                    pool.memset(ones3[:], 1.0)
                    pool.memset(ones_e[:], 1.0).then_inc(s_made, 1)

                @block.vector
                def _(dve):
                    dve.wait_ge(s_const, 16 * 14)
                    dve.memset(lg[:], 0.0).then_inc(s_lgc, CREDIT)
                    dve.sem_inc(s_lg, CREDIT)
                    dve.wait_ge(s_lgc, CREDIT)
                    dve.wait_ge(s_made, 1)
                    for r in range(3):
                        dve.tensor_copy(bias_p[:, r, :], bias_f[:]).then_inc(s_bias, 1)
                        dve.wait_ge(s_bias, 2 * r + 1)
                        if r < 2:
                            dve.tensor_tensor(bias_f[:], bias_f[:], bias_p[:, r, :], ALU.subtract).then_inc(s_bias, 1)
                            dve.wait_ge(s_bias, 2 * r + 2)
                    dve.tensor_copy(identb[:], ident[:])
                    dve.tensor_copy(upper_b[:], constf[:])
                    dve.tensor_scalar(future[:], lower[:], BIG, None, ALU.mult)
                    dve.tensor_copy(masks[:], xt[1][:].rearrange("p c s -> p (c s)")[:, 0:MASKW])
                    dve.tensor_copy(headsum[:], work[0][:, 0, 0:2 * HG]).then_inc(s_made, 1)
                    lg_tiles = lg[:].rearrange("p (w q e) -> p w q e", w=2, q=4)[:, :, :, 0:E]

                    def by_tile(v):
                        return v.rearrange("p (q w) e -> p w q e", w=2)

                    with dve.Fori(0, B // XS) as i:
                        for par in range(XS):
                            n = XS * i + par
                            xb = xin[par]
                            dve.wait_ge(s_x[par], 16 * (i + 1))
                            for t in range(TB):
                                last = dve.bn_stats(stat[:, t, :], xb[:, t, :])
                            last.then_inc(s_var, 1)
                            wait_apart(dve, s_var, 3 * n + 1, s_tick)
                            for t in range(TB):
                                last = dve.bn_aggr(mv[:, t, :], stat[:, t, :])
                            last.then_inc(s_var, 1)
                            dve.wait_ge(s_var, 3 * n + 2)
                            dve.tensor_scalar(vareps[:], mv[:, :, 1], EPS, None, ALU.add).then_inc(s_var, 1)
                            dve.wait_ge(s_lg, CREDIT + n)
                            dve.tensor_copy(by_tile(logits[:, ds(n * TB, TB), :]), lg_tiles).then_inc(s_lgc, 1)
                            dve.wait_ge(s_std, n + 1)
                            dve.reciprocal(rstd[:], std[:]).then_inc(s_lgc, 1)
                            dve.wait_ge(s_lgc, CREDIT + 2 * n + 2)
                            for t in range(TB):
                                last = dve.tensor_scalar(xb[:, t, :], xb[:, t, :], mv[:, t, 0:1],
                                                         rstd[:, t:t + 1], ALU.subtract, ALU.mult)
                            last.then_inc(s_ln, 1)
                    dve.wait_ge(s_lg, CREDIT + B)
                    dve.tensor_copy(by_tile(logit[:, T - TB:T, :]), lg_tiles).then_inc(s_lgc, 1)

                    step = [0]

                    def then(ins):
                        step[0] += 1
                        ins.then_inc(s_r, 1)
                        dve.wait_ge(s_r, step[0])

                    def over_e(v):
                        return v.unsqueeze(2).broadcast_to([P, T, E])

                    iota_b = iota_e[:].unsqueeze(1).broadcast_to([P, T, E])
                    dve.wait_ge(s_lgc, CREDIT + 2 * B + 1)
                    src = logits[:, TB:TB + T, :]
                    for s in range(2):
                        then(dve.tensor_reduce(top[s][:], src, X, ALU.max))
                        then(dve.tensor_tensor(work[0][:], src, over_e(top[s][:]), ALU.is_equal))
                        then(dve.tensor_tensor(work[0][:], work[0][:], iota_b, ALU.mult))
                        then(dve.tensor_reduce(pick[:], work[0][:], X, ALU.min))
                        then(dve.tensor_tensor(hot[s][:], work[0][:], over_e(pick[:]), ALU.is_equal))
                        if s == 0:
                            then(dve.scalar_tensor_tensor(work[1][:], hot[0][:], BIG, logit, ALU.mult, ALU.add))
                            src = work[1][:]
                    then(dve.tensor_tensor(hotb[:], hot[0][:], hot[1][:], ALU.add))
                    n_hot = step[0]
                    then(dve.tensor_tensor(work[2][:], logit, over_e(top[0][:]), ALU.subtract))
                    then(dve.tensor_tensor(pick[:], top[1][:], top[0][:], ALU.subtract))
                    n_sub = step[0]
                    dve.wait_ge(s_ract, 2)
                    then(dve.tensor_reduce(den[:], work[2][:], X, ALU.add))
                    then(dve.reciprocal(w_top[:, 0, :], den[:]))
                    then(dve.tensor_tensor(w_top[:, 1, :], pick[:], w_top[:, 0, :], ALU.mult))
                    dve.wait_ge(s_rpe, 1)
                    tot = work[0]
                    for hh in range(2):
                        then(dve.tensor_copy(tot[:, hh * T // 2:(hh + 1) * T // 2, :].rearrange("p t e -> p (t e)"),
                                             turn[2 + hh][:].rearrange("p a b -> p (a b)")))
                    pre = work[1]
                    for e in range(E):
                        last = dve.tensor_tensor_scan(pre[:, :, e], onesT[:], tot[:, :, e], 0.0, ALU.mult, ALU.add)
                    then(last)
                    then(dve.tensor_scalar(cnt[:], pre[:, T - 1, :], float(P - 1), None, ALU.add))
                    then(dve.tensor_copy(cnt_i[:], cnt[:]))
                    then(dve.tensor_scalar(cnt_i[:], cnt_i[:], 7, None, ALU.arith_shift_right))
                    then(dve.tensor_copy(nt_f[:], cnt_i[:]))
                    then(dve.tensor_tensor_scan(inc[:], ones_e[:], nt_f[:], 0.0, ALU.mult, ALU.add))
                    then(dve.tensor_tensor(base[:], inc[:], nt_f[:], ALU.subtract))
                    then(dve.tensor_scalar(base[:], base[:], float(P), None, ALU.mult))
                    then(dve.tensor_tensor(pre[:], pre[:], tot[:], ALU.subtract))
                    then(dve.tensor_tensor(pre[:], pre[:], base[:].unsqueeze(1).broadcast_to([P, T, E]), ALU.add))
                    then(dve.tensor_tensor(pre[:], rank[:].rearrange("p a t e -> p (a t) e"), pre[:], ALU.add))
                    for s in range(2):
                        then(dve.tensor_tensor(work[2][:], pre[:], hot[s][:], ALU.mult))
                        then(dve.tensor_reduce(posf[:, s, :], work[2][:], X, ALU.add))
                    then(dve.tensor_copy(y_row[:], posf[:]))
                    then(dve.tensor_scalar(lo_i[:], y_row[:], P - 1, None, ALU.bitwise_and))
                    then(dve.tensor_scalar(hi_i[:], y_row[:], 7, None, ALU.arith_shift_right))
                    then(dve.tensor_scalar(at_f[:], lo_i[:], float(MT), None, ALU.mult))
                    then(dve.tensor_tensor(list_at[:], at_f[:], hi_i[:], ALU.add))
                    then(dve.tensor_tensor(ge[:], iota_m[:].unsqueeze(2).broadcast_to([1, MT, E]),
                                           inc[0:1, :].unsqueeze(1).broadcast_to([1, MT, E]), ALU.is_ge))
                    then(dve.tensor_reduce(te_f[:], ge[:, :, 0:E - 1], X, ALU.add))
                    then(dve.tensor_copy(tile_expert[:], te_f[:]))

                N_HOT, N_SUB = 12, 14

                @block.tensor
                def _(pe):
                    pe.wait_ge(s_const, 16 * 14)
                    with pe.Fori(0, B // XS) as i:
                        for par in range(XS):
                            n = XS * i + par
                            pe.wait_ge(s_ln, n + 1)
                            for q in range(4):
                                pe.wait_ge(s_xt, CREDIT + 4 * n)
                                for t in range(2):
                                    for c in range(C):
                                        last = pe.transpose(turn[q][:, 2 * t + c, :], xin[par][:, 2 * q + t, c * P:(c + 1) * P], ident[:])
                                last.then_inc(s_turn, 1)
                            pe.wait_ge(s_xt, CREDIT + 4 * n + 4)
                            pe.wait_ge(s_lgc, CREDIT + 2 * n + 1)
                            for c in range(C):
                                for q in range(4):
                                    last = pe.matmul(lg[32 * q:32 * q + E, :], gate[:, c, :], xt[par % 2][:, c, 2 * q * P:(2 * q + 2) * P],
                                                     start=(c == 0), stop=(c == C - 1), tile_position=(0, 32 * q))
                            last.then_inc(s_lgm, 1)
                            pe.wait_ge(s_lgt, n + 1)
                            for w in range(2):
                                last = pe.transpose(lg[:, w * P:(w + 1) * P], lgt[:, w * P:(w + 1) * P], ident[:])
                            last.then_inc(s_lg, 1)
                    pe.wait_ge(s_r, N_HOT)
                    for hh in range(2):
                        rhs = hotb[:, hh * T // 2:(hh + 1) * T // 2, :]
                        pe.matmul(rank[:, hh], upper_b[:], rhs, start=True, stop=True)
                        last = pe.matmul(turn[2 + hh][:].rearrange("p a b -> p (a b)"), ones_b[:], rhs, start=True, stop=True)
                    last.then_inc(s_rpe, 1)

                @block.scalar
                def _(act):
                    act.sem_inc(s_xt, CREDIT)
                    for i in range(2):
                        act.sem_inc(s_xt_st[i], 16)
                    with act.Fori(0, B // XS) as i:
                        for par in range(XS):
                            n = XS * i + par
                            act.wait_ge(s_var, 3 * n + 3)
                            act.activation(std[:], vareps[:], ACT.Sqrt).then_inc(s_std, 1)
                            act.wait_ge(s_xt_st[par % 2], 16 * (2 * i + par // 2 + 1))
                            act.wait_ge(s_lg, CREDIT + n - 1)
                            for q in range(4):
                                act.wait_ge(s_turn, 4 * n + q + 1)
                                act.activation(xt[par % 2][:].rearrange("p c (t s) -> p t c s", s=P)[:, 2 * q:2 * q + 2],
                                               turn[q][:].rearrange("p (t c) s -> p t c s", c=C), ACT.Copy).then_inc(s_xt, 1)
                            act.wait_ge(s_lgm, n + 1)
                            act.activation(lgt[:], lg[:], ACT.Copy).then_inc(s_lgt, 1)
                    act.wait_ge(s_r, N_SUB)
                    act.activation(work[2][:], work[2][:], ACT.Exp).then_inc(s_ract, 1)
                    act.activation(pick[:], pick[:], ACT.Exp).then_inc(s_ract, 1)

        xT = sb("xT", [P, C, S])
        rot_a = sb("rot_a", [P, S])
        rot_b = sb("rot_b", [P, S])
        qk = sb("qk", [P, S])
        parts = sb("parts", [P, 3, S], BF16)
        squares = sb("squares", [P, S], BF16)
        q_op = [sb(f"q_op{i}", [P, HG, S], BF16) for i in range(2)]
        k_op = [sb(f"k_op{i}", [P, HG, S], BF16) for i in range(2)]
        v_op = sb("v_op", [P, TB, H, DK + 1])
        v_last = sb("v_last", [P, TB, HG, DK])
        prob = [sb(f"prob{i}", [P, HG, HALF]) for i in range(3)]
        o_t = [sb(f"o_t{i}", [P, HALF]) for i in range(2)]
        inv = sb("inv", [P, 4, HG])
        attn = sb("attn", [P, TB, D])
        attn_t = sb("attn_t", [P, C, S])
        resid = [sb(f"resid{i}", [P, 2, D]) for i in range(2)]
        maxrow = sb("maxrow", [2 * DK, 3, P], BF16)
        nmax = sb("nmax", [P, 1])
        nbound = sb("nbound", [1, 1])
        flag = sb("flag", [1, 1], I32)
        rowmax = sb("rowmax", [P, TB, HG, 2])
        rm = sb("rm", [P, HG * TB])
        rmb = sb("rmb", [P, 3, HG * TB], BF16)
        ew = sb("ew", [P, E, C, D])
        lists = sb("lists", [P, MT + 4], I32)
        pick_m = [sb(f"pick_m{i}", [P, 2], I32) for i in range(3)]
        x_m = [sb(f"x_m{i}", [P, 2, D]) for i in range(3)]
        xt_m = [sb(f"xt_m{i}", [P, 2, C, P]) for i in range(2)]
        y_m = [sb(f"y_m{i}", [P, 2, D]) for i in range(2)]
        pick_c = pick_m
        y_c = [x_m[0], x_m[1]]
        h_c = [y_m[0][:, 0, :], y_m[1][:, 0, :]]

        last_x = ew[:].rearrange("p e c d -> p (e c) d")[:, 0:TB]
        last_y = ew[:].rearrange("p e c d -> p (e c) d")[:, TB:3 * TB].rearrange("p (t s) d -> p t s d", s=2)

        def ps(name, shape, dt=F32):
            return ctx.enter_context(nc.psum_tensor(name, shape, dt))

        st_ps = [ps(f"st_ps{i}", [P, 2, HALF]) for i in range(2)]
        acc = ps("acc", [P, HALF])
        m0 = ps("m0", [P, HALF])
        m1 = ps("m1", [P, HALF])
        m2 = ps("m2", [P, HALF])

        names = ("xT_in xT_used qk_full qk_used rot_mul rot split sq v_full v_used v_moved n_full n_used nt_full "
                 "nt_used st exp pmask pv o_copied o_full o_inv o_used e_full e_used w_full w_used "
                 "flagged maxready slow_pe slow_dve ones k_ones scattered listed ew_in "
                 "mt_full mt_used mm_full mm_used y_bias y_relu picked pick_c_made h_c1 combined zeroed last_x last_out last_sum part_out max_out").split()
        s_ = {n: sem("s_" + n) for n in names}
        s_load = [sem(f"s_load{i}") for i in range(2)]
        s_res_in = [sem(f"s_res_in{i}") for i in range(2)]
        s_res_out = [sem(f"s_res_out{i}") for i in range(2)]
        s_xm = [sem(f"s_xm{i}") for i in range(3)]
        s_yst = [sem(f"s_yst{i}") for i in range(2)]
        s_yc = [sem(f"s_yc{i}") for i in range(2)]
        s_last_y = [sem(f"s_last_y{i}") for i in range(len(LAST))]
        s_hc = [sem(f"s_hc{i}") for i in range(2)]
        s_oc = [sem(f"s_oc{i}") for i in range(2)]

        def kind(b):
            return "plain" if b < B_MOE else "moe" if b < B_COMB else "comb"

        def walk(eng, unit, before_comb=None):
            for b in range(B_MOE):
                for g in range(G):
                    unit(b, g, "plain")
            with eng.Fori(B_MOE, B_COMB) as b:
                for g in range(G):
                    unit(b, g, "moe")
            if before_comb:
                before_comb()
            with eng.Fori(B_COMB, B_LAST) as b:
                for g in range(G):
                    unit(b, g, "comb")
            for g in range(G):
                unit(B_LAST, g, "comb")

        def qk_step(kd, hf):
            return 0 if hf == 0 else 2 if kd == "moe" else 1

        def qk_bank(kd, hf):
            return m1 if hf == 1 and kd != "moe" else m0

        def step_of(kd, what):
            late = 1 if kd == "moe" else 0
            return {"square": 3, "norms": 4, "turn": 5, "bound": 5, "find_max": 6, "store_max": 6, "load_max": 8,
                    "store0": 1, "store1": 2, "load": 3}[what] + late

        def has_prev(b, g):
            return not (isinstance(b, int) and b == 0 and g == 0)

        def has_prev_batch(b):
            return not (isinstance(b, int) and b == 0)

        def has_next(b, g):
            return not (isinstance(b, int) and b == B_LAST and g == G - 1)

        def pair0(b, g):
            return G * PU * (b - B_MOE) + PU * g

        def round0(b, g, ring):
            return G * PU // ring * (b - B_MOE) + PU // ring * g

        def per_unit(b):
            return CU_LAST if isinstance(b, int) and b >= B_LAST else CU

        def tile_c0(b, g):
            return G * CU * (b - B_COMB) + per_unit(b) * g

        def crounds(b, g):
            return G * CU // 2 * (b - B_COMB) + per_unit(b) // 2 * g

        with nc.Block() as block:

            @block.tensor
            def _(pe):
                def take(sems):
                    for name, value in sems:
                        wait(pe, s_[name], value)

                def project_qk(n, gn, hf, bn, bank):
                    if gn == 0 and hf == 0:
                        wait(pe, s_["xT_in"], 16 * (bn + 1))
                    for c in range(C):
                        last = pe.matmul(bank[:], wqk[:, gn, c, :], xT[:, c, hf * HALF:(hf + 1) * HALF], start=(c == 0), stop=(c == C - 1))
                    last.then_inc(s_["qk_full"], 1)

                def project_v(bn, i):
                    for t in range(2):
                        for c in range(C):
                            last = pe.matmul(m2[:, t * D:(t + 1) * D], xT[:, c, (2 * i + t) * P:(2 * i + t + 1) * P], wv[:, c, :],
                                             start=(c == 0), stop=(c == C - 1))
                    last.then_inc(s_["v_full"], 1)

                def norms(n):
                    wait(pe, s_["sq"], n + 1)
                    for t in range(TB):
                        last = pe.matmul(m0[:, t * 2 * HG:(t + 1) * 2 * HG], squares[:, t * P:(t + 1) * P], headsum[:], start=True, stop=True)
                    last.then_inc(s_["n_full"], 1)

                def norm_turn(n):
                    wait(pe, s_["n_used"], n + 1)
                    pe.transpose(m0[0:1, 0:P], nmax[:], ident[:]).then_inc(s_["nt_full"], 1)

                def find_max(n, sl, rnd):
                    wait_apart(pe, s_["flagged"], n + 1, s_tick)
                    v = pe.value_load(flag[0:1, 0:1], min_val=0, max_val=1)
                    with pe.If(v > 0):
                        wait_apart(pe, s_load[sl], 16 * (NLOAD * rnd + 6), s_tick)
                        with pe.Fori(0, TB) as i:
                            for w in range(2 * HG):
                                h, half = w // 2, w % 2
                                pe.wait_ge(s_["slow_dve"], CREDIT + SLOW_DVE * n + 2 * (2 * HG * i + w))
                                pe.matmul(m0[:], q_op[sl][0:96, h, ds(i * P, P)], k_op[sl][0:96, h, half * HALF:(half + 1) * HALF],
                                          start=True, stop=True).then_inc(s_["slow_pe"], 1)
                        pe.wait_ge(s_["slow_dve"], CREDIT + SLOW_DVE * (n + 1))
                        for r in range(3):
                            last = pe.matmul(m0[0:HG * TB, r * P:(r + 1) * P], rmb[:, r, :], identb[:], start=True, stop=True)
                        last.then_inc(s_["slow_pe"], 1)
                        pe.wait_ge(s_["maxready"], n + 1)
                    with pe.Else():
                        pe.sem_inc(s_["slow_pe"], SLOW_PE)

                def scores(u, g, k, pr):
                    hf, j = STEPS[k]
                    sl = g % 2
                    wait(pe, s_["exp"], EX * u + 2 * k + pr - 1)
                    for hh in range(2):
                        h = 2 * pr + hh
                        last = pe.matmul(st_ps[pr][:, hh, 0:width(k)], k_op[sl][0:99, h, j * P:(j + 1) * P],
                                         q_op[sl][0:99, h, first_q(k):first_q(k) + width(k)], start=True, stop=not is_diag(k))
                        if is_diag(k):
                            last = pe.matmul(st_ps[pr][:, hh, 0:P], identb[:], future[:], start=False, stop=True)
                    last.then_inc(s_["st"], 1)

                def values(u, g, k, b=None):
                    hf, j = STEPS[k]
                    sl = g % 2
                    first, final = j == 0, k in (7, 11)
                    if first:
                        wait(pe, s_["o_copied"], 2 * u + (1 - hf))
                        if k == 0:
                            if g == 0:
                                wait(pe, s_["v_used"], 4 * (b + 1))
                            if g == G - 1:
                                wait(pe, s_["v_moved"], b + 1)
                    wait(pe, s_["exp"], EX * u + 2 * k + 2)
                    at = first_q(k) - HALF * hf
                    for h in range(HG):
                        last = pe.matmul(acc[32 * h:32 * h + DK + 1, at:at + width(k)], v_op[:, j, HG * g + h, :], prob[k % 3][:, h, 0:width(k)],
                                         start=first, stop=final, tile_position=(0, 32 * h))
                    last.then_inc(s_["pv"], 1)

                def out_turn(u, half):
                    bank = m1 if half == 0 else m0
                    wait(pe, s_["o_copied"], 2 * u + half + 1)
                    for t in range(4):
                        last = pe.transpose(bank[:, t * P:(t + 1) * P], o_t[half][:, t * P:(t + 1) * P], ident[:])
                    last.then_inc(s_["o_full"], 1)

                def attn_turn(bp, i, bank):
                    t0 = (4, 6, 0, 2)[i]
                    for t in range(2):
                        for c in range(C):
                            last = pe.transpose(bank[:, (2 * t + c) * P:(2 * t + c + 1) * P], attn[:, t0 + t, c * P:(c + 1) * P], ident[:])
                    last.then_inc(s_["e_full"], 1)

                def out_project(bp, i, bank):
                    t0 = (4, 6, 0, 2)[i]
                    for t in range(2):
                        for c in range(C):
                            last = pe.matmul(bank[:, t * D:(t + 1) * D], attn_t[:, c, (t0 + t) * P:(t0 + t + 1) * P], wo[:, c, :],
                                             start=(c == 0), stop=(c == C - 1))
                    last.then_inc(s_["w_full"], 1)

                def expert_turn(b, g, p):
                    wait(pe, s_xm[p % 3], 32 * (round0(b, g, 3) + p // 3 + 1))
                    for t in range(2):
                        for c in range(C):
                            last = pe.transpose(m1[:, (2 * t + c) * P:(2 * t + c + 1) * P], x_m[p % 3][:, t, c * P:(c + 1) * P], ident[:])
                    last.then_inc(s_["mt_full"], 1)

                def expert_product(m, p):
                    wait(pe, s_["mt_used"], CREDIT + m + 1)
                    for t in range(2):
                        e = pe.value_load(tile_expert[0:1, ds(2 * m + t, 1)], min_val=0, max_val=E - 1)
                        pe.matmul(m2[:, t * D:(t + 1) * D], ones3[:], ebias[:, ds(e, 1), :].rearrange("p o d -> p (o d)"), start=True, stop=False)
                        for c in range(C):
                            last = pe.matmul(m2[:, t * D:(t + 1) * D], xt_m[p % 2][:, t, c, :],
                                             ew[:, ds(e, 1), c, :].rearrange("p o d -> p (o d)"), start=False, stop=(c == C - 1))
                    last.then_inc(s_["mm_full"], 1)

                def unit(b, g, kd):
                    u = G * b + g
                    n, gn = u + 1, (g + 1) % G
                    bn = b + (1 if g == G - 1 else 0)
                    prev, nxt = has_prev(b, g), has_next(b, g)
                    tail = g == 0 and has_prev_batch(b)
                    moe = kd == "moe"
                    m = pair0(b, g) if moe else None
                    done = {"qk": 2 * n, "v": 4 * (b + 1), "n": n, "nt": n, "o": 2 * u - 1, "e": G * (b - 1) if g == 0 else 0,
                            "w": G * (b - 1) if g == 0 else 0, "mt": m if moe else PAIRS if kd == "comb" and g == 0 else 0,
                            "mm": m if moe else PAIRS if kd == "comb" and g == 0 else 0}
                    if g == 1:
                        done["w"] = G * b if has_prev_batch(b) else 0

                    def free(*kinds):
                        take([(kk + "_used", done[kk] + (CREDIT if kk in ("mt", "mm") else 0)) for kk in kinds if not (isinstance(done[kk], int) and done[kk] <= 0)])

                    if moe and g == 0:
                        wait(pe, s_["ew_in"], 16)
                    gap = NS // per_unit(b)
                    for k in range(NS):
                        if k == 0:
                            wait(pe, s_load[g % 2], 16 * NLOAD * ((u // 2 + 1) if isinstance(u, int) else (2 * b + g // 2 + 1)))
                        scores(u, g, k, 0)
                        scores(u, g, k, 1)
                        if k == step_of(kd, "find_max") and nxt:
                            find_max(n, (g + 1) % 2, (n // 2) if isinstance(n, int) else 2 * b + (g + 1) // 2)
                        if moe and k % 2 == 0:
                            free("mt", "qk", "o", "e", "w")
                            expert_turn(b, g, k // 2)
                            done["mt"] += 1
                        for hf in range(2):
                            if k == qk_step(kd, hf) and nxt:
                                free("n", "nt", "o", "w", *(["mt"] if qk_bank(kd, hf) is m1 else ["qk"] if hf else []))
                                project_qk(n, gn, hf, bn, qk_bank(kd, hf))
                                done["qk"] += 1
                        if k in (2, 4, 6, 8) and g == G - 1 and nxt:
                            free("mm", "v", "e")
                            project_v(bn, k // 2 - 1)
                            done["v"] += 1
                        if k == 3 and prev:
                            free("qk", "w")
                            out_turn(u - 1, 1)
                            done["o"] += 1
                        if moe and k % 2 == 1:
                            free("mm", "v", "n", "e")
                            expert_product(m + k // 2, k // 2)
                            done["mm"] += 1
                        if tail and k in (4, 5):
                            wait(pe, s_["o_used"], 2 * u)
                            free("qk", "mt", "o", "e")
                            attn_turn(b - 1, 2 * (k - 4), m1)
                            done["e"] += 1
                            free("v", "mm")
                            attn_turn(b - 1, 2 * (k - 4) + 1, m2)
                            done["e"] += 1
                        if k == step_of(kd, "norms") and nxt:
                            free("qk", "o", "nt", "w")
                            norms(n)
                            done["n"] += 1
                        if k == step_of(kd, "turn") and nxt:
                            norm_turn(n)
                            done["nt"] += 1
                        if tail and k in (7, 9):
                            free("qk", "o", "n", "nt", "w")
                            wait(pe, s_["e_used"], 4 * (b - 1) + k - 6)
                            out_project(b - 1, k - 7, m0)
                            done["w"] += 1
                            free("mt", "e", "w")
                            out_project(b - 1, k - 6, m1)
                            done["w"] += 1
                        if k >= 2:
                            values(u, g, k - 2, b)
                        elif prev:
                            values(u - 1, (g - 1) % G, NS - 2 + k)
                        if k == 10:
                            free("qk", "mt", "w")
                            out_turn(u, 0)
                            done["o"] += 1

                pe.sem_inc(s_["mm_full"], CREDIT)
                pe.sem_inc(s_["mt_full"], CREDIT)
                project_qk(0, 0, 0, 0, m0)
                project_qk(0, 0, 1, 0, m1)
                for i in range(4):
                    wait(pe, s_["v_used"], i)
                    project_v(0, i)
                wait(pe, s_["qk_used"], 2)
                norms(0)
                norm_turn(0)
                find_max(0, 0, 0)
                pe.wait_ge(s_["k_ones"], 2)
                walk(pe, unit)
                U = G * B
                values(U - 1, G - 1, NS - 2)
                values(U - 1, G - 1, NS - 1)
                out_turn(U - 1, 1)
                wait(pe, s_["o_used"], 2 * U)
                for i in range(4):
                    wait(pe, s_["e_used"], 4 * (B - 1) + i - 1)
                    attn_turn(B - 1, i, (m1, m2)[i % 2])
                for i in range(4):
                    wait(pe, s_["w_used"], 4 * (B - 1) + i - 1)
                    wait(pe, s_["e_used"], 4 * (B - 1) + i + 1)
                    out_project(B - 1, i, (m0, acc)[i % 2])

            @block.scalar
            def _(act):
                def exps(u, k, pr):
                    wait(act, s_["pv"], NS * u + k - 2)
                    wait(act, s_["st"], EX * u + 2 * k + pr + 1)
                    act.activation(prob[k % 3][:, 2 * pr:2 * pr + 2, 0:width(k)], st_ps[pr][:, :, 0:width(k)], ACT.Exp,
                                   scale=SCALE).then_inc(s_["exp"], 1)

                def copy_v(bn, i):
                    wait(act, s_["v_full"], 4 * bn + i + 1)
                    wait(act, s_["pv"], NS * (G * bn - 1))
                    src = m2[:].rearrange("p (t h d) -> p t h d", t=2, h=H)
                    act.activation(v_op[:, 2 * i:2 * i + 2, 0:H - HG, 0:DK], src[:, :, 0:H - HG], ACT.Copy)
                    wait(act, s_["v_moved"], bn)
                    act.activation(v_last[:, 2 * i:2 * i + 2], src[:, :, H - HG:H], ACT.Copy).then_inc(s_["v_used"], 1)

                def store_max(n, sl):
                    if isinstance(n, int):
                        act.wait_ge(s_["maxready"], n + 1)
                    else:
                        wait_apart(act, s_["maxready"], n + 1, s_tick)
                    act.dma_start(max_d[sl].rearrange("r h t s -> (h t) r s"), maxrow[:]).then_inc(s_["max_out"], 16)

                def load_max(n, sl):
                    if isinstance(n, int):
                        act.wait_ge(s_["max_out"], 16 * (n + 1))
                    else:
                        wait_apart(act, s_["max_out"], 16 * (n + 1), s_tick)
                    act.dma_start(q_op[sl][96:99], max_d[sl].rearrange("r h t s -> r h (t s)")).then_inc(s_load[sl], 16)

                def store_y(m, p):
                    wait_apart(act, s_["mm_used"], CREDIT + m + 1, s_tick)
                    act.dma_start(y_d[ds(2 * m * P, 2 * P)].rearrange("(t p) d -> p t d", p=P), y_m[p % 2][:]).then_inc(s_yst[p % 2], 16)

                def load_h(b, g, i):
                    c = tile_c0(b, g) + i
                    wait_apart(act, s_oc[i % 2], 16 * (crounds(b, g) + i // 2 + 1), s_tick)
                    act.dma_start(h_c[i % 2], h_d[ds(c * P, P)]).then_inc(s_hc[i % 2], 16)

                def store_out(b, g, i):
                    c = tile_c0(b, g) + i
                    wait_apart(act, s_["combined"], CREDIT + c + 1, s_tick)
                    act.dma_start(out_rows[ds(c * P, P)], h_c[i % 2]).then_inc(s_oc[i % 2], 16)

                def square(n):
                    wait(act, s_["rot"], 2 * n + 2)
                    wait(act, s_["n_full"], n)
                    act.activation(squares[:], qk[:], ACT.Square).then_inc(s_["sq"], 1)

                def copy_o(u, half):
                    wait(act, s_["pv"], NS * u + (8, 12)[half])
                    wait(act, s_["o_used"], 2 * (u - 1) + half + 1)
                    act.activation(o_t[half][:], acc[:], ACT.Copy).then_inc(s_["o_copied"], 1)

                def copy_attn(bp, i, bank):
                    t0 = (4, 6, 0, 2)[i]
                    wait(act, s_["e_full"], 4 * bp + i + 1)
                    wait(act, s_["w_full"], 4 * bp)
                    act.activation(attn_t[:].rearrange("p c (t s) -> p t c s", s=P)[:, t0:t0 + 2],
                                   bank[:].rearrange("p (t c s) -> p t c s", t=2, c=C), ACT.Copy).then_inc(s_["e_used"], 1)

                def copy_tokens(m, p):
                    wait(act, s_["mt_full"], CREDIT + m + 1)
                    wait(act, s_["mm_full"], CREDIT + m - 1)
                    act.activation(xt_m[p % 2][:].rearrange("p t c s -> p (t c s)"), m1[:], ACT.Copy).then_inc(s_["mt_used"], 1)

                def unit(b, g, kd):
                    u = G * b + g
                    n = u + 1
                    prev, nxt = has_prev(b, g), has_next(b, g)
                    tail = g == 0 and has_prev_batch(b)
                    moe = kd == "moe"
                    m = pair0(b, g) if moe else None
                    gap = NS // per_unit(b)
                    for k in range(NS):
                        if k == 2 and prev:
                            copy_o(u - 1, 1)
                        exps(u, k, 0)
                        exps(u, k, 1)
                        if moe and k % 2 == 0:
                            copy_tokens(m + k // 2, k // 2)
                        if k in (2, 4, 6, 8) and g == G - 1 and nxt:
                            copy_v(b + 1, k // 2 - 1)
                        if moe and k % 2 == 0 and k >= 2:
                            store_y(m + k // 2 - 1, k // 2 - 1)
                        if kd == "comb" and k % gap == 0 and k > 0:
                            store_out(b, g, k // gap - 1)
                        if kd == "comb" and k % gap == 1:
                            i = k // gap + 1
                            if isinstance(b, int) and g == 1 and i == 1:
                                for q in range(2):
                                    act.wait_ge(s_res_out[q], 16 * 2 * (B - 1))
                            if not (isinstance(b, int) and tile_c0(b, g) + i >= T - TB):
                                load_h(b, g, i)
                        if tail and k in (4, 5):
                            copy_attn(b - 1, 2 * (k - 4), m1)
                            copy_attn(b - 1, 2 * (k - 4) + 1, m2)
                        if k == step_of(kd, "square") and nxt:
                            square(n)
                        if k == step_of(kd, "store_max") and nxt:
                            store_max(n, (g + 1) % 2)
                        if k == step_of(kd, "load_max") and nxt:
                            load_max(n, (g + 1) % 2)
                        if k == 9:
                            copy_o(u, 0)

                act.sem_inc(s_["mt_used"], CREDIT)
                act.wait_ge(s_["ones"], 1)
                for i in range(4):
                    copy_v(0, i)
                square(0)
                store_max(0, 0)
                load_max(0, 0)

                def y_stored():
                    for i in range(2):
                        act.wait_ge(s_yst[i], 16 * (PAIRS // 2 + 1))

                walk(act, unit, y_stored)
                U = G * B
                copy_o(U - 1, 1)
                for i in range(4):
                    copy_attn(B - 1, i, (m1, m2)[i % 2])

            @block.vector
            def _(dve):
                def rotate(n, hf, bank):
                    cols = slice(hf * HALF, (hf + 1) * HALF)
                    wait(dve, s_["qk_full"], 2 * n + hf + 1)
                    dve.tensor_tensor(rot_a[:, cols], bank[:], cosT[:, cols], ALU.mult)
                    dve.stream_shuffle(rot_b[:, cols], bank[:], [i ^ HG for i in range(32)]).then_inc(s_["qk_used"], 1)
                    wait(dve, s_["qk_used"], 2 * n + hf + 1)
                    dve.tensor_tensor(rot_b[:, cols], rot_b[:, cols], sinT[:, cols], ALU.mult).then_inc(s_["rot_mul"], 1)
                    wait(dve, s_["sq"], n)
                    wait(dve, s_["rot_mul"], 2 * n + hf + 1)
                    dve.tensor_tensor(qk[:, cols], rot_a[:, cols], rot_b[:, cols], ALU.add).then_inc(s_["rot"], 1)

                def split(n, hf):
                    cols = slice(hf * HALF, (hf + 1) * HALF)
                    c0 = 8 * n + 4 * hf
                    wait(dve, s_["rot"], 2 * n + hf + 1)
                    wait(dve, s_["part_out"], 32 * n)
                    dve.tensor_copy(parts[:, 0, cols], qk[:, cols]).then_inc(s_["split"], 1)
                    wait(dve, s_["split"], c0 + 1)
                    dve.tensor_tensor(rot_a[:, cols], qk[:, cols], parts[:, 0, cols], ALU.subtract).then_inc(s_["split"], 1)
                    wait(dve, s_["split"], c0 + 2)
                    dve.tensor_copy(parts[:, 1, cols], rot_a[:, cols]).then_inc(s_["split"], 1)
                    wait(dve, s_["split"], c0 + 3)
                    dve.tensor_tensor(parts[:, 2, cols], rot_a[:, cols], parts[:, 1, cols], ALU.subtract).then_inc(s_["split"], 1)

                def norm_max(n):
                    wait(dve, s_["n_full"], n + 1)
                    dve.tensor_reduce(nmax[:], m0[:, 0:TB * 2 * HG], X, ALU.max).then_inc(s_["n_used"], 1)

                def bound(n, sl):
                    wait(dve, s_["nt_full"], n + 1)
                    dve.tensor_reduce(nbound[:], m0[0:1, 0:P], X, ALU.max).then_inc(s_["nt_used"], 1)
                    wait(dve, s_["nt_used"], n + 1)
                    wait(dve, s_["slow_pe"], SLOW_PE * n)
                    dve.tensor_scalar(flag[:], nbound[:], NORM2, None, ALU.is_gt).then_inc(s_["flagged"], 1)
                    wait_apart(dve, s_["flagged"], n + 1, s_tick)
                    if not (isinstance(n, int) and n == 0):
                        wait_apart(dve, s_["max_out"], 16 * n, s_tick)
                    v = dve.value_load(flag[0:1, 0:1], min_val=0, max_val=1)
                    with dve.If(v > 0):
                        find_max(n)
                    with dve.Else():
                        dve.sem_inc(s_["slow_dve"], SLOW_DVE)
                        dve.memset(maxrow[:], 0.0).then_inc(s_["maxready"], 1)

                def find_max(n):
                    c0 = CREDIT + SLOW_DVE * n
                    tmp = rot_a[:, 0:HALF]
                    with dve.Fori(0, TB) as i:
                        for w in range(2 * HG):
                            h, half = w // 2, w % 2
                            at = 2 * HG * i + w
                            wait_apart(dve, s_["slow_pe"], SLOW_PE * n + at + 1, s_tick)
                            dve.tensor_tensor(tmp, m0[:], masks[:, ds(MASK0 + half * HALF - i * P, HALF)], ALU.add).then_inc(s_["slow_dve"], 1)
                            dve.wait_ge(s_["slow_dve"], c0 + 2 * at + 1)
                            dve.tensor_reduce(rowmax[:, ds(i, 1), h, half:half + 1], tmp, X, ALU.max).then_inc(s_["slow_dve"], 1)
                    c0 = c0 + 2 * SLOW
                    dve.wait_ge(s_["slow_dve"], c0)
                    dve.tensor_reduce(rm[:].rearrange("p (h t) -> p h t", h=HG), rowmax[:].rearrange("p t h w -> p h t w"), X, ALU.max).then_inc(s_["slow_dve"], 1)
                    dve.wait_ge(s_["slow_dve"], c0 + 1)
                    dve.tensor_scalar(rm[:], rm[:], -1.0, None, ALU.mult).then_inc(s_["slow_dve"], 1)
                    for r in range(2):
                        dve.wait_ge(s_["slow_dve"], c0 + 2 + 2 * r)
                        dve.tensor_copy(rmb[:, r, :], rm[:]).then_inc(s_["slow_dve"], 1)
                        dve.wait_ge(s_["slow_dve"], c0 + 3 + 2 * r)
                        dve.tensor_tensor(rm[:] if r == 0 else rmb[:, 2, :], rm[:], rmb[:, r, :], ALU.subtract).then_inc(s_["slow_dve"], 1)
                    dve.wait_ge(s_["slow_pe"], SLOW_PE * (n + 1))
                    dve.tensor_copy(maxrow[:].rearrange("p r s -> p (r s)"), m0[0:HG * TB, 0:3 * P]).then_inc(s_["maxready"], 1)

                def normalise(u, g, half):
                    bank = (m1 if half == 0 else m0)[:].rearrange("p (t h d) -> p t h d", t=4, h=HG)
                    t0 = 4 * (1 - half)
                    wait(dve, s_["o_full"], 2 * u + half + 1)
                    dve.reciprocal(inv[:], bank[:, :, :, DK]).then_inc(s_["o_inv"], 1)
                    wait(dve, s_["o_inv"], 2 * u + half + 1)
                    dve.tensor_tensor(attn[:, t0:t0 + 4, g * GD:(g + 1) * GD].rearrange("p t (h d) -> p t h d", h=HG),
                                      bank[:, :, :, 0:DK], inv[:].unsqueeze(3).broadcast_to([P, 4, HG, DK]), ALU.mult).then_inc(s_["o_used"], 1)

                def add_resid(bp, i, bank):
                    wait(dve, s_["w_full"], 4 * bp + i + 1)
                    wait(dve, s_res_in[i % 2], 16 * (2 * bp + i // 2 + 1))
                    dve.tensor_tensor(resid[i % 2][:].rearrange("p t d -> p (t d)"), bank[:], resid[i % 2][:].rearrange("p t d -> p (t d)"),
                                      ALU.add).then_inc(s_["w_used"], 1)

                def move_v(b):
                    wait(dve, s_["v_used"], 4 * (b + 1))
                    wait(dve, s_["pv"], NS * G * b)
                    dve.tensor_copy(v_op[:, :, H - HG:H, 0:DK], v_last[:]).then_inc(s_["v_moved"], 1)

                def relu(b, g, p):
                    wait(dve, s_["mm_full"], CREDIT + pair0(b, g) + p + 1)
                    wait(dve, s_yst[p % 2], 16 * (round0(b, g, 2) + p // 2 + 1))
                    dve.tensor_scalar(y_m[p % 2][:].rearrange("p t d -> p (t d)"), m2[:], 0.0, None, ALU.max).then_inc(s_["mm_used"], 1)

                def combine(b, g, i):
                    c = tile_c0(b, g) + i
                    wait(dve, s_yc[i % 2], 32 * (crounds(b, g) + i // 2 + 1))
                    wait(dve, s_hc[i % 2], 16 * (crounds(b, g) + i // 2 + 1))
                    dve.scalar_tensor_tensor(h_c[i % 2], y_c[i % 2][:, 0, :], w_top[:, 0, ds(c, 1)], h_c[i % 2], ALU.mult, ALU.add).then_inc(s_["h_c1"], 1)
                    wait(dve, s_["h_c1"], c + 1)
                    dve.scalar_tensor_tensor(h_c[i % 2], y_c[i % 2][:, 1, :], w_top[:, 1, ds(c, 1)], h_c[i % 2], ALU.mult, ALU.add).then_inc(s_["combined"], 1)

                def combine_last(i):
                    dve.wait_ge(s_last_y[i], 32 * len(LAST[i]))
                    dve.wait_ge(s_["last_x"], 16)
                    for s in range(2):
                        dve.wait_ge(s_["last_sum"], 2 * i + s) if 2 * i + s else None
                        for t in LAST[i]:
                            last = dve.scalar_tensor_tensor(last_x[:, t], last_y[:, t, s], w_top[:, s, T - TB + t:T - TB + t + 1], last_x[:, t], ALU.mult, ALU.add)
                        last.then_inc(s_["last_sum"], 1)

                def unit(b, g, kd):
                    u = G * b + g
                    n = u + 1
                    prev, nxt = has_prev(b, g), has_next(b, g)
                    tail = g == 0 and has_prev_batch(b)
                    moe = kd == "moe"
                    m = pair0(b, g) if moe else None
                    gap = NS // per_unit(b)
                    for k in range(NS):
                        for hf in range(2):
                            if k == qk_step(kd, hf) and nxt:
                                rotate(n, hf, qk_bank(kd, hf))
                                split(n, hf)
                        if k == 3 and prev:
                            normalise(u - 1, (g - 1) % G, 1)
                        if moe and k % 2 == 1:
                            relu(b, g, k // 2)
                        if k == step_of(kd, "norms") and nxt:
                            norm_max(n)
                        if k == step_of(kd, "bound") and nxt:
                            bound(n, (g + 1) % 2)
                        if k == 7 and g == 0:
                            move_v(b)
                        if tail and k in (7, 9):
                            add_resid(b - 1, k - 7, m0)
                            add_resid(b - 1, k - 6, m1)
                        if kd == "comb" and k % gap == gap - 1:
                            combine(b, g, k // gap)
                        if kd == "comb" and isinstance(b, int) and g > 0 and k == 10:
                            combine_last(g - 1)
                        if k == 10:
                            if tail:
                                wait(dve, s_["e_full"], 4 * b)
                            normalise(u, g, 0)

                dve.sem_inc(s_["combined"], CREDIT)
                dve.sem_inc(s_["slow_dve"], CREDIT)
                dve.sem_inc(s_["mm_used"], CREDIT)
                dve.memset(acc[:], 0.0)
                dve.memset(v_op[:, :, :, DK:DK + 1], 1.0).then_inc(s_["ones"], 1)
                rotate(0, 0, m0)
                split(0, 0)
                rotate(0, 1, m1)
                split(0, 1)
                norm_max(0)
                bound(0, 0)
                walk(dve, unit)
                U = G * B
                normalise(U - 1, G - 1, 1)
                dve.wait_ge(s_["last_sum"], 2 * len(LAST))
                for i in range(4):
                    t0 = (4, 6, 0, 2)[i]
                    dve.wait_ge(s_["w_full"], 4 * (B - 1) + i + 1)
                    rows = last_x[:, t0:t0 + 2].rearrange("p t d -> p (t d)")
                    dve.tensor_tensor(rows, (m0, acc)[i % 2][:], rows, ALU.add).then_inc(s_["w_used"], 1)

            @block.gpsimd
            def _(pool):
                def scatter(t):
                    for s in range(2):
                        pool.indirect_dma_start(list_d, bass.IndirectOffsetOnAxis(ap=list_at[:, s, t:t + 1], axis=0),
                                                token[:, t:t + 1], None).then_inc(s_["scattered"], 16)

                def gather_tokens(m, sl):
                    wait(pool, s_["mt_full"], CREDIT + m - 2)
                    pool.wait_ge(s_["listed"], 16)
                    pool.tensor_copy(pick_m[sl][:], lists[:, ds(2 * m, 2)]).then_inc(s_["picked"], 1)
                    wait_apart(pool, s_["picked"], m + 1, s_tick)
                    for t in range(2):
                        pool.indirect_dma_start(x_m[sl][:, t, :], None, xn_d,
                                                bass.IndirectOffsetOnAxis(ap=pick_m[sl][:, t:t + 1], axis=0)).then_inc(s_xm[sl], 16)

                def gather_outputs(c, sl):
                    wait(pool, s_["combined"], CREDIT + c - 1)
                    pool.wait_ge(s_["listed"], 16)
                    for s in range(2):
                        last = pool.tensor_copy(pick_c[sl][:, s:s + 1], y_row[:, s, ds(c, 1)])
                    last.then_inc(s_["pick_c_made"], 1)
                    wait_apart(pool, s_["pick_c_made"], c + 1, s_tick)
                    for s in range(2):
                        pool.indirect_dma_start(y_c[sl][:, s, :], None, y_d,
                                                bass.IndirectOffsetOnAxis(ap=pick_c[sl][:, s:s + 1], axis=0)).then_inc(s_yc[sl], 16)

                def gather_last(i):
                    for t in LAST[i]:
                        for s in range(2):
                            pool.indirect_dma_start(last_y[:, t, s, :], None, y_d,
                                                    bass.IndirectOffsetOnAxis(ap=y_row[:, s, T - TB + t:T - TB + t + 1], axis=0)).then_inc(s_last_y[i], 16)

                def unit(b, g, kd):
                    u = G * b + g
                    n = u + 1
                    nxt = has_next(b, g)
                    gap = NS // per_unit(b)
                    for k in range(NS):
                        if kd == "plain" and k < 8:
                            scatter(8 * u + k)
                        if kd == "moe" and k % 2 == 1:
                            gather_tokens(pair0(b, g) + k // 2 + 2, (k // 2 + 2) % 3)
                        if kd == "comb" and k % gap == 0:
                            i = k // gap + 1
                            if not (isinstance(b, int) and tile_c0(b, g) + i >= T - TB):
                                gather_outputs(tile_c0(b, g) + i, i % 2)
                        if kd == "comb" and isinstance(b, int) and k == 3 and g < len(LAST):
                            gather_last(g)
                    if kd == "plain" and isinstance(b, int) and b == B_MOE - 1 and g == G - 1:
                        pool.wait_ge(s_["scattered"], 16 * 2 * T)
                        pool.wait_ge(s_["zeroed"], 1)
                        pool.dma_start(lists[:, 0:MT], list_d.rearrange("(p m) o -> p (m o)", p=P)).then_inc(s_["listed"], 16)
                        gather_tokens(0, 0)
                        gather_tokens(1, 1)

                pool.memset(lists[:], 0).then_inc(s_["zeroed"], 1)
                pool.wait_ge(s_["zeroed"], 1)
                for i in range(2):
                    pool.memset(k_op[i][96:99, :, :], 1.0).then_inc(s_["k_ones"], 1)
                    pool.wait_ge(s_["k_ones"], i + 1)
                for b in range(B_MOE):
                    for g in range(G):
                        unit(b, g, "plain")
                with pool.Fori(B_MOE, B_COMB) as b:
                    for g in range(G):
                        unit(b, g, "moe")
                for sl in range(3):
                    pool.wait_ge(s_xm[sl], 32 * ((PAIRS + 2 - sl + 2) // 3))
                pool.wait_ge(s_["mt_full"], CREDIT + PAIRS)
                for sl in range(2):
                    pool.wait_ge(s_yst[sl], 16 * (PAIRS // 2 + 1))
                gather_outputs(0, 0)
                with pool.Fori(B_COMB, B_LAST) as b:
                    for g in range(G):
                        unit(b, g, "comb")
                pool.wait_ge(s_["mm_full"], CREDIT + PAIRS)
                for g in range(G):
                    unit(B_LAST, g, "comb")

            @block.sync
            def _(sp):
                def wait_sp(sem, value):
                    if isinstance(value, int):
                        wait(sp, sem, value)
                    else:
                        wait_apart(sp, sem, value, s_tick)

                def load_xT(bn):
                    wait_sp(s_["qk_full"], 2 * G * bn)
                    sp.dma_start(xT[:], xnt_d[ds(bn, 1)].rearrange("o p c s -> p (o c) s")).then_inc(s_["xT_in"], 16)

                def store_parts(n, sl, hf):
                    cols = slice(hf * HALF, (hf + 1) * HALF)
                    wait_sp(s_["split"], 8 * n + 4 * hf + 4)
                    sp.dma_start(part_d[sl].rearrange("r w d (h s) -> (w d h) r s", h=HG)[:, :, cols], parts[:, :, cols]).then_inc(s_["part_out"], 16)

                def load_parts(n, sl):
                    wait_sp(s_["st"], EX * (n - 1))
                    wait_sp(s_["part_out"], 32 * (n + 1))
                    d = part_d[sl]
                    sp.dma_start(flat(q_op[sl][0:48]), again(d[0, 0], 3)).then_inc(s_load[sl], 16)
                    sp.dma_start(flat(q_op[sl][48:80]), again(d[1, 0], 2)).then_inc(s_load[sl], 16)
                    sp.dma_start(flat(q_op[sl][80:96]), d[2, 0]).then_inc(s_load[sl], 16)
                    sp.dma_start(flat(k_op[sl][0:48]), d[0:3, 1]).then_inc(s_load[sl], 16)
                    sp.dma_start(flat(k_op[sl][48:80]), d[0:2, 1]).then_inc(s_load[sl], 16)
                    sp.dma_start(flat(k_op[sl][80:96]), d[0, 1]).then_inc(s_load[sl], 16)

                def flat(v):
                    return v.rearrange("p h s -> p (h s)")

                def again(v, times):
                    return bass.AP(tensor=v.tensor, offset=v.offset, ap=[[0, times]] + [list(q) for q in v.ap])

                def load_resid(bp, i):
                    t0 = (4, 6, 0, 2)[i]
                    wait_sp(s_res_out[i % 2], 16 * (2 * bp + i // 2))
                    sp.dma_start(resid[i % 2][:], x_rows[ds(bp * S + t0 * P, 2 * P)].rearrange("(t p) d -> p t d", p=P)).then_inc(s_res_in[i % 2], 16)

                def store_h(bp, i):
                    t0 = (4, 6, 0, 2)[i]
                    wait_sp(s_["w_used"], 4 * bp + i + 1)
                    sp.dma_start(h_d[ds(bp * S + t0 * P, 2 * P)].rearrange("(t p) d -> p t d", p=P), resid[i % 2][:]).then_inc(s_res_out[i % 2], 16)

                def store_last_y(m):
                    wait_sp(s_["mm_used"], CREDIT + m + PU)
                    sp.dma_start(y_d[ds(2 * (m + PU - 1) * P, 2 * P)].rearrange("(t p) d -> p t d", p=P), y_m[1][:]).then_inc(s_yst[1], 16)

                def store_last_out(b, g):
                    c = tile_c0(b, g) + per_unit(b) - 1
                    wait_sp(s_["combined"], CREDIT + c + 1)
                    sp.dma_start(out_rows[ds(c * P, P)], h_c[1]).then_inc(s_oc[1], 16)

                def unit(b, g, kd):
                    u = G * b + g
                    n = u + 1
                    prev, nxt = has_prev(b, g), has_next(b, g)
                    tail = g == 0 and has_prev_batch(b)
                    moe = kd == "moe"
                    m = pair0(b, g) if moe else None
                    c0 = tile_c0(b, g) if kd == "comb" else None
                    gap = NS // per_unit(b)
                    for k in range(NS):
                        if k == 6 and g == G - 2 and nxt and not (isinstance(b, int) and b == B_LAST):
                            load_xT(b + 1)
                        if tail and k == 0:
                            load_resid(b - 1, 0)
                            load_resid(b - 1, 1)
                        for hf in range(2):
                            if k == step_of(kd, f"store{hf}") and nxt:
                                store_parts(n, (g + 1) % 2, hf)
                        if k == step_of(kd, "load") and nxt:
                            load_parts(n, (g + 1) % 2)
                        if tail and k == 9:
                            for i in range(2):
                                store_h(b - 1, i)
                            for i in range(2):
                                load_resid(b - 1, i + 2)
                        if tail and k == 11:
                            store_h(b - 1, 2)
                            store_h(b - 1, 3)
                        if kd == "comb" and isinstance(b, int) and k == 0 and g == 0:
                            sp.wait_ge(s_["mm_full"], CREDIT + PAIRS)
                            sp.dma_start(last_x, x_rows[(B - 1) * S:B * S].rearrange("(t p) d -> p t d", p=P)).then_inc(s_["last_x"], 16)
                    if moe:
                        store_last_y(m)
                    if kd == "comb":
                        store_last_out(b, g)

                load_xT(0)
                for i in range(2):
                    sp.sem_inc(s_yst[i], 16)
                    sp.sem_inc(s_oc[i], 16)
                sp.dma_start(ew[:], a["expert_wT"].rearrange("e (c p) d -> p e c d", p=P)).then_inc(s_["ew_in"], 16)
                store_parts(0, 0, 0)
                store_parts(0, 0, 1)
                load_parts(0, 0)

                def first_h():
                    for i in range(2):
                        sp.wait_ge(s_yst[i], 16 * (PAIRS // 2 + 1))
                    sp.dma_start(h_c[0], h_d[0:P]).then_inc(s_hc[0], 16)

                walk(sp, unit, first_h)
                for i in range(4):
                    t0 = (4, 6, 0, 2)[i]
                    sp.wait_ge(s_["w_used"], 4 * (B - 1) + i + 1)
                    sp.dma_start(out_rows[(B - 1) * S + t0 * P:(B - 1) * S + (t0 + 2) * P].rearrange("(t p) d -> p t d", p=P), last_x[:, t0:t0 + 2]).then_inc(s_["last_out"], 16)
                sp.wait_ge(s_["last_out"], 16 * 4)
                for i in range(2):
                    sp.wait_ge(s_oc[i], 16 * ((T - TB) // 2 + 1))


_NAMES = {"x": "L0_attn_x", "Wv": "L0_attn_Wv", "Wo": "L0_attn_Wo", "expert_b": "L0_ffn_expert_b"}


def _shape_constants():
    inv_freq = (np.float32(1.0) / np.power(np.float32(10000.0), np.arange(0, DK, 2, dtype=np.float32) / np.float32(DK))).astype(np.float32)
    ang = np.outer(np.arange(S, dtype=np.float32), inv_freq).astype(np.float32)
    cos, sin = np.cos(ang).astype(np.float32), np.sin(ang).astype(np.float32)
    dim = np.arange(P) // HG % DK
    pair = dim // 2
    sign = np.where(dim % 2 == 0, -1.0, 1.0).astype(np.float32)
    head = np.arange(P) % HG + HG * (np.arange(P) // GD)
    return {
        "cosT": np.ascontiguousarray(cos[:, pair].T),
        "sinT": np.ascontiguousarray(sin[:, pair].T * sign[:, None]),
        "ident": np.eye(P, dtype=np.float32),
        "upper": np.triu(np.ones((P, P), np.float32), 1),
        "lower": np.tril(np.ones((P, P), np.float32), -1),
        "headsum": (head[:, None] == np.arange(2 * HG)[None, :]).astype(np.float32),
        "iota_e": np.tile(np.arange(E, dtype=np.float32) - 99.0, (P, 1)),
        "masks": np.where(np.arange(MASKW)[None, :] - MASK0 <= np.arange(P)[:, None], np.float32(0), np.float32(BIG)),
        "iota_m": np.arange(MT, dtype=np.float32)[None, :],
    }


def kernel(**inputs):
    import concourse.bacc as _bacc
    from concourse.bass_utils import run_bass_kernel_spmd as _run

    nc = _bacc.Bacc("TRN2", target_bir_lowering=False, num_devices=1)
    arrays = {k: np.ascontiguousarray(inputs[v]) for k, v in _NAMES.items()}
    arrays["gate_wT"] = np.ascontiguousarray(np.asarray(inputs["L0_ffn_gate_w"]).T)
    arrays["expert_wT"] = np.ascontiguousarray(np.asarray(inputs["L0_ffn_expert_w"]).transpose(0, 2, 1))
    wq, wk = (np.asarray(inputs[k]).reshape(C, P, G, HG, DK).transpose(1, 2, 0, 4, 3).reshape(P, G, C, GD) for k in ("L0_attn_Wq", "L0_attn_Wk"))
    arrays["Wqk"] = np.ascontiguousarray(np.concatenate([wq, wk], axis=3))
    arrays.update(_shape_constants())
    feeds, a = {}, {}
    for name, v in arrays.items():
        feeds[f"in_{name}"] = v
        a[name] = nc.dram_tensor(f"in_{name}", v.shape, mybir.dt.from_np(v.dtype), kind="ExternalInput").ap()
    a["out"] = nc.dram_tensor("out_0", (B, S, D), F32, kind="ExternalOutput").ap()
    build(nc, a)
    r = _run(nc, [feeds], core_ids=[0])
    return r.results[0]["out_0"]
```

```python
from contextlib import ExitStack

import numpy as np

import concourse.bass as bass
from concourse import mybir

F32 = mybir.dt.float32
BF16 = mybir.dt.bfloat16
I32 = mybir.dt.int32
ALU = mybir.AluOpType
ACT = mybir.ActivationFunctionType
X = mybir.AxisListType.X
ds = bass.ds

P = 128
B, S, D = 8, 1024, 256
H, DK = 16, 16
G = 4
HG = H // G
GD = HG * DK
C = D // P
TB = S // P
T = B * TB
N = B * S
E = 16
MT = 2 * N // P + E
PAIRS = MT // 2
PU = 6
B_MOE, B_COMB = 2, 5
B_LAST = B - 1
CU = 4
CU_LAST = 6
assert (B_COMB - B_MOE) * G * PU == PAIRS
assert G * (CU * (B_LAST - B_COMB) + CU_LAST) == T - TB
HALF = S // 2
SCALE = DK ** -0.5
SAFE = 60.0
NORM2 = SAFE / SCALE
BIG = -1.0e38
EPS = 1e-5

STEPS = [(1, j) for j in range(8)] + [(0, j) for j in range(4)]
NS = len(STEPS)
EX = 2 * NS
CREDIT = 2
MASK0 = S - P
MASKW = MASK0 + S
SLOW = TB * HG * 2
SLOW_PE = SLOW + 1
SLOW_DVE = 2 * SLOW + 6
LAST = [(0, 1, 2), (3, 4, 5), (6, 7)]
R_PICKED, R_LIST, R_ALL = 14, 41, 44
SCATTER_U = 3
SCATTER_T = -(-T // (G * B_MOE - SCATTER_U))
XS = 4
NLOAD = 7


def first_q(k):
    hf, j = STEPS[k]
    return max(HALF * hf, P * j)


def width(k):
    return HALF * (STEPS[k][0] + 1) - first_q(k)


def is_diag(k):
    hf, j = STEPS[k]
    return j * P >= HALF * hf


def wait(eng, sem, value):
    if isinstance(value, int) and value <= 0:
        return
    eng.wait_ge(sem, value)


def wait_apart(eng, sem, value, tick):
    eng.wait_ge(sem, value)
    eng.sem_inc(tick, 1)


def build(nc, a):
    xnt_d = nc.dram_tensor("xnt_scratch", [B, P, C, S], F32, kind="Internal").ap()
    xn_d = nc.dram_tensor("xn_scratch", [N, D], F32, kind="Internal").ap()
    h_d = nc.dram_tensor("h_scratch", [N, D], F32, kind="Internal").ap()
    y_d = nc.dram_tensor("y_scratch", [MT * P, D], F32, kind="Internal").ap()
    list_d = nc.dram_tensor("list_scratch", [P * MT, 1], I32, kind="Internal").ap()
    part_d = [nc.dram_tensor(f"part_scratch{i}", [3, 2, DK, HG * S], BF16, kind="Internal").ap() for i in range(2)]
    bias_d = nc.dram_tensor("bias_scratch", [3, E, D], BF16, kind="Internal").ap()
    max_d = [nc.dram_tensor(f"max_scratch{i}", [3, HG, TB, P], BF16, kind="Internal").ap() for i in range(2)]

    x_rows = a["x"].rearrange("b s d -> (b s) d")
    out_rows = a["out"].rearrange("b s d -> (b s) d")

    with ExitStack() as ctx:
        def sb(name, shape, dt=F32, to=ctx):
            return to.enter_context(nc.sbuf_tensor(name, shape, dt))

        def sem(name):
            return ctx.enter_context(nc.semaphore(name))

        ident = sb("ident", [P, P])
        identb = sb("identb", [P, P], BF16)
        headsum = sb("headsum", [P, 2 * HG], BF16)
        wv = sb("wv", [P, C, D])
        wo = sb("wo", [P, C, D])
        wqk = sb("wqk", [P, G, C, P])
        cosT = sb("cosT", [P, S])
        sinT = sb("sinT", [P, S])
        w_top = sb("w_top", [P, 2, T])
        y_row = sb("y_row", [P, 2, T], I32)
        list_at = sb("list_at", [P, 2, T], I32)
        token = sb("token", [P, T], I32)
        tile_expert = sb("tile_expert", [1, MT], I32)
        zero_i = sb("zero_i", [P, MT], I32)
        ebias = sb("ebias", [3, E, D], BF16)
        ones3 = sb("ones3", [3, P], BF16)
        future = sb("future", [P, P], BF16)
        masks = sb("masks", [P, MASKW], BF16)

        ew = sb("ew", [P, E, C, D])
        room = [0]

        def carve(shape, dt=F32):
            words = int(np.prod(shape)) // (2 if dt is BF16 else 1)
            v = ew[:].rearrange("p e c d -> p (e c d)")[:, room[0]:room[0] + words]
            room[0] += words
            v = v if dt is F32 else v.bitcast(dt)
            return v.rearrange("p (a b) -> p a b", a=shape[0])

        logits = carve([TB + T, E])
        logit = logits[:, TB:TB + T, :]
        ge = ew[0:1].rearrange("p e c d -> p (e c d)")[:, room[0]:room[0] + MT * E].rearrange("p (m e) -> p m e", m=MT)
        work = [carve([T, E]) for _ in range(3)]
        hot = [carve([T, E]) for _ in range(2)]
        mask_f = ew[:].rearrange("p e c d -> p (e c d)")[:, (TB + T) * E:(TB + T) * E + MASKW]
        rank = carve([T, E])
        hotb = carve([T, E], BF16)
        posf = carve([2, T])
        at_f = carve([2, T])
        lo_i = carve([2, T], I32)
        iota_e = sb("iota_e", [P, E])
        iota_m = sb("iota_m", [1, MT])
        ones_b = sb("ones_b", [P, P], BF16)
        upper_b = sb("upper_b", [P, P], BF16)
        top = [sb(f"top{i}", [P, T]) for i in range(2)]
        pick = sb("pick", [P, T])
        den = sb("den", [P, T])
        onesT = sb("onesT", [P, T])
        cnt = sb("cnt", [P, E])
        cnt_i = sb("cnt_i", [P, E], I32)
        nt_f = sb("nt_f", [P, E])
        inc = sb("inc", [P, E])
        base = sb("base", [P, E])
        ones_e = sb("ones_e", [P, E])
        hi_i = sb("hi_i", [P, 2, T], I32)
        te_f = sb("te_f", [1, MT])

        s_r = sem("s_r")
        s_ract = sem("s_ract")
        s_rpe = sem("s_rpe")
        s_const = sem("s_const")
        s_first = sem("s_first")
        s_made = sem("s_made")
        s_tick = sem("s_tick")

        with ExitStack() as p1:
            def sb1(name, shape, dt=F32):
                return sb(name, shape, dt, p1)

            def ps1(name, shape, dt=F32):
                return p1.enter_context(nc.psum_tensor(name, shape, dt))

            gate = sb1("gate", [P, C, E])
            xin = [sb1(f"xin{i}", [P, TB, D]) for i in range(XS)]
            xt = [sb1(f"xt_out{i}", [P, C, S]) for i in range(2)]
            stat = sb1("stat", [P, TB, 6])
            mv = sb1("mv", [P, TB, 2])
            vareps = sb1("vareps", [P, TB])
            std = sb1("std", [P, TB])
            rstd = sb1("rstd", [P, TB])
            lower = sb1("lower", [P, P])
            bias_f = sb1("bias_f", [E, D])
            bias_p = sb1("bias_p", [E, 3, D], BF16)
            constf = sb1("constf", [P, P])

            turn = [ps1(f"turn{i}", [P, 4, P]) for i in range(4)]
            lg = ps1("lg", [P, 2 * P])
            lgt = sb1("lgt", [P, 2 * P])

            s_x = [sem(f"s_x{i}") for i in range(XS)]
            s_var = sem("s_var")
            s_std = sem("s_std")
            s_ln = sem("s_ln")
            s_turn = sem("s_turn")
            s_xt = sem("s_xt")
            s_lg = sem("s_lg")
            s_lgm = sem("s_lgm")
            s_lgt = sem("s_lgt")
            s_lgc = sem("s_lgc")
            s_xn_st = [sem(f"s_xn_st{i}") for i in range(XS)]
            s_xt_st = [sem(f"s_xt_st{i}") for i in range(2)]
            s_zero = sem("s_zero")
            s_list0 = sem("s_list0")
            s_bias_d = sem("s_bias_d")

            with nc.Block() as block:

                @block.sync
                def _(sp):
                    def load_x(n):
                        sp.dma_start(xin[n % XS][:], a["x"][n].rearrange("(t p) d -> p t d", p=P)).then_inc(s_x[n % XS], 16)

                    load_x(0)
                    sp.dma_start(ident[:], a["ident"]).then_inc(s_first, 16)
                    sp.dma_start(gate[:], a["gate_wT"].rearrange("(c p) e -> p c e", p=P)).then_inc(s_first, 16)
                    for n in range(1, XS):
                        load_x(n)
                    sp.dma_start(bias_f[:], a["expert_b"]).then_inc(s_const, 16)
                    sp.dma_start(lower[:], a["lower"]).then_inc(s_const, 16)
                    sp.dma_start(constf[:], a["upper"]).then_inc(s_const, 16)
                    sp.dma_start(iota_e[:], a["iota_e"]).then_inc(s_const, 16)
                    sp.dma_start(iota_m[:], a["iota_m"]).then_inc(s_const, 16)
                    sp.dma_start(hot[0][:, 0, 0:2 * HG], a["headsum"]).then_inc(s_const, 16)
                    sp.dma_start(wv[:], a["Wv"].rearrange("(c p) n -> p c n", p=P)).then_inc(s_const, 16)
                    sp.dma_start(wo[:], a["Wo"].rearrange("(c p) n -> p c n", p=P)).then_inc(s_const, 16)
                    sp.dma_start(wqk[:], a["Wqk"]).then_inc(s_const, 16)
                    sp.dma_start(cosT[:], a["cosT"]).then_inc(s_const, 16)
                    sp.dma_start(sinT[:], a["sinT"]).then_inc(s_const, 16)
                    sp.dma_start(mask_f, a["masks"]).then_inc(s_const, 16)
                    sp.wait_ge(s_zero, 1)
                    sp.dma_start(list_d.rearrange("(p m) o -> p (m o)", p=P), zero_i[:]).then_inc(s_list0, 16)
                    for n in range(B):
                        sp.wait_ge(s_ln, n + 1)
                        sp.dma_start(xn_d[n * S:(n + 1) * S].rearrange("(t p) d -> p t d", p=P), xin[n % XS][:]).then_inc(s_xn_st[n % XS], 16)
                        sp.wait_ge(s_xt, CREDIT + 4 * n + 4)
                        sp.dma_start(xnt_d[n], xt[n % 2][:]).then_inc(s_xt_st[n % 2], 16)
                        if 1 <= n and n - 1 + XS < B:
                            sp.wait_ge(s_xn_st[(n - 1) % XS], 16 * ((n - 1) // XS + 1))
                            load_x(n - 1 + XS)
                    sp.wait_ge(s_made, 6)
                    sp.dma_start(bias_d.rearrange("r e d -> e r d"), bias_p[:]).then_inc(s_bias_d, 16)
                    sp.wait_ge(s_bias_d, 16)
                    sp.dma_start(ebias[:], bias_d).then_inc(s_bias_d, 16)
                    sp.wait_ge(s_bias_d, 32)
                    for i in range(XS):
                        sp.wait_ge(s_xn_st[i], 16 * (B // XS))
                    for i in range(2):
                        sp.wait_ge(s_xt_st[i], 16 * (B // 2 + 1))
                    sp.wait_ge(s_const, 16 * 12)
                    sp.wait_ge(s_list0, 16)

                @block.gpsimd
                def _(pool):
                    pool.memset(zero_i[:], 0).then_inc(s_zero, 1)
                    pool.iota(token[:], pattern=[[P, T]], base=0, channel_multiplier=1)
                    pool.memset(ones_b[:], 1.0)
                    pool.memset(onesT[:], 1.0)
                    pool.memset(ones3[:], 1.0)
                    pool.memset(ones_e[:], 1.0).then_inc(s_made, 1)
                    pool.wait_ge(s_const, 16 * 12)
                    cast = [1]

                    def one(ins):
                        ins.then_inc(s_made, 1)
                        cast[0] += 1
                        pool.wait_ge(s_made, cast[0])

                    pool.wait_ge(s_made, 1)
                    for r in range(3):
                        one(pool.tensor_copy(bias_p[:, r, :], bias_f[:]))
                        if r < 2:
                            one(pool.tensor_tensor(bias_f[:], bias_f[:], bias_p[:, r, :], ALU.subtract))
                    one(pool.tensor_copy(identb[:], ident[:]))
                    one(pool.tensor_copy(upper_b[:], constf[:]))
                    one(pool.tensor_scalar(future[:], lower[:], BIG, None, ALU.mult))
                    one(pool.tensor_copy(masks[:], mask_f))
                    one(pool.tensor_copy(headsum[:], hot[0][:, 0, 0:2 * HG]))

                @block.vector
                def _(dve):
                    dve.memset(lg[:], 0.0).then_inc(s_lgc, CREDIT)
                    dve.sem_inc(s_lg, CREDIT)
                    dve.wait_ge(s_lgc, CREDIT)
                    dve.sem_inc(s_lgm, 1)
                    lg_tiles = lg[:].rearrange("p (w q e) -> p w q e", w=2, q=4)[:, :, :, 0:E]

                    def by_tile(v):
                        return v.rearrange("p (q w) e -> p w q e", w=2)

                    with dve.Fori(0, B // XS) as i:
                        for par in range(XS):
                            n = XS * i + par
                            xb = xin[par]
                            dve.wait_ge(s_x[par], 16 * (i + 1))
                            for t in range(TB):
                                last = dve.bn_stats(stat[:, t, :], xb[:, t, :])
                            last.then_inc(s_var, 1)
                            wait_apart(dve, s_var, 3 * n + 1, s_tick)
                            for t in range(TB):
                                last = dve.bn_aggr(mv[:, t, :], stat[:, t, :])
                            last.then_inc(s_var, 1)
                            dve.wait_ge(s_var, 3 * n + 2)
                            dve.tensor_scalar(vareps[:], mv[:, :, 1], EPS, None, ALU.add).then_inc(s_var, 1)
                            dve.wait_ge(s_std, n + 1)
                            dve.reciprocal(rstd[:], std[:]).then_inc(s_lgc, 1)
                            dve.wait_ge(s_lgc, CREDIT + 2 * n + 1)
                            for t in range(TB):
                                last = dve.tensor_scalar(xb[:, t, :], xb[:, t, :], mv[:, t, 0:1],
                                                         rstd[:, t:t + 1], ALU.subtract, ALU.mult)
                            last.then_inc(s_ln, 1)
                            dve.wait_ge(s_lg, CREDIT + n + 1)
                            dve.tensor_copy(by_tile(logits[:, ds(n * TB, TB), :]), lg_tiles).then_inc(s_lgc, 1)
                    dve.wait_ge(s_lg, CREDIT + B + 1)
                    dve.tensor_copy(by_tile(logit[:, T - TB:T, :]), lg_tiles).then_inc(s_lgc, 1)
                    dve.wait_ge(s_lgc, CREDIT + 2 * B + 1)

                @block.tensor
                def _(pe):
                    pe.wait_ge(s_first, 16 * 2)

                    def turn_logits(n):
                        pe.wait_ge(s_lgt, n + 1)
                        for w in range(2):
                            last = pe.transpose(lg[:, w * P:(w + 1) * P], lgt[:, w * P:(w + 1) * P], ident[:])
                        last.then_inc(s_lg, 1)

                    with pe.Fori(0, B // XS) as i:
                        for par in range(XS):
                            n = XS * i + par
                            turn_logits(n)
                            pe.wait_ge(s_ln, n + 1)
                            for q in range(4):
                                pe.wait_ge(s_xt, CREDIT + 4 * n)
                                for t in range(2):
                                    for c in range(C):
                                        last = pe.transpose(turn[q][:, 2 * t + c, :], xin[par][:, 2 * q + t, c * P:(c + 1) * P], ident[:])
                                last.then_inc(s_turn, 1)
                            pe.wait_ge(s_xt, CREDIT + 4 * n + 4)
                            pe.wait_ge(s_lgc, CREDIT + 2 * n + 2)
                            for c in range(C):
                                for q in range(4):
                                    last = pe.matmul(lg[32 * q:32 * q + E, :], gate[:, c, :], xt[par % 2][:, c, 2 * q * P:(2 * q + 2) * P],
                                                     start=(c == 0), stop=(c == C - 1), tile_position=(0, 32 * q))
                            last.then_inc(s_lgm, 1)
                    turn_logits(B)

                @block.scalar
                def _(act):
                    act.sem_inc(s_xt, CREDIT)
                    for i in range(2):
                        act.sem_inc(s_xt_st[i], 16)

                    def copy_logits(n):
                        act.wait_ge(s_lgm, n + 1)
                        act.activation(lgt[:], lg[:], ACT.Copy).then_inc(s_lgt, 1)

                    with act.Fori(0, B // XS) as i:
                        for par in range(XS):
                            n = XS * i + par
                            act.wait_ge(s_var, 3 * n + 3)
                            act.activation(std[:], vareps[:], ACT.Sqrt).then_inc(s_std, 1)
                            copy_logits(n)
                            act.wait_ge(s_xt_st[par % 2], 16 * (2 * i + par // 2 + 1))
                            act.wait_ge(s_lg, CREDIT + n)
                            for q in range(4):
                                act.wait_ge(s_turn, 4 * n + q + 1)
                                act.activation(xt[par % 2][:].rearrange("p c (t s) -> p t c s", s=P)[:, 2 * q:2 * q + 2],
                                               turn[q][:].rearrange("p (t c) s -> p t c s", c=C), ACT.Copy).then_inc(s_xt, 1)
                    copy_logits(B)

        xT = sb("xT", [P, C, S])
        rot_a = sb("rot_a", [P, S])
        rot_b = sb("rot_b", [P, S])
        qk = sb("qk", [P, S])
        parts = sb("parts", [P, 3, S], BF16)
        squares = sb("squares", [P, S], BF16)
        q_op = [sb(f"q_op{i}", [P, HG, S], BF16) for i in range(2)]
        k_op = [sb(f"k_op{i}", [P, HG, S], BF16) for i in range(2)]
        v_op = sb("v_op", [P, TB, H, DK + 1])
        v_last = sb("v_last", [P, TB, HG, DK])
        prob = [sb(f"prob{i}", [P, HG, HALF]) for i in range(3)]
        o_t = [sb(f"o_t{i}", [P, HALF]) for i in range(2)]
        inv = sb("inv", [P, 4, HG])
        attn = sb("attn", [P, TB, D])
        attn_t = sb("attn_t", [P, C, S])
        resid = [sb(f"resid{i}", [P, 2, D]) for i in range(2)]
        maxrow = sb("maxrow", [2 * DK, 3, P], BF16)
        nmax = sb("nmax", [P, 1])
        nbound = sb("nbound", [1, 1])
        flag = sb("flag", [1, 1], I32)
        rowmax = sb("rowmax", [P, TB, HG, 2])
        rm = sb("rm", [P, HG * TB])
        rmb = sb("rmb", [P, 3, HG * TB], BF16)
        lists = sb("lists", [P, MT + 4], I32)
        pick_m = [sb(f"pick_m{i}", [P, 2], I32) for i in range(3)]
        x_m = [sb(f"x_m{i}", [P, 2, D]) for i in range(3)]
        xt_m = [sb(f"xt_m{i}", [P, 2, C, P]) for i in range(2)]
        y_m = [sb(f"y_m{i}", [P, 2, D]) for i in range(2)]
        pick_c = pick_m
        y_c = [x_m[0], x_m[1]]
        h_c = [y_m[0][:, 0, :], y_m[1][:, 0, :]]

        last_x = ew[:].rearrange("p e c d -> p (e c) d")[:, 0:TB]
        last_y = ew[:].rearrange("p e c d -> p (e c) d")[:, TB:3 * TB].rearrange("p (t s) d -> p t s d", s=2)

        def ps(name, shape, dt=F32):
            return ctx.enter_context(nc.psum_tensor(name, shape, dt))

        st_ps = [ps(f"st_ps{i}", [P, 2, HALF]) for i in range(2)]
        acc = ps("acc", [P, HALF])
        m0 = ps("m0", [P, HALF])
        m1 = ps("m1", [P, HALF])
        m2 = ps("m2", [P, HALF])

        names = ("xT_in qk_full qk_used rot_mul rot split sq v_full v_used v_moved n_full n_used "
                 "nt_full nt_used st exp pv o_copied o_full o_inv o_used e_full e_used w_full w_used "
                 "flagged maxready slow_pe slow_dve ones k_ones scattered listed ew_in mt_full mt_used "
                 "mm_full mm_used picked pick_c_made h_c1 combined zeroed last_x last_out last_sum "
                 "part_out max_out ").split()
        s_ = {n: sem("s_" + n) for n in names}
        s_load = [sem(f"s_load{i}") for i in range(2)]
        s_res_in = [sem(f"s_res_in{i}") for i in range(2)]
        s_res_out = [sem(f"s_res_out{i}") for i in range(2)]
        s_xm = [sem(f"s_xm{i}") for i in range(3)]
        s_yst = [sem(f"s_yst{i}") for i in range(2)]
        s_yc = [sem(f"s_yc{i}") for i in range(2)]
        s_last_y = [sem(f"s_last_y{i}") for i in range(len(LAST))]
        s_hc = [sem(f"s_hc{i}") for i in range(2)]
        s_oc = [sem(f"s_oc{i}") for i in range(2)]

        def walk(eng, unit, before_comb=None):
            for b in range(B_MOE):
                for g in range(G):
                    unit(b, g, "plain")
            with eng.Fori(B_MOE, B_COMB) as b:
                for g in range(G):
                    unit(b, g, "moe")
            if before_comb:
                before_comb()
            with eng.Fori(B_COMB, B_LAST) as b:
                for g in range(G):
                    unit(b, g, "comb")
            for g in range(G):
                unit(B_LAST, g, "comb")

        def qk_step(kd, hf):
            return 0 if hf == 0 else 2 if kd == "moe" else 1

        def qk_bank(kd, hf):
            return m1 if hf == 1 and kd != "moe" else m0

        def step_of(kd, what):
            late = 1 if kd == "moe" else 0
            return {"square": 3, "norms": 4, "turn": 5, "bound": 5, "find_max": 6, "store_max": 6, "load_max": 8,
                    "store0": 1, "store1": 2, "load": 3}[what] + late

        def has_prev(b, g):
            return not (isinstance(b, int) and b == 0 and g == 0)

        def has_prev_batch(b):
            return not (isinstance(b, int) and b == 0)

        def has_next(b, g):
            return not (isinstance(b, int) and b == B_LAST and g == G - 1)

        def pair0(b, g):
            return G * PU * (b - B_MOE) + PU * g

        def round0(b, g, ring):
            return G * PU // ring * (b - B_MOE) + PU // ring * g

        def per_unit(b):
            return CU_LAST if isinstance(b, int) and b >= B_LAST else CU

        def tile_c0(b, g):
            return G * CU * (b - B_COMB) + per_unit(b) * g

        def crounds(b, g):
            return G * CU // 2 * (b - B_COMB) + per_unit(b) // 2 * g

        with nc.Block() as block:

            @block.tensor
            def _(pe):
                def take(sems):
                    for name, value in sems:
                        wait(pe, s_[name], value)

                def project_qk(n, gn, hf, bn, bank):
                    if gn == 0 and hf == 0:
                        wait(pe, s_["xT_in"], 16 * (bn + 1))
                    for c in range(C):
                        last = pe.matmul(bank[:], wqk[:, gn, c, :], xT[:, c, hf * HALF:(hf + 1) * HALF], start=(c == 0), stop=(c == C - 1))
                    last.then_inc(s_["qk_full"], 1)

                def project_v(bn, i):
                    for t in range(2):
                        for c in range(C):
                            last = pe.matmul(m2[:, t * D:(t + 1) * D], xT[:, c, (2 * i + t) * P:(2 * i + t + 1) * P], wv[:, c, :],
                                             start=(c == 0), stop=(c == C - 1))
                    last.then_inc(s_["v_full"], 1)

                def norms(n):
                    wait(pe, s_["sq"], n + 1)
                    for t in range(TB):
                        last = pe.matmul(m0[:, t * 2 * HG:(t + 1) * 2 * HG], squares[:, t * P:(t + 1) * P], headsum[:], start=True, stop=True)
                    last.then_inc(s_["n_full"], 1)

                def norm_turn(n):
                    wait(pe, s_["n_used"], n + 1)
                    pe.transpose(m0[0:1, 0:P], nmax[:], ident[:]).then_inc(s_["nt_full"], 1)

                def count_round(i):
                    pe.wait_ge(s_r, R_PICKED + i)
                    pe.matmul(m2[:], (ones_b, upper_b)[i // 2][:], hotb[:, i % 2 * T // 2:(i % 2 + 1) * T // 2, :],
                              start=True, stop=True).then_inc(s_rpe, 1)

                def find_max(n, sl, rnd):
                    wait_apart(pe, s_["flagged"], n + 1, s_tick)
                    v = pe.value_load(flag[0:1, 0:1], min_val=0, max_val=1)
                    with pe.If(v > 0):
                        wait_apart(pe, s_load[sl], 16 * (NLOAD * rnd + 6), s_tick)
                        with pe.Fori(0, TB) as i:
                            for w in range(2 * HG):
                                h, half = w // 2, w % 2
                                pe.wait_ge(s_["slow_dve"], CREDIT + SLOW_DVE * n + 2 * (2 * HG * i + w))
                                pe.matmul(m0[:], q_op[sl][0:96, h, ds(i * P, P)], k_op[sl][0:96, h, half * HALF:(half + 1) * HALF],
                                          start=True, stop=True).then_inc(s_["slow_pe"], 1)
                        pe.wait_ge(s_["slow_dve"], CREDIT + SLOW_DVE * (n + 1))
                        for r in range(3):
                            last = pe.matmul(m0[0:HG * TB, r * P:(r + 1) * P], rmb[:, r, :], identb[:], start=True, stop=True)
                        last.then_inc(s_["slow_pe"], 1)
                        pe.wait_ge(s_["maxready"], n + 1)
                    with pe.Else():
                        pe.sem_inc(s_["slow_pe"], SLOW_PE)

                def scores(u, g, k, pr):
                    hf, j = STEPS[k]
                    sl = g % 2
                    wait(pe, s_["exp"], EX * u + 2 * k + pr - 1)
                    for hh in range(2):
                        h = 2 * pr + hh
                        last = pe.matmul(st_ps[pr][:, hh, 0:width(k)], k_op[sl][0:99, h, j * P:(j + 1) * P],
                                         q_op[sl][0:99, h, first_q(k):first_q(k) + width(k)], start=True, stop=not is_diag(k))
                        if is_diag(k):
                            last = pe.matmul(st_ps[pr][:, hh, 0:P], identb[:], future[:], start=False, stop=True)
                    last.then_inc(s_["st"], 1)

                def values(u, g, k, b=None):
                    hf, j = STEPS[k]
                    sl = g % 2
                    first, final = j == 0, k in (7, 11)
                    if first:
                        wait(pe, s_["o_copied"], 2 * u + (1 - hf))
                        if k == 0:
                            if g == 0:
                                wait(pe, s_["v_used"], 4 * (b + 1))
                            if g == G - 1:
                                wait(pe, s_["v_moved"], b + 1)
                    wait(pe, s_["exp"], EX * u + 2 * k + 2)
                    at = first_q(k) - HALF * hf
                    for h in range(HG):
                        last = pe.matmul(acc[32 * h:32 * h + DK + 1, at:at + width(k)], v_op[:, j, HG * g + h, :], prob[k % 3][:, h, 0:width(k)],
                                         start=first, stop=final, tile_position=(0, 32 * h))
                    last.then_inc(s_["pv"], 1)

                def out_turn(u, half):
                    bank = m1 if half == 0 else m0
                    wait(pe, s_["o_copied"], 2 * u + half + 1)
                    for t in range(4):
                        last = pe.transpose(bank[:, t * P:(t + 1) * P], o_t[half][:, t * P:(t + 1) * P], ident[:])
                    last.then_inc(s_["o_full"], 1)

                def attn_turn(bp, i, bank):
                    t0 = (4, 6, 0, 2)[i]
                    for t in range(2):
                        for c in range(C):
                            last = pe.transpose(bank[:, (2 * t + c) * P:(2 * t + c + 1) * P], attn[:, t0 + t, c * P:(c + 1) * P], ident[:])
                    last.then_inc(s_["e_full"], 1)

                def out_project(bp, i, bank):
                    t0 = (4, 6, 0, 2)[i]
                    for t in range(2):
                        for c in range(C):
                            last = pe.matmul(bank[:, t * D:(t + 1) * D], attn_t[:, c, (t0 + t) * P:(t0 + t + 1) * P], wo[:, c, :],
                                             start=(c == 0), stop=(c == C - 1))
                    last.then_inc(s_["w_full"], 1)

                def expert_turn(b, g, p):
                    wait(pe, s_xm[p % 3], 32 * (round0(b, g, 3) + p // 3 + 1))
                    for t in range(2):
                        for c in range(C):
                            last = pe.transpose(m1[:, (2 * t + c) * P:(2 * t + c + 1) * P], x_m[p % 3][:, t, c * P:(c + 1) * P], ident[:])
                    last.then_inc(s_["mt_full"], 1)

                def expert_product(m, p):
                    wait(pe, s_["mt_used"], CREDIT + m + 1)
                    for t in range(2):
                        e = pe.value_load(tile_expert[0:1, ds(2 * m + t, 1)], min_val=0, max_val=E - 1)
                        pe.matmul(m2[:, t * D:(t + 1) * D], ones3[:], ebias[:, ds(e, 1), :].rearrange("p o d -> p (o d)"), start=True, stop=False)
                        for c in range(C):
                            last = pe.matmul(m2[:, t * D:(t + 1) * D], xt_m[p % 2][:, t, c, :],
                                             ew[:, ds(e, 1), c, :].rearrange("p o d -> p (o d)"), start=False, stop=(c == C - 1))
                    last.then_inc(s_["mm_full"], 1)

                def unit(b, g, kd):
                    u = G * b + g
                    n, gn = u + 1, (g + 1) % G
                    bn = b + (1 if g == G - 1 else 0)
                    prev, nxt = has_prev(b, g), has_next(b, g)
                    tail = g == 0 and has_prev_batch(b)
                    moe = kd == "moe"
                    m = pair0(b, g) if moe else None
                    done = {"qk": 2 * n, "v": 4 * (b + 1), "n": n, "nt": n, "o": 2 * u - 1, "e": G * (b - 1) if g == 0 else 0,
                            "w": G * (b - 1) if g == 0 else 0, "mt": m if moe else PAIRS if kd == "comb" and g == 0 else 0,
                            "mm": m if moe else PAIRS if kd == "comb" and g == 0 else 0}
                    if g == 1:
                        done["w"] = G * b if has_prev_batch(b) else 0

                    def free(*kinds):
                        take([(kk + "_used", done[kk] + (CREDIT if kk in ("mt", "mm") else 0)) for kk in kinds if not (isinstance(done[kk], int) and done[kk] <= 0)])

                    if moe and g == 0:
                        wait(pe, s_["ew_in"], 16)
                        pe.wait_ge(s_r, R_ALL)
                    gap = NS // per_unit(b)
                    for k in range(NS):
                        if k == 0:
                            wait(pe, s_load[g % 2], 16 * NLOAD * ((u // 2 + 1) if isinstance(u, int) else (2 * b + g // 2 + 1)))
                        scores(u, g, k, 0)
                        scores(u, g, k, 1)
                        if k == step_of(kd, "find_max") and nxt:
                            find_max(n, (g + 1) % 2, (n // 2) if isinstance(n, int) else 2 * b + (g + 1) // 2)
                        if moe and k % 2 == 0:
                            free("mt", "qk", "o", "e", "w")
                            expert_turn(b, g, k // 2)
                            done["mt"] += 1
                        for hf in range(2):
                            if k == qk_step(kd, hf) and nxt:
                                free("n", "nt", "o", "w", *(["mt"] if qk_bank(kd, hf) is m1 else ["qk"] if hf else []))
                                project_qk(n, gn, hf, bn, qk_bank(kd, hf))
                                done["qk"] += 1
                        if k in (2, 4, 6, 8) and g == G - 1 and nxt:
                            free("mm", "v", "e")
                            project_v(bn, k // 2 - 1)
                            done["v"] += 1
                        if isinstance(b, int) and u == 1 and k in (4, 5, 6, 7):
                            free("v")
                            count_round(k - 4)
                        if k == 3 and prev:
                            free("qk", "w")
                            out_turn(u - 1, 1)
                            done["o"] += 1
                        if moe and k % 2 == 1:
                            free("mm", "v", "n", "e")
                            expert_product(m + k // 2, k // 2)
                            done["mm"] += 1
                        if tail and k in (4, 5):
                            wait(pe, s_["o_used"], 2 * u)
                            free("qk", "mt", "o", "e")
                            attn_turn(b - 1, 2 * (k - 4), m1)
                            done["e"] += 1
                            free("v", "mm")
                            attn_turn(b - 1, 2 * (k - 4) + 1, m2)
                            done["e"] += 1
                        if k == step_of(kd, "norms") and nxt:
                            free("qk", "o", "nt", "w")
                            norms(n)
                            done["n"] += 1
                        if k == step_of(kd, "turn") and nxt:
                            norm_turn(n)
                            done["nt"] += 1
                        if tail and k in (7, 9):
                            free("qk", "o", "n", "nt", "w")
                            wait(pe, s_["e_used"], 4 * (b - 1) + k - 6)
                            out_project(b - 1, k - 7, m0)
                            done["w"] += 1
                            free("mt", "e", "w")
                            out_project(b - 1, k - 6, m1)
                            done["w"] += 1
                        if k >= 2:
                            values(u, g, k - 2, b)
                        elif prev:
                            values(u - 1, (g - 1) % G, NS - 2 + k)
                        if k == 10:
                            free("qk", "mt", "w")
                            out_turn(u, 0)
                            done["o"] += 1

                pe.sem_inc(s_["mm_full"], CREDIT)
                pe.sem_inc(s_["mt_full"], CREDIT)
                project_qk(0, 0, 0, 0, m0)
                project_qk(0, 0, 1, 0, m1)
                for i in range(4):
                    wait(pe, s_["v_used"], i)
                    project_v(0, i)
                wait(pe, s_["qk_used"], 2)
                norms(0)
                norm_turn(0)
                find_max(0, 0, 0)
                pe.wait_ge(s_["k_ones"], 2)
                walk(pe, unit)
                U = G * B
                values(U - 1, G - 1, NS - 2)
                values(U - 1, G - 1, NS - 1)
                out_turn(U - 1, 1)
                wait(pe, s_["o_used"], 2 * U)
                for i in range(4):
                    wait(pe, s_["e_used"], 4 * (B - 1) + i - 1)
                    attn_turn(B - 1, i, (m1, m2)[i % 2])
                for i in range(4):
                    wait(pe, s_["w_used"], 4 * (B - 1) + i - 1)
                    wait(pe, s_["e_used"], 4 * (B - 1) + i + 1)
                    out_project(B - 1, i, (m0, acc)[i % 2])

            @block.scalar
            def _(act):
                def exps(u, k, pr):
                    wait(act, s_["pv"], NS * u + k - 2)
                    wait(act, s_["st"], EX * u + 2 * k + pr + 1)
                    act.activation(prob[k % 3][:, 2 * pr:2 * pr + 2, 0:width(k)], st_ps[pr][:, :, 0:width(k)], ACT.Exp,
                                   scale=SCALE).then_inc(s_["exp"], 1)

                def copy_v(bn, i):
                    wait(act, s_["v_full"], 4 * bn + i + 1)
                    wait(act, s_["pv"], NS * (G * bn - 1))
                    src = m2[:].rearrange("p (t h d) -> p t h d", t=2, h=H)
                    act.activation(v_op[:, 2 * i:2 * i + 2, 0:H - HG, 0:DK], src[:, :, 0:H - HG], ACT.Copy)
                    wait(act, s_["v_moved"], bn)
                    act.activation(v_last[:, 2 * i:2 * i + 2], src[:, :, H - HG:H], ACT.Copy).then_inc(s_["v_used"], 1)

                def store_max(n, sl):
                    if isinstance(n, int):
                        act.wait_ge(s_["maxready"], n + 1)
                    else:
                        wait_apart(act, s_["maxready"], n + 1, s_tick)
                    act.dma_start(max_d[sl].rearrange("r h t s -> (h t) r s"), maxrow[:]).then_inc(s_["max_out"], 16)

                def load_max(n, sl):
                    if isinstance(n, int):
                        act.wait_ge(s_["max_out"], 16 * (n + 1))
                    else:
                        wait_apart(act, s_["max_out"], 16 * (n + 1), s_tick)
                    act.dma_start(q_op[sl][96:99], max_d[sl].rearrange("r h t s -> r h (t s)")).then_inc(s_load[sl], 16)

                def store_y(m, p):
                    wait_apart(act, s_["mm_used"], CREDIT + m + 1, s_tick)
                    act.dma_start(y_d[ds(2 * m * P, 2 * P)].rearrange("(t p) d -> p t d", p=P), y_m[p % 2][:]).then_inc(s_yst[p % 2], 16)

                def square(n):
                    wait(act, s_["rot"], 2 * n + 2)
                    wait(act, s_["n_full"], n)
                    act.activation(squares[:], qk[:], ACT.Square).then_inc(s_["sq"], 1)

                def copy_o(u, half):
                    wait(act, s_["pv"], NS * u + (8, 12)[half])
                    wait(act, s_["o_used"], 2 * (u - 1) + half + 1)
                    act.activation(o_t[half][:], acc[:], ACT.Copy).then_inc(s_["o_copied"], 1)

                def copy_attn(bp, i, bank):
                    t0 = (4, 6, 0, 2)[i]
                    wait(act, s_["e_full"], 4 * bp + i + 1)
                    wait(act, s_["w_full"], 4 * bp)
                    act.activation(attn_t[:].rearrange("p c (t s) -> p t c s", s=P)[:, t0:t0 + 2],
                                   bank[:].rearrange("p (t c s) -> p t c s", t=2, c=C), ACT.Copy).then_inc(s_["e_used"], 1)

                def copy_tokens(m, p):
                    wait(act, s_["mt_full"], CREDIT + m + 1)
                    wait(act, s_["mm_full"], CREDIT + m - 1)
                    act.activation(xt_m[p % 2][:].rearrange("p t c s -> p (t c s)"), m1[:], ACT.Copy).then_inc(s_["mt_used"], 1)

                def unit(b, g, kd):
                    u = G * b + g
                    n = u + 1
                    prev, nxt = has_prev(b, g), has_next(b, g)
                    tail = g == 0 and has_prev_batch(b)
                    moe = kd == "moe"
                    m = pair0(b, g) if moe else None
                    gap = NS // per_unit(b)
                    for k in range(NS):
                        if isinstance(b, int) and (u, k) == (1, 0):
                            act.wait_ge(s_r, R_PICKED)
                            act.activation(work[2], work[2], ACT.Exp).then_inc(s_ract, 1)
                            act.activation(pick[:], pick[:], ACT.Exp).then_inc(s_ract, 1)
                        if k == 2 and prev:
                            copy_o(u - 1, 1)
                        exps(u, k, 0)
                        exps(u, k, 1)
                        if moe and k % 2 == 0:
                            copy_tokens(m + k // 2, k // 2)
                        if k in (2, 4, 6, 8) and g == G - 1 and nxt:
                            copy_v(b + 1, k // 2 - 1)
                        if moe and k % 2 == 0 and k >= 2:
                            store_y(m + k // 2 - 1, k // 2 - 1)
                        if tail and k in (4, 5):
                            copy_attn(b - 1, 2 * (k - 4), m1)
                            copy_attn(b - 1, 2 * (k - 4) + 1, m2)
                        if k == step_of(kd, "square") and nxt:
                            square(n)
                        if k == step_of(kd, "store_max") and nxt:
                            store_max(n, (g + 1) % 2)
                        if k == step_of(kd, "load_max") and nxt:
                            load_max(n, (g + 1) % 2)
                        if k == 9:
                            copy_o(u, 0)

                act.sem_inc(s_["mt_used"], CREDIT)
                act.wait_ge(s_["ones"], 1)
                for i in range(4):
                    copy_v(0, i)
                square(0)
                store_max(0, 0)
                load_max(0, 0)
                walk(act, unit)
                U = G * B
                copy_o(U - 1, 1)
                for i in range(4):
                    copy_attn(B - 1, i, (m1, m2)[i % 2])

            @block.vector
            def _(dve):
                def rotate(n, hf, bank):
                    cols = slice(hf * HALF, (hf + 1) * HALF)
                    wait(dve, s_["qk_full"], 2 * n + hf + 1)
                    dve.tensor_tensor(rot_a[:, cols], bank[:], cosT[:, cols], ALU.mult)
                    dve.stream_shuffle(rot_b[:, cols], bank[:], [i ^ HG for i in range(32)]).then_inc(s_["qk_used"], 1)
                    wait(dve, s_["qk_used"], 2 * n + hf + 1)
                    dve.tensor_tensor(rot_b[:, cols], rot_b[:, cols], sinT[:, cols], ALU.mult).then_inc(s_["rot_mul"], 1)
                    wait(dve, s_["sq"], n)
                    wait(dve, s_["rot_mul"], 2 * n + hf + 1)
                    dve.tensor_tensor(qk[:, cols], rot_a[:, cols], rot_b[:, cols], ALU.add).then_inc(s_["rot"], 1)

                def split(n, hf):
                    cols = slice(hf * HALF, (hf + 1) * HALF)
                    c0 = 8 * n + 4 * hf
                    wait(dve, s_["rot"], 2 * n + hf + 1)
                    wait(dve, s_["part_out"], 32 * n)
                    dve.tensor_copy(parts[:, 0, cols], qk[:, cols]).then_inc(s_["split"], 1)
                    wait(dve, s_["split"], c0 + 1)
                    dve.tensor_tensor(rot_a[:, cols], qk[:, cols], parts[:, 0, cols], ALU.subtract).then_inc(s_["split"], 1)
                    wait(dve, s_["split"], c0 + 2)
                    dve.tensor_copy(parts[:, 1, cols], rot_a[:, cols]).then_inc(s_["split"], 1)
                    wait(dve, s_["split"], c0 + 3)
                    dve.tensor_tensor(parts[:, 2, cols], rot_a[:, cols], parts[:, 1, cols], ALU.subtract).then_inc(s_["split"], 1)

                def norm_max(n):
                    wait(dve, s_["n_full"], n + 1)
                    dve.tensor_reduce(nmax[:], m0[:, 0:TB * 2 * HG], X, ALU.max).then_inc(s_["n_used"], 1)

                def bound(n, sl):
                    wait(dve, s_["nt_full"], n + 1)
                    dve.tensor_reduce(nbound[:], m0[0:1, 0:P], X, ALU.max).then_inc(s_["nt_used"], 1)
                    wait(dve, s_["nt_used"], n + 1)
                    wait(dve, s_["slow_pe"], SLOW_PE * n)
                    dve.tensor_scalar(flag[:], nbound[:], NORM2, None, ALU.is_gt).then_inc(s_["flagged"], 1)
                    wait_apart(dve, s_["flagged"], n + 1, s_tick)
                    if not (isinstance(n, int) and n == 0):
                        wait_apart(dve, s_["max_out"], 16 * n, s_tick)
                    v = dve.value_load(flag[0:1, 0:1], min_val=0, max_val=1)
                    with dve.If(v > 0):
                        find_max(n)
                    with dve.Else():
                        dve.sem_inc(s_["slow_dve"], SLOW_DVE)
                        dve.memset(maxrow[:], 0.0).then_inc(s_["maxready"], 1)

                def find_max(n):
                    c0 = CREDIT + SLOW_DVE * n
                    tmp = rot_a[:, 0:HALF]
                    with dve.Fori(0, TB) as i:
                        for w in range(2 * HG):
                            h, half = w // 2, w % 2
                            at = 2 * HG * i + w
                            wait_apart(dve, s_["slow_pe"], SLOW_PE * n + at + 1, s_tick)
                            dve.tensor_tensor(tmp, m0[:], masks[:, ds(MASK0 + half * HALF - i * P, HALF)], ALU.add).then_inc(s_["slow_dve"], 1)
                            dve.wait_ge(s_["slow_dve"], c0 + 2 * at + 1)
                            dve.tensor_reduce(rowmax[:, ds(i, 1), h, half:half + 1], tmp, X, ALU.max).then_inc(s_["slow_dve"], 1)
                    c0 = c0 + 2 * SLOW
                    dve.wait_ge(s_["slow_dve"], c0)
                    dve.tensor_reduce(rm[:].rearrange("p (h t) -> p h t", h=HG), rowmax[:].rearrange("p t h w -> p h t w"), X, ALU.max).then_inc(s_["slow_dve"], 1)
                    dve.wait_ge(s_["slow_dve"], c0 + 1)
                    dve.tensor_scalar(rm[:], rm[:], -1.0, None, ALU.mult).then_inc(s_["slow_dve"], 1)
                    for r in range(2):
                        dve.wait_ge(s_["slow_dve"], c0 + 2 + 2 * r)
                        dve.tensor_copy(rmb[:, r, :], rm[:]).then_inc(s_["slow_dve"], 1)
                        dve.wait_ge(s_["slow_dve"], c0 + 3 + 2 * r)
                        dve.tensor_tensor(rm[:] if r == 0 else rmb[:, 2, :], rm[:], rmb[:, r, :], ALU.subtract).then_inc(s_["slow_dve"], 1)
                    dve.wait_ge(s_["slow_pe"], SLOW_PE * (n + 1))
                    dve.tensor_copy(maxrow[:].rearrange("p r s -> p (r s)"), m0[0:HG * TB, 0:3 * P]).then_inc(s_["maxready"], 1)

                def normalise(u, g, half):
                    bank = (m1 if half == 0 else m0)[:].rearrange("p (t h d) -> p t h d", t=4, h=HG)
                    t0 = 4 * (1 - half)
                    wait(dve, s_["o_full"], 2 * u + half + 1)
                    dve.reciprocal(inv[:], bank[:, :, :, DK]).then_inc(s_["o_inv"], 1)
                    wait(dve, s_["o_inv"], 2 * u + half + 1)
                    dve.tensor_tensor(attn[:, t0:t0 + 4, g * GD:(g + 1) * GD].rearrange("p t (h d) -> p t h d", h=HG),
                                      bank[:, :, :, 0:DK], inv[:].unsqueeze(3).broadcast_to([P, 4, HG, DK]), ALU.mult).then_inc(s_["o_used"], 1)

                def add_resid(bp, i, bank):
                    wait(dve, s_["w_full"], 4 * bp + i + 1)
                    wait(dve, s_res_in[i % 2], 16 * (2 * bp + i // 2 + 1))
                    dve.tensor_tensor(resid[i % 2][:].rearrange("p t d -> p (t d)"), bank[:], resid[i % 2][:].rearrange("p t d -> p (t d)"),
                                      ALU.add).then_inc(s_["w_used"], 1)

                def move_v(b):
                    wait(dve, s_["v_used"], 4 * (b + 1))
                    wait(dve, s_["pv"], NS * G * b)
                    dve.tensor_copy(v_op[:, :, H - HG:H, 0:DK], v_last[:]).then_inc(s_["v_moved"], 1)

                def relu(b, g, p):
                    wait(dve, s_["mm_full"], CREDIT + pair0(b, g) + p + 1)
                    wait(dve, s_yst[p % 2], 16 * (round0(b, g, 2) + p // 2 + 1))
                    dve.tensor_scalar(y_m[p % 2][:].rearrange("p t d -> p (t d)"), m2[:], 0.0, None, ALU.max).then_inc(s_["mm_used"], 1)

                def combine(b, g, i):
                    c = tile_c0(b, g) + i
                    wait(dve, s_yc[i % 2], 32 * (crounds(b, g) + i // 2 + 1))
                    wait(dve, s_hc[i % 2], 16 * (crounds(b, g) + i // 2 + 1))
                    dve.scalar_tensor_tensor(h_c[i % 2], y_c[i % 2][:, 0, :], w_top[:, 0, ds(c, 1)], h_c[i % 2], ALU.mult, ALU.add).then_inc(s_["h_c1"], 1)
                    wait(dve, s_["h_c1"], c + 1)
                    dve.scalar_tensor_tensor(h_c[i % 2], y_c[i % 2][:, 1, :], w_top[:, 1, ds(c, 1)], h_c[i % 2], ALU.mult, ALU.add).then_inc(s_["combined"], 1)

                step = [0]

                def then(ins):
                    step[0] += 1
                    ins.then_inc(s_r, 1)
                    dve.wait_ge(s_r, step[0])

                def over_e(v):
                    return v.unsqueeze(2).broadcast_to([P, T, E])

                def pick_expert(s):
                    src = (logit, work[1])[s]
                    then(dve.tensor_reduce(top[s][:], src, X, ALU.max))
                    then(dve.tensor_tensor(work[0], src, over_e(top[s][:]), ALU.is_equal))
                    then(dve.tensor_tensor(work[0], work[0], iota_e[:].unsqueeze(1).broadcast_to([P, T, E]), ALU.mult))
                    then(dve.tensor_reduce(pick[:], work[0], X, ALU.min))
                    then(dve.tensor_tensor(hot[s], work[0], over_e(pick[:]), ALU.is_equal))
                    if s == 0:
                        then(dve.scalar_tensor_tensor(work[1], hot[0], BIG, logit, ALU.mult, ALU.add))

                def to_exp():
                    then(dve.tensor_tensor(hotb, hot[0], hot[1], ALU.add))
                    then(dve.tensor_tensor(work[2], logit, over_e(top[0][:]), ALU.subtract))
                    then(dve.tensor_tensor(pick[:], top[1][:], top[0][:], ALU.subtract))
                    assert step[0] == R_PICKED

                def copy_round(i):
                    dve.wait_ge(s_rpe, i + 1)
                    dst = (work[0], rank)[i // 2][:, i % 2 * T // 2:(i % 2 + 1) * T // 2, :]
                    then(dve.tensor_copy(dst.rearrange("p t e -> p (t e)"), m2[:]))

                def weights_and_bases():
                    dve.wait_ge(s_ract, 2)
                    then(dve.tensor_reduce(den[:], work[2], X, ALU.add))
                    then(dve.reciprocal(w_top[:, 0, :], den[:]))
                    then(dve.tensor_tensor(w_top[:, 1, :], pick[:], w_top[:, 0, :], ALU.mult))
                    tot, pre = work[0], work[1]
                    for e in range(E):
                        last = dve.tensor_tensor_scan(pre[:, :, e], onesT[:], tot[:, :, e], 0.0, ALU.mult, ALU.add)
                    then(last)
                    then(dve.tensor_scalar(cnt[:], pre[:, T - 1, :], float(P - 1), None, ALU.add))
                    then(dve.tensor_copy(cnt_i[:], cnt[:]))
                    then(dve.tensor_scalar(cnt_i[:], cnt_i[:], 7, None, ALU.arith_shift_right))
                    then(dve.tensor_copy(nt_f[:], cnt_i[:]))
                    then(dve.tensor_tensor_scan(inc[:], ones_e[:], nt_f[:], 0.0, ALU.mult, ALU.add))
                    then(dve.tensor_tensor(base[:], inc[:], nt_f[:], ALU.subtract))
                    then(dve.tensor_scalar(base[:], base[:], float(P), None, ALU.mult))

                def places():
                    tot, pre = work[0], work[1]
                    then(dve.tensor_tensor(pre, pre, tot, ALU.subtract))
                    then(dve.tensor_tensor(pre, pre, base[:].unsqueeze(1).broadcast_to([P, T, E]), ALU.add))
                    then(dve.tensor_tensor(pre, rank, pre, ALU.add))
                    for s in range(2):
                        then(dve.tensor_tensor(work[2], pre, hot[s], ALU.mult))
                        then(dve.tensor_reduce(posf[:, s, :], work[2], X, ALU.add))
                    then(dve.tensor_copy(y_row[:], posf))
                    then(dve.tensor_scalar(lo_i, y_row[:], P - 1, None, ALU.bitwise_and))
                    then(dve.tensor_scalar(hi_i[:], y_row[:], 7, None, ALU.arith_shift_right))
                    then(dve.tensor_scalar(at_f, lo_i, float(MT), None, ALU.mult))
                    then(dve.tensor_tensor(list_at[:], at_f, hi_i[:], ALU.add))
                    assert step[0] == R_LIST

                def tile_experts():
                    then(dve.tensor_tensor(ge, iota_m[:].unsqueeze(2).broadcast_to([1, MT, E]),
                                           inc[0:1, :].unsqueeze(1).broadcast_to([1, MT, E]), ALU.is_ge))
                    then(dve.tensor_reduce(te_f[:], ge[:, :, 0:E - 1], X, ALU.add))
                    then(dve.tensor_copy(tile_expert[:], te_f[:]))
                    assert step[0] == R_ALL

                def router(u, k):
                    if (u, k) == (0, 6):
                        pick_expert(1)
                        to_exp()
                    if u == 1 and k in (4, 5, 6, 7):
                        copy_round(k - 4)
                    if (u, k) == (1, 8):
                        weights_and_bases()
                    if (u, k) == (2, 7):
                        places()
                    if (u, k) == (3, 7):
                        tile_experts()

                def combine_last(i):
                    dve.wait_ge(s_last_y[i], 32 * len(LAST[i]))
                    dve.wait_ge(s_["last_x"], 16)
                    for s in range(2):
                        dve.wait_ge(s_["last_sum"], 2 * i + s) if 2 * i + s else None
                        for t in LAST[i]:
                            last = dve.scalar_tensor_tensor(last_x[:, t], last_y[:, t, s], w_top[:, s, T - TB + t:T - TB + t + 1], last_x[:, t], ALU.mult, ALU.add)
                        last.then_inc(s_["last_sum"], 1)

                def unit(b, g, kd):
                    u = G * b + g
                    n = u + 1
                    prev, nxt = has_prev(b, g), has_next(b, g)
                    tail = g == 0 and has_prev_batch(b)
                    moe = kd == "moe"
                    m = pair0(b, g) if moe else None
                    gap = NS // per_unit(b)
                    for k in range(NS):
                        for hf in range(2):
                            if k == qk_step(kd, hf) and nxt:
                                rotate(n, hf, qk_bank(kd, hf))
                                if hf == 1 and prev:
                                    normalise(u - 1, (g - 1) % G, 1)
                                split(n, hf)
                        if k == 3 and not nxt:
                            normalise(u - 1, (g - 1) % G, 1)
                        if moe and k % 2 == 1:
                            relu(b, g, k // 2)
                        if k == step_of(kd, "norms") and nxt:
                            norm_max(n)
                        if k == step_of(kd, "bound") and nxt:
                            bound(n, (g + 1) % 2)
                        if isinstance(b, int) and b == 0:
                            router(u, k)
                        if k == 7 and g == 0:
                            move_v(b)
                        if tail and k in (7, 9):
                            add_resid(b - 1, k - 7, m0)
                            add_resid(b - 1, k - 6, m1)
                        if kd == "comb" and k % gap == gap - 1 and k != 2:
                            combine(b, g, k // gap)
                        if kd == "comb" and gap == 3 and k == 3:
                            combine(b, g, 0)
                        if k == 10:
                            if tail:
                                wait(dve, s_["e_full"], 4 * b)
                            normalise(u, g, 0)
                            if kd == "comb" and isinstance(b, int) and g > 0:
                                combine_last(g - 1)

                dve.sem_inc(s_["combined"], CREDIT)
                dve.sem_inc(s_["slow_dve"], CREDIT)
                dve.sem_inc(s_["mm_used"], CREDIT)
                dve.memset(acc[:], 0.0)
                dve.memset(v_op[:, :, :, DK:DK + 1], 1.0).then_inc(s_["ones"], 1)
                rotate(0, 0, m0)
                split(0, 0)
                rotate(0, 1, m1)
                split(0, 1)
                norm_max(0)
                bound(0, 0)
                pick_expert(0)
                walk(dve, unit)
                U = G * B
                normalise(U - 1, G - 1, 1)
                dve.wait_ge(s_["last_sum"], 2 * len(LAST))
                for i in range(4):
                    t0 = (4, 6, 0, 2)[i]
                    dve.wait_ge(s_["w_full"], 4 * (B - 1) + i + 1)
                    rows = last_x[:, t0:t0 + 2].rearrange("p t d -> p (t d)")
                    dve.tensor_tensor(rows, (m0, acc)[i % 2][:], rows, ALU.add).then_inc(s_["w_used"], 1)

            @block.gpsimd
            def _(pool):
                def scatter(t):
                    for s in range(2):
                        pool.indirect_dma_start(list_d, bass.IndirectOffsetOnAxis(ap=list_at[:, s, t:t + 1], axis=0),
                                                token[:, t:t + 1], None).then_inc(s_["scattered"], 16)

                def gather_tokens(m, sl):
                    wait(pool, s_["mt_full"], CREDIT + m - 2)
                    pool.wait_ge(s_["listed"], 16)
                    pool.tensor_copy(pick_m[sl][:], lists[:, ds(2 * m, 2)]).then_inc(s_["picked"], 1)
                    wait_apart(pool, s_["picked"], m + 1, s_tick)
                    for t in range(2):
                        pool.indirect_dma_start(x_m[sl][:, t, :], None, xn_d,
                                                bass.IndirectOffsetOnAxis(ap=pick_m[sl][:, t:t + 1], axis=0)).then_inc(s_xm[sl], 16)

                def gather_outputs(c, sl):
                    wait(pool, s_["combined"], CREDIT + c - 1)
                    pool.wait_ge(s_["listed"], 16)
                    for s in range(2):
                        last = pool.tensor_copy(pick_c[sl][:, s:s + 1], y_row[:, s, ds(c, 1)])
                    last.then_inc(s_["pick_c_made"], 1)
                    wait_apart(pool, s_["pick_c_made"], c + 1, s_tick)
                    for s in range(2):
                        pool.indirect_dma_start(y_c[sl][:, s, :], None, y_d,
                                                bass.IndirectOffsetOnAxis(ap=pick_c[sl][:, s:s + 1], axis=0)).then_inc(s_yc[sl], 16)

                def gather_last(i, t):
                    for s in range(2):
                        pool.indirect_dma_start(last_y[:, t, s, :], None, y_d,
                                                bass.IndirectOffsetOnAxis(ap=y_row[:, s, T - TB + t:T - TB + t + 1], axis=0)).then_inc(s_last_y[i], 16)

                def unit(b, g, kd):
                    u = G * b + g
                    n = u + 1
                    nxt = has_next(b, g)
                    gap = NS // per_unit(b)
                    for k in range(NS):
                        if kd == "plain" and u >= SCATTER_U:
                            if (u, k) == (SCATTER_U, 0):
                                pool.wait_ge(s_r, R_LIST)
                            for t in [k] if k < NS - 1 else range(NS - 1, SCATTER_T):
                                if SCATTER_T * (u - SCATTER_U) + t < T:
                                    scatter(SCATTER_T * (u - SCATTER_U) + t)
                        if kd == "moe" and k % 2 == 1:
                            gather_tokens(pair0(b, g) + k // 2 + 2, (k // 2 + 2) % 3)
                        if kd == "comb" and k % gap == 0:
                            i = k // gap + 1
                            if not (isinstance(b, int) and tile_c0(b, g) + i >= T - TB):
                                gather_outputs(tile_c0(b, g) + i, i % 2)
                        if kd == "comb" and isinstance(b, int) and g < len(LAST) and k in (1, 5, 9) and k // 4 < len(LAST[g]):
                            gather_last(g, LAST[g][k // 4])
                    if kd == "plain" and isinstance(b, int) and b == B_MOE - 1 and g == G - 1:
                        pool.wait_ge(s_["scattered"], 16 * 2 * T)
                        pool.wait_ge(s_["zeroed"], 1)
                        pool.dma_start(lists[:, 0:MT], list_d.rearrange("(p m) o -> p (m o)", p=P)).then_inc(s_["listed"], 16)
                        gather_tokens(0, 0)
                        gather_tokens(1, 1)

                pool.memset(lists[:], 0).then_inc(s_["zeroed"], 1)
                pool.wait_ge(s_["zeroed"], 1)
                for i in range(2):
                    pool.memset(k_op[i][96:99, :, :], 1.0).then_inc(s_["k_ones"], 1)
                    pool.wait_ge(s_["k_ones"], i + 1)
                for b in range(B_MOE):
                    for g in range(G):
                        unit(b, g, "plain")
                with pool.Fori(B_MOE, B_COMB) as b:
                    for g in range(G):
                        unit(b, g, "moe")
                for sl in range(3):
                    pool.wait_ge(s_xm[sl], 32 * ((PAIRS + 2 - sl + 2) // 3))
                pool.wait_ge(s_["mt_full"], CREDIT + PAIRS)
                for sl in range(2):
                    pool.wait_ge(s_yst[sl], 16 * (PAIRS // 2 + 1))
                gather_outputs(0, 0)
                with pool.Fori(B_COMB, B_LAST) as b:
                    for g in range(G):
                        unit(b, g, "comb")
                pool.wait_ge(s_["mm_full"], CREDIT + PAIRS)
                for g in range(G):
                    unit(B_LAST, g, "comb")

            @block.sync
            def _(sp):
                def wait_sp(sem, value):
                    if isinstance(value, int):
                        wait(sp, sem, value)
                    else:
                        wait_apart(sp, sem, value, s_tick)

                def load_xT(bn):
                    wait_sp(s_["qk_full"], 2 * G * bn)
                    sp.dma_start(xT[:], xnt_d[ds(bn, 1)].rearrange("o p c s -> p (o c) s")).then_inc(s_["xT_in"], 16)

                def store_parts(n, sl, hf):
                    cols = slice(hf * HALF, (hf + 1) * HALF)
                    wait_sp(s_["split"], 8 * n + 4 * hf + 4)
                    sp.dma_start(part_d[sl].rearrange("r w d (h s) -> (w d h) r s", h=HG)[:, :, cols], parts[:, :, cols]).then_inc(s_["part_out"], 16)

                def load_parts(n, sl):
                    wait_sp(s_["st"], EX * (n - 1))
                    wait_sp(s_["part_out"], 32 * (n + 1))
                    d = part_d[sl]
                    sp.dma_start(flat(q_op[sl][0:48]), again(d[0, 0], 3)).then_inc(s_load[sl], 16)
                    sp.dma_start(flat(q_op[sl][48:80]), again(d[1, 0], 2)).then_inc(s_load[sl], 16)
                    sp.dma_start(flat(q_op[sl][80:96]), d[2, 0]).then_inc(s_load[sl], 16)
                    sp.dma_start(flat(k_op[sl][0:48]), d[0:3, 1]).then_inc(s_load[sl], 16)
                    sp.dma_start(flat(k_op[sl][48:80]), d[0:2, 1]).then_inc(s_load[sl], 16)
                    sp.dma_start(flat(k_op[sl][80:96]), d[0, 1]).then_inc(s_load[sl], 16)

                def flat(v):
                    return v.rearrange("p h s -> p (h s)")

                def again(v, times):
                    return bass.AP(tensor=v.tensor, offset=v.offset, ap=[[0, times]] + [list(q) for q in v.ap])

                def load_resid(bp, i):
                    t0 = (4, 6, 0, 2)[i]
                    wait_sp(s_res_out[i % 2], 16 * (2 * bp + i // 2))
                    sp.dma_start(resid[i % 2][:], x_rows[ds(bp * S + t0 * P, 2 * P)].rearrange("(t p) d -> p t d", p=P)).then_inc(s_res_in[i % 2], 16)

                def store_h(bp, i):
                    t0 = (4, 6, 0, 2)[i]
                    wait_sp(s_["w_used"], 4 * bp + i + 1)
                    sp.dma_start(h_d[ds(bp * S + t0 * P, 2 * P)].rearrange("(t p) d -> p t d", p=P), resid[i % 2][:]).then_inc(s_res_out[i % 2], 16)

                def store_last_y(m):
                    wait_sp(s_["mm_used"], CREDIT + m + PU)
                    sp.dma_start(y_d[ds(2 * (m + PU - 1) * P, 2 * P)].rearrange("(t p) d -> p t d", p=P), y_m[1][:]).then_inc(s_yst[1], 16)

                def load_h(b, g, i):
                    c = tile_c0(b, g) + i
                    wait_sp(s_oc[i % 2], 16 * (crounds(b, g) + i // 2 + 1))
                    sp.dma_start(h_c[i % 2], h_d[ds(c * P, P)]).then_inc(s_hc[i % 2], 16)

                def store_out(b, g, i):
                    c = tile_c0(b, g) + i
                    wait_sp(s_["combined"], CREDIT + c + 1)
                    sp.dma_start(out_rows[ds(c * P, P)], h_c[i % 2]).then_inc(s_oc[i % 2], 16)

                def store_last_out(b, g):
                    c = tile_c0(b, g) + per_unit(b) - 1
                    wait_sp(s_["combined"], CREDIT + c + 1)
                    sp.dma_start(out_rows[ds(c * P, P)], h_c[1]).then_inc(s_oc[1], 16)

                def unit(b, g, kd):
                    u = G * b + g
                    n = u + 1
                    prev, nxt = has_prev(b, g), has_next(b, g)
                    tail = g == 0 and has_prev_batch(b)
                    moe = kd == "moe"
                    m = pair0(b, g) if moe else None
                    c0 = tile_c0(b, g) if kd == "comb" else None
                    gap = NS // per_unit(b)
                    for k in range(NS):
                        if k == 6 and g == G - 2 and nxt and not (isinstance(b, int) and b == B_LAST):
                            load_xT(b + 1)
                        if tail and k == 0:
                            load_resid(b - 1, 0)
                            load_resid(b - 1, 1)
                        if isinstance(b, int) and (u, k) == (G + 1, 10):
                            sp.wait_ge(s_r, R_ALL)
                            sp.dma_start(ew[:], a["expert_wT"].rearrange("e (c p) d -> p e c d", p=P)).then_inc(s_["ew_in"], 16)
                        for hf in range(2):
                            if k == step_of(kd, f"store{hf}") and nxt:
                                store_parts(n, (g + 1) % 2, hf)
                        if k == step_of(kd, "load") and nxt:
                            load_parts(n, (g + 1) % 2)
                        if tail and k == 9:
                            for i in range(2):
                                store_h(b - 1, i)
                            for i in range(2):
                                load_resid(b - 1, i + 2)
                        if tail and k == 11:
                            store_h(b - 1, 2)
                            store_h(b - 1, 3)
                        if kd == "comb" and k % gap == 0 and k > 0:
                            store_out(b, g, k // gap - 1)
                        if kd == "comb" and k % gap == 1:
                            i = k // gap + 1
                            if isinstance(b, int) and g == 1 and i == 1:
                                for q in range(2):
                                    sp.wait_ge(s_res_out[q], 16 * 2 * (B - 1))
                            if not (isinstance(b, int) and tile_c0(b, g) + i >= T - TB):
                                load_h(b, g, i)
                        if kd == "comb" and isinstance(b, int) and k == 0 and g == 0:
                            sp.wait_ge(s_["mm_full"], CREDIT + PAIRS)
                            sp.dma_start(last_x, x_rows[(B - 1) * S:B * S].rearrange("(t p) d -> p t d", p=P)).then_inc(s_["last_x"], 16)
                    if moe:
                        store_last_y(m)
                    if kd == "comb":
                        store_last_out(b, g)

                load_xT(0)
                for i in range(2):
                    sp.sem_inc(s_yst[i], 16)
                    sp.sem_inc(s_oc[i], 16)
                store_parts(0, 0, 0)
                store_parts(0, 0, 1)
                load_parts(0, 0)

                def first_h():
                    for i in range(2):
                        sp.wait_ge(s_yst[i], 16 * (PAIRS // 2 + 1))
                    sp.dma_start(h_c[0], h_d[0:P]).then_inc(s_hc[0], 16)

                walk(sp, unit, first_h)
                for i in range(4):
                    t0 = (4, 6, 0, 2)[i]
                    sp.wait_ge(s_["w_used"], 4 * (B - 1) + i + 1)
                    sp.dma_start(out_rows[(B - 1) * S + t0 * P:(B - 1) * S + (t0 + 2) * P].rearrange("(t p) d -> p t d", p=P), last_x[:, t0:t0 + 2]).then_inc(s_["last_out"], 16)
                sp.wait_ge(s_["last_out"], 16 * 4)
                for i in range(2):
                    sp.wait_ge(s_oc[i], 16 * ((T - TB) // 2 + 1))


_NAMES = {"x": "L0_attn_x", "Wv": "L0_attn_Wv", "Wo": "L0_attn_Wo", "expert_b": "L0_ffn_expert_b"}


def _shape_constants():
    inv_freq = (np.float32(1.0) / np.power(np.float32(10000.0), np.arange(0, DK, 2, dtype=np.float32) / np.float32(DK))).astype(np.float32)
    ang = np.outer(np.arange(S, dtype=np.float32), inv_freq).astype(np.float32)
    cos, sin = np.cos(ang).astype(np.float32), np.sin(ang).astype(np.float32)
    dim = np.arange(P) // HG % DK
    pair = dim // 2
    sign = np.where(dim % 2 == 0, -1.0, 1.0).astype(np.float32)
    head = np.arange(P) % HG + HG * (np.arange(P) // GD)
    return {
        "cosT": np.ascontiguousarray(cos[:, pair].T),
        "sinT": np.ascontiguousarray(sin[:, pair].T * sign[:, None]),
        "ident": np.eye(P, dtype=np.float32),
        "upper": np.triu(np.ones((P, P), np.float32), 1),
        "lower": np.tril(np.ones((P, P), np.float32), -1),
        "headsum": (head[:, None] == np.arange(2 * HG)[None, :]).astype(np.float32),
        "iota_e": np.tile(np.arange(E, dtype=np.float32) - 99.0, (P, 1)),
        "masks": np.where(np.arange(MASKW)[None, :] - MASK0 <= np.arange(P)[:, None], np.float32(0), np.float32(BIG)),
        "iota_m": np.arange(MT, dtype=np.float32)[None, :],
    }


def kernel(**inputs):
    import concourse.bacc as _bacc
    from concourse.bass_utils import run_bass_kernel_spmd as _run

    nc = _bacc.Bacc("TRN2", target_bir_lowering=False, num_devices=1)
    arrays = {k: np.ascontiguousarray(inputs[v]) for k, v in _NAMES.items()}
    arrays["gate_wT"] = np.ascontiguousarray(np.asarray(inputs["L0_ffn_gate_w"]).T)
    arrays["expert_wT"] = np.ascontiguousarray(np.asarray(inputs["L0_ffn_expert_w"]).transpose(0, 2, 1))
    wq, wk = (np.asarray(inputs[k]).reshape(C, P, G, HG, DK).transpose(1, 2, 0, 4, 3).reshape(P, G, C, GD) for k in ("L0_attn_Wq", "L0_attn_Wk"))
    arrays["Wqk"] = np.ascontiguousarray(np.concatenate([wq, wk], axis=3))
    arrays.update(_shape_constants())
    feeds, a = {}, {}
    for name, v in arrays.items():
        feeds[f"in_{name}"] = v
        a[name] = nc.dram_tensor(f"in_{name}", v.shape, mybir.dt.from_np(v.dtype), kind="ExternalInput").ap()
    a["out"] = nc.dram_tensor("out_0", (B, S, D), F32, kind="ExternalOutput").ap()
    build(nc, a)
    r = _run(nc, [feeds], core_ids=[0])
    return r.results[0]["out_0"]
```
